# Optimizing a Trainium2 kernel written in Bass

```python
import numpy as np
import jax
import jax.numpy as jnp

def _softmax(x, axis=-1):
    return jax.nn.softmax(x, axis=axis)

def _gelu(x):
    return jax.nn.gelu(x, approximate=True)

def _silu(x):
    return jax.nn.silu(x)

def _sigmoid(x):
    return jax.nn.sigmoid(x)

def _layernorm(x, axis=-1, eps=1e-05):
    m = jnp.mean(x, axis=axis, keepdims=True)
    v = jnp.var(x, axis=axis, keepdims=True)
    return (x - m) / jnp.sqrt(v + eps)

def _scatter_add(tgt, idx, src, axis=0):
    return tgt.at[idx].add(src)

def _segment_sum(src, seg, n):
    return jax.ops.segment_sum(src, seg, n)
kernel_name = 'mk_conv_attn_hybrid_d2_conv_nchw256_r4_d4c63b'

def setup_inputs(seed: int=0):
    np.random.seed(seed)
    _w = jnp.asarray

    def _rec_inputs():
        import jax
        import jax.numpy as jnp
        _gk = jax.random.key(seed)
        x = -0.0002928 + 1 * jax.random.normal(jax.random.fold_in(_gk, 1), (4, 64, 16, 16), jnp.float32)
        return x
    x = _rec_inputs()

    def _L0_conv_setup():
        import jax, jax.numpy as jnp
        import numpy as np
        B, C, H, W = (4, 64, 16, 16)
        G, K, PAD, STRIDE, DIL, DWK = (8, 3, 1, 1, 1, 3)
        P = K * K
        GC = C // G

        def _dwconv(x, w, b, pad):
            y = jax.lax.conv_general_dilated(x, w, (1, 1), [(pad, pad), (pad, pad)], feature_group_count=C, dimension_numbers=('NCHW', 'OIHW', 'NCHW'))
            return y + b[None, :, None, None]

        def _conv1x1(x, w, b):
            return jnp.einsum('bchw,cd->bdhw', x, w) + b[None, :, None, None]

        def _ln(x, g, b, eps=1e-05):
            mu = x.mean(-1, keepdims=True)
            var = ((x - mu) ** 2).mean(-1, keepdims=True)
            return (x - mu) * jax.lax.rsqrt(var + eps) * g + b

        def _bilinear_sample(img, grid):
            gc, Hp, Wp = img.shape
            ix = ((grid[..., 0] + 1.0) * Wp - 1.0) * 0.5
            iy = ((grid[..., 1] + 1.0) * Hp - 1.0) * 0.5
            x0 = jnp.floor(ix)
            y0 = jnp.floor(iy)
            x1 = x0 + 1.0
            y1 = y0 + 1.0
            imgf = img.reshape(gc, Hp * Wp)

            def gather(yy, xx):
                valid = (xx >= 0) & (xx <= Wp - 1) & (yy >= 0) & (yy <= Hp - 1)
                xi = jnp.clip(xx, 0, Wp - 1).astype(jnp.int32)
                yi = jnp.clip(yy, 0, Hp - 1).astype(jnp.int32)
                return imgf[:, yi * Wp + xi] * valid
            w00 = (x1 - ix) * (y1 - iy)
            w01 = (ix - x0) * (y1 - iy)
            w10 = (x1 - ix) * (iy - y0)
            w11 = (ix - x0) * (iy - y0)
            return gather(y0, x0) * w00 + gather(y0, x1) * w01 + gather(y1, x0) * w10 + gather(y1, x1) * w11

        def _dcnv3_core(x, offset, mask):
            xp = jnp.pad(x, ((0, 0), (PAD, PAD), (PAD, PAD), (0, 0)))
            Hp, Wp = (H + 2 * PAD, W + 2 * PAD)
            base = DIL * (K - 1) // 2 + 0.5
            ref_y = (base + jnp.arange(H, dtype=jnp.float32) * STRIDE) / Hp
            ref_x = (base + jnp.arange(W, dtype=jnp.float32) * STRIDE) / Wp
            ref = jnp.stack([jnp.broadcast_to(ref_x[None, :], (H, W)), jnp.broadcast_to(ref_y[:, None], (H, W))], -1)
            lin = jnp.arange(K, dtype=jnp.float32) * DIL - DIL * (K - 1) // 2
            gx, gy = jnp.meshgrid(lin, lin, indexing='ij')
            dil_grid = jnp.stack([gx / Wp, gy / Hp], -1).reshape(P, 2)
            loc = ref[:, :, None, None, :] + dil_grid[None, None, None, :, :]
            loc = jnp.broadcast_to(loc, (H, W, G, P, 2))[None]
            norm = jnp.array([Wp, Hp], jnp.float32)
            loc = loc + offset.reshape(B, H, W, G, P, 2) / norm
            sg = 2.0 * loc - 1.0
            xin = xp.reshape(B, Hp, Wp, G, GC).transpose(0, 3, 4, 1, 2).reshape(B * G, GC, Hp, Wp)
            sgf = sg.reshape(B, H * W, G, P, 2).transpose(0, 2, 1, 3, 4).reshape(B * G, H * W, P, 2)
            sampled = jax.vmap(_bilinear_sample)(xin, sgf)
            m = mask.reshape(B, H * W, G, P).transpose(0, 2, 1, 3).reshape(B * G, 1, H * W, P)
            out = (sampled * m).sum(-1)
            return out.reshape(B, G, GC, H * W).transpose(0, 3, 1, 2).reshape(B, H, W, C)

        def _dcn(x, inproj_w, inproj_b, dw_w, dw_b, ln_g, ln_b, off_w, off_b, mask_w, mask_b, outproj_w, outproj_b):
            xproj = x @ inproj_w + inproj_b
            x1 = _dwconv(x.transpose(0, 3, 1, 2), dw_w, dw_b, (DWK - 1) // 2).transpose(0, 2, 3, 1)
            x1 = jax.nn.gelu(_ln(x1, ln_g, ln_b), approximate=False)
            offset = x1 @ off_w + off_b
            m = jax.nn.softmax((x1 @ mask_w + mask_b).reshape(B, H, W, G, P), -1).reshape(B, H, W, G * P)
            out = _dcnv3_core(xproj, offset, m)
            return out @ outproj_w + outproj_b

        def _forward(x, proj1_w, proj1_b, conv0_w, conv0_b, inproj_w, inproj_b, dw_w, dw_b, ln_g, ln_b, off_w, off_b, mask_w, mask_b, outproj_w, outproj_b, conv_w, conv_b, proj2_w, proj2_b):
            shortcut = x
            h = jax.nn.gelu(_conv1x1(x, proj1_w, proj1_b), approximate=False)
            u = h
            h = _dwconv(h, conv0_w, conv0_b, 2)
            attn = _dcn(h.transpose(0, 2, 3, 1), inproj_w, inproj_b, dw_w, dw_b, ln_g, ln_b, off_w, off_b, mask_w, mask_b, outproj_w, outproj_b)
            attn = _conv1x1(attn.transpose(0, 3, 1, 2), conv_w, conv_b)
            h = _conv1x1(u * attn, proj2_w, proj2_b)
            return h + shortcut
        key = jax.random.key(seed)
        ks = jax.random.split(key, 12)
        s = lambda k, shape, fan: jax.random.normal(k, shape, jnp.float32) / np.sqrt(fan)
        return {'x': jax.random.normal(ks[0], (B, C, H, W), jnp.float32), 'proj1_w': s(ks[1], (C, C), C), 'proj1_b': jnp.zeros((C,), jnp.float32), 'conv0_w': s(ks[2], (C, 1, 5, 5), 25), 'conv0_b': jnp.zeros((C,), jnp.float32), 'inproj_w': s(ks[3], (C, C), C), 'inproj_b': jnp.zeros((C,), jnp.float32), 'dw_w': s(ks[4], (C, 1, DWK, DWK), DWK * DWK), 'dw_b': jnp.zeros((C,), jnp.float32), 'ln_g': jnp.ones((C,), jnp.float32), 'ln_b': jnp.zeros((C,), jnp.float32), 'off_w': s(ks[5], (C, G * P * 2), C) * 0.1, 'off_b': jnp.zeros((G * P * 2,), jnp.float32), 'mask_w': s(ks[6], (C, G * P), C), 'mask_b': jnp.zeros((G * P,), jnp.float32), 'outproj_w': s(ks[7], (C, C), C), 'outproj_b': jnp.zeros((C,), jnp.float32), 'conv_w': s(ks[8], (C, C), C), 'conv_b': jnp.zeros((C,), jnp.float32), 'proj2_w': s(ks[9], (C, C), C), 'proj2_b': jnp.zeros((C,), jnp.float32)}
    _L0_conv_all = _L0_conv_setup()
    _L0_conv_in = {k: v for k, v in _L0_conv_all.items() if k in ('proj1_w', 'proj1_b', 'conv0_w', 'conv0_b', 'inproj_w', 'inproj_b', 'dw_w', 'dw_b', 'ln_g', 'ln_b', 'off_w', 'off_b', 'mask_w', 'mask_b', 'outproj_w', 'outproj_b', 'conv_w', 'conv_b', 'proj2_w', 'proj2_b')}
    del _L0_conv_all

    def _L1_attn_setup():
        import jax, jax.numpy as jnp
        import numpy as np
        F_DIM = 64
        key = jax.random.key(seed)
        ks = jax.random.split(key, 8)
        B, S, F = (8, 512, F_DIM)
        scale = 1.0 / np.sqrt(F)
        return {'x': jax.random.normal(ks[0], (B, S, F), dtype=jnp.float32), 'att_w': jax.random.normal(ks[1], (3 * F,), dtype=jnp.float32) * scale, 'z_w': jax.random.normal(ks[2], (F, 2 * F), dtype=jnp.float32) * scale, 'z_b': jax.random.normal(ks[3], (F,), dtype=jnp.float32) * 0.01, 'r_w': jax.random.normal(ks[4], (F, 2 * F), dtype=jnp.float32) * scale, 'r_b': jax.random.normal(ks[5], (F,), dtype=jnp.float32) * 0.01, 'f_w': jax.random.normal(ks[6], (F, 2 * F), dtype=jnp.float32) * scale, 'f_b': jax.random.normal(ks[7], (F,), dtype=jnp.float32) * 0.01}
    _L1_attn_all = _L1_attn_setup()
    _L1_attn_in = {k: v for k, v in _L1_attn_all.items() if k in ('att_w', 'z_w', 'z_b', 'r_w', 'r_b', 'f_w', 'f_b')}
    del _L1_attn_all

    def _L1_ffn_setup():
        import jax, jax.numpy as jnp
        import numpy as np
        NUM_EXPERTS = 8
        TOP_K = 2
        B, S, D = (8, 2048, 64)

        def _moe(tokens, router_w, w1, b1, w2, b2):
            N = tokens.shape[0]
            E = router_w.shape[0]
            logits = tokens.astype(jnp.float32) @ router_w.astype(jnp.float32).T
            probs = jax.nn.softmax(logits, axis=-1)
            rw, re = jax.lax.top_k(probs, TOP_K)
            if TOP_K > 1:
                rw = rw / jnp.maximum(rw.sum(-1, keepdims=True), 1e-12)
            rw = rw.astype(tokens.dtype)
            combine = jnp.zeros((N, E), tokens.dtype).at[jnp.arange(N)[:, None], re].set(rw)
            out = tokens
            for e in range(E):
                h = jax.nn.gelu(tokens @ w1[e] + b1[e], approximate=False)
                y = h @ w2[e] + b2[e]
                out = out + combine[:, e:e + 1] * y
            return out
        key = jax.random.key(seed)
        ks = jax.random.split(key, 4)
        scale = 1.0 / np.sqrt(D).astype(np.float32)
        return {'input_embeddings': jax.random.normal(ks[0], (B, S, D), jnp.float32), 'router_w': jax.random.normal(ks[1], (NUM_EXPERTS, D), jnp.float32) * scale, 'w1': jax.random.normal(ks[2], (NUM_EXPERTS, D, D), jnp.float32) * scale, 'b1': jnp.zeros((NUM_EXPERTS, D), jnp.float32), 'w2': jax.random.normal(ks[3], (NUM_EXPERTS, D, D), jnp.float32) * scale, 'b2': jnp.zeros((NUM_EXPERTS, D), jnp.float32)}
    _L1_ffn_all = _L1_ffn_setup()
    _L1_ffn_in = {k: v for k, v in _L1_ffn_all.items() if k in ('router_w', 'w1', 'b1', 'w2', 'b2')}
    del _L1_ffn_all
    return {'x': x, 'L0_conv_proj1_w': _L0_conv_in['proj1_w'], 'L0_conv_proj1_b': _L0_conv_in['proj1_b'], 'L0_conv_conv0_w': _L0_conv_in['conv0_w'], 'L0_conv_conv0_b': _L0_conv_in['conv0_b'], 'L0_conv_inproj_w': _L0_conv_in['inproj_w'], 'L0_conv_inproj_b': _L0_conv_in['inproj_b'], 'L0_conv_dw_w': _L0_conv_in['dw_w'], 'L0_conv_dw_b': _L0_conv_in['dw_b'], 'L0_conv_ln_g': _L0_conv_in['ln_g'], 'L0_conv_ln_b': _L0_conv_in['ln_b'], 'L0_conv_off_w': _L0_conv_in['off_w'], 'L0_conv_off_b': _L0_conv_in['off_b'], 'L0_conv_mask_w': _L0_conv_in['mask_w'], 'L0_conv_mask_b': _L0_conv_in['mask_b'], 'L0_conv_outproj_w': _L0_conv_in['outproj_w'], 'L0_conv_outproj_b': _L0_conv_in['outproj_b'], 'L0_conv_conv_w': _L0_conv_in['conv_w'], 'L0_conv_conv_b': _L0_conv_in['conv_b'], 'L0_conv_proj2_w': _L0_conv_in['proj2_w'], 'L0_conv_proj2_b': _L0_conv_in['proj2_b'], 'L1_attn_att_w': _L1_attn_in['att_w'], 'L1_attn_z_w': _L1_attn_in['z_w'], 'L1_attn_z_b': _L1_attn_in['z_b'], 'L1_attn_r_w': _L1_attn_in['r_w'], 'L1_attn_r_b': _L1_attn_in['r_b'], 'L1_attn_f_w': _L1_attn_in['f_w'], 'L1_attn_f_b': _L1_attn_in['f_b'], 'L1_ffn_router_w': _L1_ffn_in['router_w'], 'L1_ffn_w1': _L1_ffn_in['w1'], 'L1_ffn_b1': _L1_ffn_in['b1'], 'L1_ffn_w2': _L1_ffn_in['w2'], 'L1_ffn_b2': _L1_ffn_in['b2']}

def reference(x, L0_conv_proj1_w, L0_conv_proj1_b, L0_conv_conv0_w, L0_conv_conv0_b, L0_conv_inproj_w, L0_conv_inproj_b, L0_conv_dw_w, L0_conv_dw_b, L0_conv_ln_g, L0_conv_ln_b, L0_conv_off_w, L0_conv_off_b, L0_conv_mask_w, L0_conv_mask_b, L0_conv_outproj_w, L0_conv_outproj_b, L0_conv_conv_w, L0_conv_conv_b, L0_conv_proj2_w, L0_conv_proj2_b, L1_attn_att_w, L1_attn_z_w, L1_attn_z_b, L1_attn_r_w, L1_attn_r_b, L1_attn_f_w, L1_attn_f_b, L1_ffn_router_w, L1_ffn_w1, L1_ffn_b1, L1_ffn_w2, L1_ffn_b2):
    import jax
    import jax.numpy as jnp

    def _L0_conv_ref(x, proj1_w, proj1_b, conv0_w, conv0_b, inproj_w, inproj_b, dw_w, dw_b, ln_g, ln_b, off_w, off_b, mask_w, mask_b, outproj_w, outproj_b, conv_w, conv_b, proj2_w, proj2_b):
        import jax, jax.numpy as jnp
        import numpy as np
        B, C, H, W = (4, 64, 16, 16)
        G, K, PAD, STRIDE, DIL, DWK = (8, 3, 1, 1, 1, 3)
        P = K * K
        GC = C // G

        def _dwconv(x, w, b, pad):
            y = jax.lax.conv_general_dilated(x, w, (1, 1), [(pad, pad), (pad, pad)], feature_group_count=C, dimension_numbers=('NCHW', 'OIHW', 'NCHW'))
            return y + b[None, :, None, None]

        def _conv1x1(x, w, b):
            return jnp.einsum('bchw,cd->bdhw', x, w) + b[None, :, None, None]

        def _ln(x, g, b, eps=1e-05):
            mu = x.mean(-1, keepdims=True)
            var = ((x - mu) ** 2).mean(-1, keepdims=True)
            return (x - mu) * jax.lax.rsqrt(var + eps) * g + b

        def _bilinear_sample(img, grid):
            gc, Hp, Wp = img.shape
            ix = ((grid[..., 0] + 1.0) * Wp - 1.0) * 0.5
            iy = ((grid[..., 1] + 1.0) * Hp - 1.0) * 0.5
            x0 = jnp.floor(ix)
            y0 = jnp.floor(iy)
            x1 = x0 + 1.0
            y1 = y0 + 1.0
            imgf = img.reshape(gc, Hp * Wp)

            def gather(yy, xx):
                valid = (xx >= 0) & (xx <= Wp - 1) & (yy >= 0) & (yy <= Hp - 1)
                xi = jnp.clip(xx, 0, Wp - 1).astype(jnp.int32)
                yi = jnp.clip(yy, 0, Hp - 1).astype(jnp.int32)
                return imgf[:, yi * Wp + xi] * valid
            w00 = (x1 - ix) * (y1 - iy)
            w01 = (ix - x0) * (y1 - iy)
            w10 = (x1 - ix) * (iy - y0)
            w11 = (ix - x0) * (iy - y0)
            return gather(y0, x0) * w00 + gather(y0, x1) * w01 + gather(y1, x0) * w10 + gather(y1, x1) * w11

        def _dcnv3_core(x, offset, mask):
            xp = jnp.pad(x, ((0, 0), (PAD, PAD), (PAD, PAD), (0, 0)))
            Hp, Wp = (H + 2 * PAD, W + 2 * PAD)
            base = DIL * (K - 1) // 2 + 0.5
            ref_y = (base + jnp.arange(H, dtype=jnp.float32) * STRIDE) / Hp
            ref_x = (base + jnp.arange(W, dtype=jnp.float32) * STRIDE) / Wp
            ref = jnp.stack([jnp.broadcast_to(ref_x[None, :], (H, W)), jnp.broadcast_to(ref_y[:, None], (H, W))], -1)
            lin = jnp.arange(K, dtype=jnp.float32) * DIL - DIL * (K - 1) // 2
            gx, gy = jnp.meshgrid(lin, lin, indexing='ij')
            dil_grid = jnp.stack([gx / Wp, gy / Hp], -1).reshape(P, 2)
            loc = ref[:, :, None, None, :] + dil_grid[None, None, None, :, :]
            loc = jnp.broadcast_to(loc, (H, W, G, P, 2))[None]
            norm = jnp.array([Wp, Hp], jnp.float32)
            loc = loc + offset.reshape(B, H, W, G, P, 2) / norm
            sg = 2.0 * loc - 1.0
            xin = xp.reshape(B, Hp, Wp, G, GC).transpose(0, 3, 4, 1, 2).reshape(B * G, GC, Hp, Wp)
            sgf = sg.reshape(B, H * W, G, P, 2).transpose(0, 2, 1, 3, 4).reshape(B * G, H * W, P, 2)
            sampled = jax.vmap(_bilinear_sample)(xin, sgf)
            m = mask.reshape(B, H * W, G, P).transpose(0, 2, 1, 3).reshape(B * G, 1, H * W, P)
            out = (sampled * m).sum(-1)
            return out.reshape(B, G, GC, H * W).transpose(0, 3, 1, 2).reshape(B, H, W, C)

        def _dcn(x, inproj_w, inproj_b, dw_w, dw_b, ln_g, ln_b, off_w, off_b, mask_w, mask_b, outproj_w, outproj_b):
            xproj = x @ inproj_w + inproj_b
            x1 = _dwconv(x.transpose(0, 3, 1, 2), dw_w, dw_b, (DWK - 1) // 2).transpose(0, 2, 3, 1)
            x1 = jax.nn.gelu(_ln(x1, ln_g, ln_b), approximate=False)
            offset = x1 @ off_w + off_b
            m = jax.nn.softmax((x1 @ mask_w + mask_b).reshape(B, H, W, G, P), -1).reshape(B, H, W, G * P)
            out = _dcnv3_core(xproj, offset, m)
            return out @ outproj_w + outproj_b

        def _forward(x, proj1_w, proj1_b, conv0_w, conv0_b, inproj_w, inproj_b, dw_w, dw_b, ln_g, ln_b, off_w, off_b, mask_w, mask_b, outproj_w, outproj_b, conv_w, conv_b, proj2_w, proj2_b):
            shortcut = x
            h = jax.nn.gelu(_conv1x1(x, proj1_w, proj1_b), approximate=False)
            u = h
            h = _dwconv(h, conv0_w, conv0_b, 2)
            attn = _dcn(h.transpose(0, 2, 3, 1), inproj_w, inproj_b, dw_w, dw_b, ln_g, ln_b, off_w, off_b, mask_w, mask_b, outproj_w, outproj_b)
            attn = _conv1x1(attn.transpose(0, 3, 1, 2), conv_w, conv_b)
            h = _conv1x1(u * attn, proj2_w, proj2_b)
            return h + shortcut
        return _forward(x, proj1_w, proj1_b, conv0_w, conv0_b, inproj_w, inproj_b, dw_w, dw_b, ln_g, ln_b, off_w, off_b, mask_w, mask_b, outproj_w, outproj_b, conv_w, conv_b, proj2_w, proj2_b)

    def _L1_attn_ref(x, att_w, z_w, z_b, r_w, r_b, f_w, f_b):
        import jax, jax.numpy as jnp
        import numpy as np
        F_DIM = 64
        F = x.shape[-1]
        wa, wb, wc = (att_w[:F], att_w[F:2 * F], att_w[2 * F:])
        a = jnp.einsum('bif,f->bi', x, wa)
        b = jnp.einsum('bjf,f->bj', x, wb)
        c = jnp.einsum('bif,bjf->bij', x * wc, x)
        scores = a[:, :, None] + b[:, None, :] + c
        attn_weight = jax.nn.softmax(scores, axis=2)
        attn = jnp.einsum('bij,bjf->bif', attn_weight, x)
        cat = jnp.concatenate([x, attn], axis=-1)
        z = jnp.tanh(jnp.einsum('bsg,fg->bsf', cat, z_w) + z_b)
        r = jax.nn.sigmoid(jnp.einsum('bsg,fg->bsf', cat, r_w) + r_b)
        f = jax.nn.sigmoid(jnp.einsum('bsg,fg->bsf', cat, f_w) + f_b)
        return r * x + f * z

    def _L1_ffn_ref(input_embeddings, router_w, w1, b1, w2, b2):
        import jax, jax.numpy as jnp
        import numpy as np
        NUM_EXPERTS = 8
        TOP_K = 2
        B, S, D = (8, 2048, 64)

        def _moe(tokens, router_w, w1, b1, w2, b2):
            N = tokens.shape[0]
            E = router_w.shape[0]
            logits = tokens.astype(jnp.float32) @ router_w.astype(jnp.float32).T
            probs = jax.nn.softmax(logits, axis=-1)
            rw, re = jax.lax.top_k(probs, TOP_K)
            if TOP_K > 1:
                rw = rw / jnp.maximum(rw.sum(-1, keepdims=True), 1e-12)
            rw = rw.astype(tokens.dtype)
            combine = jnp.zeros((N, E), tokens.dtype).at[jnp.arange(N)[:, None], re].set(rw)
            out = tokens
            for e in range(E):
                h = jax.nn.gelu(tokens @ w1[e] + b1[e], approximate=False)
                y = h @ w2[e] + b2[e]
                out = out + combine[:, e:e + 1] * y
            return out
        b, s, d = input_embeddings.shape
        tokens = input_embeddings.reshape(b * s, d)
        return _moe(tokens, router_w, w1, b1, w2, b2).reshape(b, s, d)

    def _gn(v, G=32, eps=1e-05):
        B_, C_, H_, W_ = v.shape
        g = v.reshape(B_, G, C_ // G, H_, W_)
        m = jnp.mean(g, axis=(2, 3, 4), keepdims=True)
        s = jnp.var(g, axis=(2, 3, 4), keepdims=True)
        return ((g - m) / jnp.sqrt(s + eps)).reshape(v.shape)

    def _ln_c(v, eps=1e-06):
        m = jnp.mean(v, axis=1, keepdims=True)
        s = jnp.var(v, axis=1, keepdims=True)
        return (v - m) / jnp.sqrt(s + eps)

    def _ln_t(v, eps=1e-05):
        m = jnp.mean(v, axis=-1, keepdims=True)
        s = jnp.var(v, axis=-1, keepdims=True)
        return (v - m) / jnp.sqrt(s + eps)

    def _to_tokens(v):
        B_, C_, H_, W_ = v.shape
        return v.reshape(B_, C_, H_ * W_).transpose(0, 2, 1)

    def _from_tokens(t, like):
        B_, C_, H_, W_ = like.shape
        return t.transpose(0, 2, 1).reshape(B_, C_, H_, W_)
    x = _L0_conv_ref(x, L0_conv_proj1_w, L0_conv_proj1_b, L0_conv_conv0_w, L0_conv_conv0_b, L0_conv_inproj_w, L0_conv_inproj_b, L0_conv_dw_w, L0_conv_dw_b, L0_conv_ln_g, L0_conv_ln_b, L0_conv_off_w, L0_conv_off_b, L0_conv_mask_w, L0_conv_mask_b, L0_conv_outproj_w, L0_conv_outproj_b, L0_conv_conv_w, L0_conv_conv_b, L0_conv_proj2_w, L0_conv_proj2_b)
    t = _to_tokens(x)
    t = t + _L1_attn_ref(_ln_t(t), L1_attn_att_w, L1_attn_z_w, L1_attn_z_b, L1_attn_r_w, L1_attn_r_b, L1_attn_f_w, L1_attn_f_b)
    t = t + _L1_ffn_ref(_ln_t(t), L1_ffn_router_w, L1_ffn_w1, L1_ffn_b1, L1_ffn_w2, L1_ffn_b2)
    x = _from_tokens(t, x)
    return x

_drawn_inputs = setup_inputs


def setup_inputs(seed=0):
    import zlib

    import numpy as np

    out = dict(_drawn_inputs(seed))
    spreads = {'L0_conv_proj1_b': (0.0, 0.1),
     'L0_conv_conv0_b': (0.0, 0.1),
     'L0_conv_inproj_b': (0.0, 0.1),
     'L0_conv_dw_b': (0.0, 0.37),
     'L0_conv_ln_g': (1.0, 0.6),
     'L0_conv_ln_b': (0.0, 0.516),
     'L0_conv_off_b': (0.0, 0.1),
     'L0_conv_outproj_b': (0.0, 0.1),
     'L0_conv_conv_b': (0.0, 0.1),
     'L0_conv_proj2_b': (0.0, 0.1),
     'L1_ffn_b1': (0.0, 0.419),
     'L1_ffn_b2': (0.0, 0.274)}
    factors = {'L1_attn_z_b': 5.605, 'L1_attn_r_b': 22.499, 'L1_attn_f_b': 31.15}
    for name, (base, spread) in spreads.items():
        noise = np.random.default_rng([zlib.crc32(name.encode()), seed]).standard_normal(out[name].shape)
        drawn = base * np.exp(spread * noise) if base else spread * noise
        out[name] = jnp.asarray(drawn.astype(out[name].dtype))
    for name, factor in factors.items():
        out[name] = (out[name] * factor).astype(out[name].dtype)
    return out
```

```python
from contextlib import ExitStack

import concourse.bass as bass
from concourse import mybir

ALU = mybir.AluOpType
ACT = mybir.ActivationFunctionType
AX_X = mybir.AxisListType.X
F32 = mybir.dt.float32
I32 = mybir.dt.int32

P = 128
B, C, H, W = 4, 64, 16, 16
BL = 2
HW = H * W
N = BL * HW
G, GC, K3 = 8, 8, 3
NP_ = K3 * K3
XL = 8
XH = W // XL
OM = 3 * G * NP_
E = 8
EP = E // 2
K5 = 5
UP, UR = W + 4, 2 * H + 6
HP_, HR = W + 2, 2 * H + 3
UA = 2 * H + 2
HA = 2 * H + 1
VP = W + 4
VWX = XL + 4
PE5, PE3 = 11, 4
XG = XL * G
OFF = 2 * NP_ * XG

FIELDS = [
    ("proj1", P), ("w5", 25), ("w3", 9), ("b_proj1", 1), ("b_conv0", 1), ("b_dw", 1), ("g_ln", 1), ("b_ln", 1),
    ("eps", 1), ("one", 1), ("minus_one", 1), ("b_proj2", 1), ("b_outproj", 1), ("b_conv", 1), ("wa", 1), ("wb", 1), ("wc", 1),
    ("b_z", 1), ("b_r", 1), ("b_f", 1), ("b1", EP),
    ("ident", P), ("center", P), ("mean", P),
    ("inproj", C), ("b_inproj", C), ("offmask", OM), ("b_offmask", OM),
    ("outproj_t", P), ("conv", P), ("proj2", P), ("proj2_t", P),
    ("zx", P), ("za", P), ("rx", P), ("ra", P), ("fx", P), ("fa", P),
    ("w1", EP * P), ("w2", EP * C), ("router", E), ("b2", C), ("pick", EP * P),
    ("base", 2 * NP_ * XL), ("grid", W),
]
COL = {}
_at = 0
for _name, _width in FIELDS:
    COL[_name] = (_at, _width)
    _at += _width
NCOL = _at
CUTS = [0, COL["ident"][0], COL["inproj"][0], COL["outproj_t"][0], COL["w1"][0], NCOL]


def conv_attn_moe(nc, A_x, A_w, v_dram, out):
    ctx = ExitStack()
    with ctx:
        def sb(name, shape, dt=F32):
            return ctx.enter_context(nc.sbuf_tensor(name, shape, dt))

        def sem(name):
            return ctx.enter_context(nc.semaphore(name))

        wts = sb("wts", [P, NCOL])

        def w(name, a=0, b=None):
            at, width = COL[name]
            return wts[:, at + a:at + (width if b is None else b)]

        def wr(name, p0, p1, a=0, b=None):
            at, width = COL[name]
            return wts[p0:p1, at + a:at + (width if b is None else b)]

        x_in = sb("x_in", [P, N])
        ones = sb("ones", [1, P])
        zeros = sb("zeros", [P, B * VP * VP * C // P])
        diag5 = sb("diag5", [P, PE5, P])
        cen3 = sb("cen3", [P, PE3, P])
        w_oc = sb("w_oc", [P, P])
        b_oc = sb("b_oc", [P, 1])
        w2c = sb("w2c", [P, P])
        half_rf = sb("half_rf", [P, 2])
        warm = sb("warm", [1, 16])

        upad = sb("upad", [P, UR, UP])
        u_dense = sb("u_dense", [P, N])
        acc5 = sb("acc5", [P, UA, W])
        hpad = sb("hpad", [P, HR, HP_])
        h_dense = sb("h_dense", [P, N])
        acc3 = sb("acc3", [P, HA, W])
        sq = sb("sq", [P, N])
        std = sb("std", [P, N])
        xn = sb("xn", [P, N])
        x1 = sb("x1", [P, N])
        v_tok = sb("v_tok", [P, XL * C])
        v_win = sb("v_win", [P, K5, VWX * C])
        lg = sb("lg", [P, NP_, XG])
        lmax = sb("lmax", [P, XG])
        lsub = sb("lsub", [P, NP_, XG])
        prob = sb("prob", [P, NP_, XG])
        psum_p = sb("psum_p", [P, XG])
        rsum = sb("rsum", [P, XG])
        hat = sb("hat", [P, K3, 2, NP_, XG])
        o_abs = sb("o_abs", [P, 2 * NP_ * XG])
        over_sum = sb("over_sum", [P, 1])
        far = sb("far", [1, 1], I32)
        ym = sb("ym", [P, K3, NP_ * XG])
        terms = sb("terms", [P, K3, K3, NP_ * XG])
        a5 = sb("a5", [P, K5, K5, XG])
        prod = sb("prod", [P, K5, K5, XL * C])
        samp = sb("samp", [P, XL * C])
        samp_t = sb("samp_t", [P, N])
        zu = sb("zu", [P, N])
        xb = sb("xb", [P, N])

        s_pos = sb("s_pos", [P, 2, NP_, XG])
        s_hy = sb("s_hy", [P, NP_, XG])
        s_hx = sb("s_hx", [P, NP_, XG])
        s_v = sb("s_v", [P, W * C])
        s_term = sb("s_term", [P, XL * C])

        prod_flat = prod[:, :, :, :].rearrange("p y x c -> p (y x c)")
        terms_flat = terms[:, :, :, :].rearrange("p x y c -> p (x y c)")
        taken = {"prod": 0, "terms": 0}

        def late(*shape, place="prod"):
            size = 1
            for n in shape:
                size *= n
            at = taken[place]
            flat = (prod_flat if place == "prod" else terms_flat)[:, at:at + size]
            taken[place] += size
            return flat if len(shape) == 1 else flat.rearrange("p (a n) -> p a n", a=shape[0])

        t0 = late(N, place="terms")
        xh = late(N, place="terms")
        q = late(N, place="terms")
        xh_tok = late(4, P, place="terms")
        smax = sb("smax", [P, 8])
        a_col = sb("a_col", [P, 8])
        stop_ = sb("stop_", [P, 8])
        nbias = sb("nbias", [P, 8])
        pr = late(8, HW)
        prsum = sb("prsum", [P, 8])
        prinv = sb("prinv", [P, 8])
        prT = late(B, 2 * HW)
        att = late(N)
        zt = late(N)
        rt = late(N)
        ft = late(N)
        rx_ = late(N)
        fz_ = late(N)
        gsum = late(N)
        t2 = late(N, place="terms")
        sq2 = late(N)
        std2 = late(N)
        sq3 = late(N)
        std3 = late(N)
        x2 = late(N)
        base_out = late(N, place="terms")
        rl = sb("rl", [P, 8, E])
        rmax = sb("rmax", [P, 8])
        rsub = sb("rsub", [P, 8, E])
        rexp = sb("rexp", [P, 8, E])
        rs = sb("rs", [P, 8])
        rinv = sb("rinv", [P, 8])
        rp = sb("rp", [P, 8, E])
        m1 = sb("m1", [P, 8])
        e1 = sb("e1", [P, 8, E])
        r1 = sb("r1", [P, 8, E])
        k1 = sb("k1", [P, 8])
        p1 = sb("p1", [P, 8, E])
        rest = sb("rest", [P, 8, E])
        m2 = sb("m2", [P, 8])
        e2 = sb("e2", [P, 8, E])
        r2 = sb("r2", [P, 8, E])
        k2 = sb("k2", [P, 8])
        p2 = sb("p2", [P, 8, E])
        both = sb("both", [P, 8, E])
        tot = sb("tot", [P, 8])
        tinv = sb("tinv", [P, 8])
        csel = sb("csel", [P, 8, E])
        comb = sb("comb", [P, 8, E])
        rank = sb("rank", [P, E])
        comb_t = late(2, N, place="terms")
        h_act = late(2, N)
        h_cmb = late(2, N)
        res = late(N)

        ps = ctx.enter_context(nc.psum_tensor("ps", [P, 8, 512], F32))

        x_loaded = sem("x_loaded")
        w_loaded = [sem(f"w_loaded{i}") for i in range(len(CUTS) - 1)]
        pads_zero = sem("pads_zero")
        zeros_set = sem("zeros_set")
        v_cleared = sem("v_cleared")
        consts_set = sem("consts_set")
        diag5_set = sem("diag5_set")
        cen3_set = sem("cen3_set")
        half_set = sem("half_set")
        proj1_done = sem("proj1_done")
        u_ready = sem("u_ready")
        u_copied = sem("u_copied")
        xb_ready = sem("xb_ready")
        acc5_step = sem("acc5_step")
        conv5_done = sem("conv5_done")
        h_ready = sem("h_ready")
        h_copied = sem("h_copied")
        acc3_step = sem("acc3_step")
        combos_done = sem("combos_done")
        combos_copied = sem("combos_copied")
        d1_done = sem("d1_done")
        v_done = sem("v_done")
        v_copied = sem("v_copied")
        v_stored = sem("v_stored")
        v_windowed = sem("v_windowed")
        sq1_done = sem("sq1_done")
        var1_done = sem("var1_done")
        std1_done = sem("std1_done")
        xn_inv = sem("xn_inv")
        xn_done = sem("xn_done")
        x1_done = sem("x1_done")
        off_done = sem("off_done")
        lg_copied = sem("lg_copied")
        hats_done = sem("hats_done")
        abs_done = sem("abs_done")
        near_hat = sem("near_hat")
        lmax_done = sem("lmax_done")
        lsub_done = sem("lsub_done")
        prob_done = sem("prob_done")
        psum_done = sem("psum_done")
        rsum_done = sem("rsum_done")
        ym_done = sem("ym_done")
        terms_done = sem("terms_done")
        a5_step = sem("a5_step")
        prod_done = sem("prod_done")
        samp_done = sem("samp_done")
        samp_read = sem("samp_read")
        over_done = sem("over_done")
        over_total = sem("over_total")
        far_set = sem("far_set")
        slow_done = sem("slow_done")
        slow_loaded = sem("slow_loaded")
        sT_done = sem("sT_done")
        sT_copied = sem("sT_copied")
        attn0_done = sem("attn0_done")
        zu_done = sem("zu_done")
        t0_done = sem("t0_done")
        t0_copied = sem("t0_copied")
        sq2_done = sem("sq2_done")
        var2_done = sem("var2_done")
        std2_done = sem("std2_done")
        xh_inv = sem("xh_inv")
        xh_done = sem("xh_done")
        q_done = sem("q_done")
        xtok_done = sem("xtok_done")
        xtok_copied = sem("xtok_copied")
        acol_done = sem("acol_done")
        acol_copied = sem("acol_copied")
        scores_done = sem("scores_done")
        smax_done = sem("smax_done")
        stop_done = sem("stop_done")
        nbias_done = sem("nbias_done")
        exp_done = sem("exp_done")
        prinv_done = sem("prinv_done")
        pnorm_done = sem("pnorm_done")
        pT_done = sem("pT_done")
        pT_copied = sem("pT_copied")
        att_done = sem("att_done")
        att_copied = sem("att_copied")
        gates_done = sem("gates_done")
        z_done = sem("z_done")
        r_done = sem("r_done")
        f_done = sem("f_done")
        mix_step = sem("mix_step")
        t2_done = sem("t2_done")
        d3_done = sem("d3_done")
        sq3_done = sem("sq3_done")
        var3_done = sem("var3_done")
        std3_done = sem("std3_done")
        x2_inv = sem("x2_inv")
        x2_done = sem("x2_done")
        base_done = sem("base_done")
        route_done = sem("route_done")
        route_step = sem("route_step")
        rexp_done = sem("rexp_done")
        comb_done = sem("comb_done")
        combT_done = sem("combT_done")
        combT_copied = sem("combT_copied")
        hid_done = sem("hid_done")
        gelu_done = sem("gelu_done")
        spread_done = sem("spread_done")
        hcmb_done = sem("hcmb_done")
        y_done = sem("y_done")
        res_done = sem("res_done")
        out_stored = sem("out_stored")
        pool_step = sem("pool_step")

        def img(ap, rows, width):
            return ap

        def u_in(rows, dy, dx):
            return upad[:, dy:dy + rows, dx:dx + W]

        def u_img(dy, dx):
            return upad[:, dy:dy + 2 * (H + 2), dx:dx + W].rearrange("p (b r) x -> p b r x", b=BL)[:, :, 0:H, :]

        def h_in(rows, dy, dx):
            return hpad[:, dy:dy + rows, dx:dx + W]

        def h_img(dy, dx):
            r = hpad[:, dy:dy + H, dx:dx + W]
            r2 = hpad[:, dy + H + 1:dy + H + 1 + H, dx:dx + W]
            return r, r2

        def psi(bank):
            return ps[:, bank, :].rearrange("p (b y x) -> p b y x", b=BL, y=H)

        def tokens(tile, p0, p1, xl):
            return tile[p0:p1, xl:N:XL]

        om_ps = ps[:, 4:8, :].rearrange("p b (k c) -> p (b k) c", k=2)
        off_ps = om_ps[:, :, 0:2 * NP_ * G].rearrange("p x (q g) -> p q x g", g=G)
        msk_ps = om_ps[:, :, 2 * NP_ * G:OM].rearrange("p x (q g) -> p q x g", g=G)

        block = ctx.enter_context(nc.Block())

        @block.sync
        def _(sp):
            sp.dma_start(x_in[:, :], A_x).then_inc(x_loaded, 16)
            for i in (1, 3):
                sp.dma_start(wts[:, CUTS[i]:CUTS[i + 1]], A_w[:, CUTS[i]:CUTS[i + 1]]).then_inc(w_loaded[i], 16)
            sp.wait_ge(zeros_set, 1)
            sp.dma_start(v_dram.rearrange("b y x c -> (b y x c)").rearrange("(p n) -> p n", p=P),
                         zeros[:, :]).then_inc(v_cleared, 16)
            sp.wait_ge(v_cleared, 16)
            sp.wait_ge(v_copied, 1)
            for b in range(B):
                inside = v_dram[b, 2:2 + H, 2:2 + W, :].rearrange("y x c -> y (x c)")
                for xhi in range(XH):
                    p0 = b * 32 + xhi
                    sp.dma_start(inside[:, xhi * XL * C:(xhi + 1) * XL * C],
                                 v_tok[p0:b * 32 + 32:XH, :]).then_inc(v_stored, 16)
            sp.wait_ge(v_stored, 16 * B * XH)
            for b in range(B):
                rows = v_dram[b].rearrange("y x c -> y (x c)")
                for xhi in range(XH):
                    for dy in range(K5):
                        sp.dma_start(v_win[b * 32 + xhi:b * 32 + 32:XH, dy, :],
                                     rows[dy:dy + H, xhi * XL * C:(xhi * XL + VWX) * C]).then_inc(v_windowed, 16)
            sp.wait_ge(res_done, 1)
            sp.dma_start(out, res[:, :]).then_inc(out_stored, 16)
            sp.wait_ge(out_stored, 16)

        @block.gpsimd
        def _(pool):
            nc.gpsimd.memset(upad[:, :, :], 0.0).then_inc(pads_zero, 1)
            nc.gpsimd.memset(hpad[:, :, :], 0.0).then_inc(pads_zero, 1)
            nc.gpsimd.memset(zeros[:, :], 0.0).then_inc(zeros_set, 1)
            nc.gpsimd.memset(ones[:, :], 1.0).then_inc(consts_set, 1)
            pool.wait_ge(w_loaded[0], 16)
            pool.wait_ge(w_loaded[1], 16)
            nc.gpsimd.tensor_tensor(
                cen3[:, :, :], w("center").unsqueeze(1).broadcast_to([P, PE3, P]),
                w("w3", 0, PE3).unsqueeze(2).broadcast_to([P, PE3, P]), ALU.mult).then_inc(cen3_set, 1)
            pool.wait_ge(x_loaded, 16)
            nc.gpsimd.tensor_scalar(xb[:, :], x_in[:, :], w("b_proj2"), None, ALU.add).then_inc(xb_ready, 1)
            for i, name in enumerate(("b_r", "b_f")):
                nc.gpsimd.tensor_scalar(half_rf[:, i:i + 1], w(name), 0.5, None, ALU.mult).then_inc(half_set, 1)
            for e in range(E):
                nc.gpsimd.memset(rank[:, e:e + 1], float(E - e)).then_inc(consts_set, 1)
            pool.wait_ge(u_ready, 1)
            nc.gpsimd.tensor_copy(u_dense[:, :].rearrange("p (b y x) -> p b y x", b=BL, y=H),
                                  u_img(2, 2)).then_inc(u_copied, 1)
            pool.wait_ge(far_set, 1)
            is_far = pool.value_load(far[0:1, 0:1], min_val=0, max_val=1)
            steps = [0]

            def ordered(ins):
                steps[0] += 1
                ins.then_inc(pool_step, 1)
                pool.wait_ge(pool_step, steps[0])

            with pool.If(is_far > 0):
                pool.wait_ge(w_loaded[4], 16)
                pool.wait_ge(samp_done, 1)
                ordered(nc.gpsimd.tensor_tensor(
                    s_pos[:, :, :, :].rearrange("p c q x -> p (c q x)"),
                    hat[:, 2, :, :, :].rearrange("p c q x -> p (c q x)"),
                    hat[:, 0, :, :, :].rearrange("p c q x -> p (c q x)"), ALU.subtract))
                pos4 = s_pos[:, :, :, :].rearrange("p c q (x g) -> p (c q) x g", g=G)
                base4 = w("base").rearrange("p (q x) -> p q x", x=XL).unsqueeze(3).broadcast_to([P, 2 * NP_, XL, G])
                ordered(nc.gpsimd.tensor_tensor(pos4, pos4, base4, ALU.add))
                nc.gpsimd.memset(samp[:, :], 0.0)
                pool.drain()
                hy = s_hy[:, :, :].rearrange("p q x -> p (q x)")
                hx = s_hx[:, :, :].rearrange("p q x -> p (q x)")
                minus = lsub[:, :, :].rearrange("p q x -> p (q x)")
                g0, gw = COL["grid"]

                def hats(dst, axis, coordinate):
                    at = wts[:, bass.ds(g0 + coordinate, 1)].broadcast_to([P, NP_ * XG])
                    nc.gpsimd.tensor_tensor(dst, s_pos[:, axis, :, :].rearrange("p q x -> p (q x)"), at, ALU.subtract)
                    pool.drain()
                    nc.gpsimd.tensor_scalar(minus, dst, 0.0, None, ALU.min)
                    pool.drain()
                    nc.gpsimd.tensor_scalar(dst, dst, 0.0, None, ALU.max)
                    pool.drain()
                    nc.gpsimd.tensor_tensor(dst, minus, dst, ALU.subtract)
                    pool.drain()
                    nc.gpsimd.tensor_scalar(dst, dst, 1.0, 0.0, ALU.add, ALU.max)
                    pool.drain()

                with pool.Fori(0, H) as y:
                    for b in range(B):
                        row = v_dram[b, :, :, :].rearrange("y x c -> y (x c)")[bass.ds(y + 2, 1), 2 * C:(2 + W) * C]
                        pool.dma_start(s_v[b * 32:(b + 1) * 32, :],
                                       row.broadcast_to([32, W * C])).then_inc(slow_loaded, 16)
                    hats(hy, 1, y)
                    pool.wait_ge(slow_loaded, 16 * B * (y + 1))
                    nc.gpsimd.tensor_tensor(hy, hy, prob[:, :, :].rearrange("p q x -> p (q x)"), ALU.mult)
                    pool.drain()
                    with pool.Fori(0, W) as x:
                        hats(hx, 0, x)
                        nc.gpsimd.tensor_tensor(hx, hx, hy, ALU.mult)
                        pool.drain()
                        for a, b, n in ((0, 4, 4), (0, 2, 2), (0, 1, 1), (0, 8, 1)):
                            nc.gpsimd.tensor_tensor(s_hx[:, a:a + n, :], s_hx[:, a:a + n, :], s_hx[:, b:b + n, :],
                                                    ALU.add)
                            pool.drain()
                        nc.gpsimd.tensor_tensor(
                            s_term[:, :].rearrange("p (x g c) -> p x g c", x=XL, g=G),
                            s_hx[:, 0, :].rearrange("p (x g) -> p x g", g=G).unsqueeze(3).broadcast_to([P, XL, G, GC]),
                            s_v[:, bass.ds(x * C, C)].rearrange("p (g c) -> p g c", g=G).unsqueeze(1)
                            .broadcast_to([P, XL, G, GC]), ALU.mult)
                        pool.drain()
                        nc.gpsimd.tensor_tensor(samp[:, :], samp[:, :], s_term[:, :], ALU.add)
                        pool.drain()
                s3 = samp[:, :].rearrange("p (x c) -> p x c", c=GC)
                nc.gpsimd.tensor_tensor(s3, s3, rsum[:, :].unsqueeze(2).broadcast_to([P, XG, GC]), ALU.mult)
                pool.drain()
            nc.gpsimd.memset(warm[0:1, 15:16], 0.0).then_inc(slow_done, 1)
            pool.wait_ge(x2_done, 1)
            nc.gpsimd.tensor_tensor(base_out[:, :], t2[:, :], x2[:, :], ALU.add).then_inc(base_done, 1)

        @block.scalar
        def _(act):
            act.dma_start(wts[:, CUTS[0]:CUTS[1]], A_w[:, CUTS[0]:CUTS[1]]).then_inc(w_loaded[0], 16)
            for i in (2, 4):
                act.dma_start(wts[:, CUTS[i]:CUTS[i + 1]], A_w[:, CUTS[i]:CUTS[i + 1]]).then_inc(w_loaded[i], 16)

            preloads = [0]

            def preload(func):
                n = preloads[0]
                preloads[0] += 1
                nc.scalar.activation(warm[0:1, n:n + 1], w("eps")[0:1, :], func)

            act.wait_ge(w_loaded[0], 16)
            preload(ACT.Gelu)
            act.wait_ge(proj1_done, 1)
            act.wait_ge(pads_zero, 1)
            nc.scalar.activation(u_img(2, 2), psi(0), ACT.Gelu, bias=w("b_proj1")).then_inc(u_ready, 1)
            preload(ACT.Sqrt)
            act.wait_ge(combos_done, 1)
            nc.scalar.activation(w_oc[:, :], ps[:, 3, 0:P], ACT.Copy)
            nc.scalar.activation(b_oc[:, :], ps[:, 3, P:P + 1], ACT.Identity, bias=w("b_conv"))
            nc.scalar.activation(w2c[:, :], ps[:, 3, 2 * P:3 * P], ACT.Copy).then_inc(combos_copied, 1)
            for bl in range(BL):
                act.wait_ge(h_ready, bl + 1)
                nc.scalar.activation(h_dense[:, bl * HW:(bl + 1) * HW].rearrange("p (y x) -> p y x", y=H),
                                     h_img(1, 1)[bl], ACT.Copy).then_inc(h_copied, 1)
            act.wait_ge(d1_done, 1)
            nc.scalar.activation(sq[:, :], ps[:, 2, :], ACT.Square).then_inc(sq1_done, 1)
            act.wait_ge(var1_done, 1)
            nc.scalar.activation(std[:, :], ps[:, 3, :], ACT.Sqrt, bias=w("eps")).then_inc(std1_done, 1)
            act.wait_ge(v_done, 1)
            nc.scalar.activation(v_tok[:, :], ps[:, 0, :], ACT.Copy).then_inc(v_copied, 1)
            preload(ACT.Gelu)
            act.wait_ge(xn_done, 1)
            nc.scalar.activation(x1[:, :], xn[:, :], ACT.Gelu, bias=w("b_ln"), scale=w("g_ln")).then_inc(x1_done, 1)
            preload(ACT.Exp)
            act.wait_ge(off_done, 1)
            nc.scalar.activation(lg[:, :, :].rearrange("p q (x g) -> p q x g", g=G), msk_ps,
                                 ACT.Copy).then_inc(lg_copied, 1)
            nc.scalar.activation(o_abs[:, :].rearrange("p (q x g) -> p q x g", x=XL, g=G), off_ps,
                                 ACT.Abs).then_inc(abs_done, 1)
            hat_x = [hat[:, k, :, :, :].rearrange("p c q (x g) -> p (c q) x g", g=G) for k in range(K3)]
            nc.scalar.activation(hat_x[2], off_ps, ACT.Relu).then_inc(hats_done, 1)
            act.wait_ge(lsub_done, 1)
            nc.scalar.activation(prob[:, :, :], lsub[:, :, :], ACT.Exp).then_inc(prob_done, 1)
            nc.scalar.activation(hat_x[0], off_ps, ACT.Relu, scale=-1.0).then_inc(hats_done, 1)
            act.wait_ge(abs_done, 1)
            nc.scalar.activation(s_pos[:, :, :, :].rearrange("p c q x -> p (c q x)"), o_abs[:, :], ACT.Relu, bias=w("minus_one"),
                                 accum_out=over_sum[:, :]).then_inc(over_done, 1)
            act.wait_ge(sT_done, 1)
            nc.scalar.activation(samp_t[:, :].rearrange("p (q x) -> p x q", x=XL),
                                 ps[:, 2, :].rearrange("p (x q) -> p x q", x=XL), ACT.Copy).then_inc(sT_copied, 1)
            preload(ACT.Sqrt)
            act.wait_ge(t0_done, 1)
            nc.scalar.activation(sq2[:, :], ps[:, 5, :], ACT.Square).then_inc(sq2_done, 1)
            act.wait_ge(var2_done, 1)
            nc.scalar.activation(std2[:, :], ps[:, 6, :], ACT.Sqrt, bias=w("eps")).then_inc(std2_done, 1)
            preload(ACT.Exp)
            act.wait_ge(xtok_done, 1)
            nc.scalar.activation(xh_tok[:, :, :], ps[:, 7, :].rearrange("p (t c) -> p t c", t=4),
                                 ACT.Copy).then_inc(xtok_copied, 1)
            act.wait_ge(acol_done, 1)
            for bh in range(2):
                nc.scalar.activation(a_col[:, 4 * bh:4 * bh + 4], ps[:, 6 - bh, 4 * bh:4 * bh + 4],
                                     ACT.Copy).then_inc(acol_copied, 1)
            for t in range(8):
                act.wait_ge(nbias_done, t // 2 + 1)
                nc.scalar.activation(pr[:, t, :], ps[:, t // 2, (t % 2) * HW:(t % 2 + 1) * HW], ACT.Exp,
                                     bias=nbias[:, t:t + 1], accum_out=prsum[:, t:t + 1]).then_inc(exp_done, 1)
            for b in range(1, B, 2):
                act.wait_ge(pT_done, b + 1)
                nc.scalar.activation(prT[:, b, :], ps[:, 4 + b, :], ACT.Copy).then_inc(pT_copied, 1)
            act.wait_ge(att_done, 1)
            nc.scalar.activation(att[:, :], ps[:, 0, :], ACT.Copy).then_inc(att_copied, 1)
            act.wait_ge(gates_done, 1)
            nc.scalar.activation(rt[:, :], ps[:, 1, :], ACT.Tanh, bias=half_rf[:, 0:1], scale=0.5).then_inc(r_done, 1)
            act.wait_ge(gates_done, 2)
            nc.scalar.activation(zt[:, :], ps[:, 2, :], ACT.Tanh, bias=w("b_z")).then_inc(z_done, 1)
            act.wait_ge(gates_done, 3)
            nc.scalar.activation(ft[:, :], ps[:, 3, :], ACT.Tanh, bias=half_rf[:, 1:2], scale=0.5).then_inc(f_done, 1)
            preload(ACT.Sqrt)
            act.wait_ge(d3_done, 1)
            nc.scalar.activation(sq3[:, :], ps[:, 4, :], ACT.Square).then_inc(sq3_done, 1)
            act.wait_ge(var3_done, 1)
            nc.scalar.activation(std3[:, :], ps[:, 5, :], ACT.Sqrt, bias=w("eps")).then_inc(std3_done, 1)
            preload(ACT.Exp)
            act.wait_ge(route_step, 4)
            nc.scalar.activation(rexp[:, :, :], rsub[:, :, :], ACT.Exp).then_inc(rexp_done, 1)
            for i in range(2 * EP):
                ep = i // 2
                act.wait_ge(hid_done, i + 1)
                if i >= 2:
                    act.wait_ge(hcmb_done, i - 1)
                nc.scalar.activation(h_act[:, i % 2, :], ps[:, i % 2, :], ACT.Gelu,
                                     bias=w("b1", ep, ep + 1)).then_inc(gelu_done, 1)

        @block.vector
        def _(dve):
            v = nc.vector
            dve.wait_ge(w_loaded[0], 16)
            dve.wait_ge(w_loaded[1], 16)
            v.tensor_tensor(diag5[:, :, :], w("ident").unsqueeze(1).broadcast_to([P, PE5, P]),
                            w("w5", 0, PE5).unsqueeze(2).broadcast_to([P, PE5, P]), ALU.mult).then_inc(diag5_set, 1)
            dve.wait_ge(u_ready, 1)
            for k in range(PE5, 25):
                src = u_in(UA, k // 5, k % 5)
                if k == PE5:
                    v.tensor_scalar(acc5[:, :, :], src, w("w5", k, k + 1), w("b_conv0"), ALU.mult,
                                    ALU.add).then_inc(acc5_step, 1)
                else:
                    dve.wait_ge(acc5_step, k - PE5)
                    v.scalar_tensor_tensor(out=acc5[:, :, :], in0=src, scalar=w("w5", k, k + 1), in1=acc5[:, :, :],
                                           op0=ALU.mult, op1=ALU.add).then_inc(acc5_step, 1)
            dve.wait_ge(acc5_step, 25 - PE5)
            dve.wait_ge(conv5_done, 1)
            dve.wait_ge(pads_zero, 2)
            for bl in range(BL):
                v.tensor_tensor(h_img(1, 1)[bl], psi(1)[:, bl], acc5[:, bl * (H + 2):bl * (H + 2) + H, :],
                                ALU.add).then_inc(h_ready, 1)
            dve.wait_ge(h_ready, 2)
            for k in range(PE3, 9):
                src = h_in(HA, k // 3, k % 3)
                if k == PE3:
                    v.tensor_scalar(acc3[:, :, :], src, w("w3", k, k + 1), w("b_dw"), ALU.mult,
                                    ALU.add).then_inc(acc3_step, 1)
                else:
                    dve.wait_ge(acc3_step, k - PE3)
                    v.scalar_tensor_tensor(out=acc3[:, :, :], in0=src, scalar=w("w3", k, k + 1), in1=acc3[:, :, :],
                                           op0=ALU.mult, op1=ALU.add).then_inc(acc3_step, 1)
            dve.wait_ge(std1_done, 1)
            v.reciprocal(std[:, :], std[:, :]).then_inc(xn_inv, 1)
            dve.wait_ge(xn_inv, 1)
            v.tensor_tensor(xn[:, :], ps[:, 2, :], std[:, :], ALU.mult).then_inc(xn_done, 1)
            dve.wait_ge(lg_copied, 1)
            v.tensor_reduce(lmax[:, :], lg[:, :, :].rearrange("p q x -> p x q"), AX_X, ALU.max).then_inc(lmax_done, 1)
            dve.wait_ge(lmax_done, 1)
            v.tensor_tensor(lsub[:, :, :], lg[:, :, :], lmax[:, :].unsqueeze(1).broadcast_to([P, NP_, XG]),
                            ALU.subtract).then_inc(lsub_done, 1)
            v.memset(a5[:, :, :, :], 0.0).then_inc(a5_step, 1)
            dve.wait_ge(abs_done, 1)
            v.tensor_scalar(hat[:, 1, :, :, :].rearrange("p c q x -> p (c q x)"), o_abs[:, :], -1.0, 1.0,
                            ALU.mult, ALU.add).then_inc(near_hat, 1)
            dve.wait_ge(prob_done, 1)
            v.tensor_reduce(psum_p[:, :], prob[:, :, :].rearrange("p q x -> p x q"), AX_X,
                            ALU.add).then_inc(psum_done, 1)
            dve.wait_ge(psum_done, 1)
            v.reciprocal(rsum[:, :], psum_p[:, :]).then_inc(rsum_done, 1)
            dve.wait_ge(hats_done, 2)
            dve.wait_ge(near_hat, 1)
            v.tensor_tensor(ym[:, :, :], hat[:, :, 1, :, :].rearrange("p k q x -> p k (q x)"),
                            prob[:, :, :].rearrange("p q x -> p (q x)").unsqueeze(1).broadcast_to([P, K3, NP_ * XG]),
                            ALU.mult).then_inc(ym_done, 1)
            dve.wait_ge(ym_done, 1)
            for jx in range(K3):
                v.tensor_tensor(
                    terms[:, jx, :, :], ym[:, :, :],
                    hat[:, jx, 0, :, :].rearrange("p q x -> p (q x)").unsqueeze(1).broadcast_to([P, K3, NP_ * XG]),
                    ALU.mult).then_inc(terms_done, 1)
            n = 1
            for jx in range(K3):
                dve.wait_ge(terms_done, jx + 1)
                for jy in range(K3):
                    dve.wait_ge(a5_step, n)
                    n += 1
                    part = a5[:, jy:jy + K3, jx:jx + K3, :].rearrange("p y x c -> p x y c")
                    v.tensor_tensor(part, part, terms[:, jx, jy, :].rearrange("p (i j c) -> p i j c", i=K3, j=K3),
                                    ALU.add).then_inc(a5_step, 1)
            dve.wait_ge(a5_step, n)
            dve.wait_ge(v_windowed, 16 * B * XH * K5)
            for dy in range(K5):
                win = v_win[:, dy, :]
                for dx in range(K5):
                    ins = v.tensor_tensor(
                        prod[:, dy, dx, :].rearrange("p (x c) -> p x c", c=GC),
                        win[:, dx * C:(dx + XL) * C].rearrange("p (x c) -> p x c", c=GC),
                        a5[:, dy, dx, :].unsqueeze(2).broadcast_to([P, XG, GC]), ALU.mult)
                ins.then_inc(prod_done, 1)
                if dy == 0:
                    dve.wait_ge(over_total, 1)
                    v.tensor_scalar(far[:, :], ps[0:1, 0, 0:1], 0.0, None, ALU.is_gt).then_inc(far_set, 1)
            dve.wait_ge(samp_read, 1)
            dve.wait_ge(rsum_done, 1)
            v.tensor_tensor(samp[:, :].rearrange("p (x c) -> p x c", c=GC),
                            ps[:, 1, :].rearrange("p (x c) -> p x c", c=GC),
                            rsum[:, :].unsqueeze(2).broadcast_to([P, XG, GC]), ALU.mult).then_inc(samp_done, 1)
            dve.wait_ge(attn0_done, 1)
            dve.wait_ge(u_copied, 1)
            dve.wait_ge(combos_copied, 1)
            v.scalar_tensor_tensor(out=zu[:, :], in0=ps[:, 3, :], scalar=b_oc[:, 0:1], in1=u_dense[:, :],
                                   op0=ALU.add, op1=ALU.mult).then_inc(zu_done, 1)
            dve.wait_ge(t0_done, 1)
            dve.wait_ge(xb_ready, 1)
            v.tensor_tensor(t0[:, :], ps[:, 4, :], xb[:, :], ALU.add).then_inc(t0_copied, 1)
            dve.wait_ge(std2_done, 1)
            v.reciprocal(std2[:, :], std2[:, :]).then_inc(xh_inv, 1)
            dve.wait_ge(xh_inv, 1)
            v.tensor_tensor(xh[:, :], ps[:, 5, :], std2[:, :], ALU.mult).then_inc(xh_done, 1)
            dve.wait_ge(xh_done, 1)
            v.tensor_scalar(q[:, :], xh[:, :], w("wc"), w("wb"), ALU.mult, ALU.add).then_inc(q_done, 1)
            for b in range(B):
                dve.wait_ge(scores_done, b + 1)
                sl = slice(2 * b, 2 * b + 2)
                v.tensor_reduce(smax[:, sl], ps[:, b, :].rearrange("p (t j) -> p t j", t=2), AX_X,
                                ALU.max).then_inc(smax_done, 1)
                dve.wait_ge(smax_done, b + 1)
                dve.wait_ge(acol_copied, 2)
                v.tensor_tensor(stop_[:, sl], smax[:, sl], a_col[:, sl], ALU.add).then_inc(stop_done, 1)
                dve.wait_ge(stop_done, b + 1)
                v.tensor_tensor(nbias[:, sl], a_col[:, sl], stop_[:, sl], ALU.subtract).then_inc(nbias_done, 1)
            for t in range(8):
                dve.wait_ge(exp_done, t + 1)
                v.reciprocal(prinv[:, t:t + 1], prsum[:, t:t + 1]).then_inc(prinv_done, 1)
                dve.wait_ge(prinv_done, t + 1)
                v.tensor_scalar(pr[:, t, :], pr[:, t, :], prinv[:, t:t + 1], None, ALU.mult).then_inc(pnorm_done, 1)
            for b in range(0, B, 2):
                dve.wait_ge(pT_done, b + 1)
                v.tensor_copy(prT[:, b, :], ps[:, 4 + b, :]).then_inc(pT_copied, 1)
            dve.wait_ge(r_done, 1)
            v.scalar_tensor_tensor(out=rx_[:, :], in0=rt[:, :], scalar=1.0, in1=xh[:, :], op0=ALU.add,
                                   op1=ALU.mult).then_inc(mix_step, 1)
            dve.wait_ge(z_done, 1)
            dve.wait_ge(f_done, 1)
            v.scalar_tensor_tensor(out=fz_[:, :], in0=ft[:, :], scalar=1.0, in1=zt[:, :], op0=ALU.add,
                                   op1=ALU.mult).then_inc(mix_step, 1)
            dve.wait_ge(mix_step, 2)
            v.tensor_tensor(gsum[:, :], rx_[:, :], fz_[:, :], ALU.add).then_inc(mix_step, 1)
            dve.wait_ge(mix_step, 3)
            dve.wait_ge(t0_copied, 1)
            v.scalar_tensor_tensor(out=t2[:, :], in0=gsum[:, :], scalar=0.5, in1=t0[:, :], op0=ALU.mult,
                                   op1=ALU.add).then_inc(t2_done, 1)
            dve.wait_ge(std3_done, 1)
            v.reciprocal(std3[:, :], std3[:, :]).then_inc(x2_inv, 1)
            dve.wait_ge(x2_inv, 1)
            v.tensor_tensor(x2[:, :], ps[:, 4, :], std3[:, :], ALU.mult).then_inc(x2_done, 1)

            count = [0]

            def routed(ins):
                count[0] += 1
                ins.then_inc(route_step, 1)
                dve.wait_ge(route_step, count[0])

            def over_e(t):
                return t[:, :].unsqueeze(2).broadcast_to([P, 8, E])

            rank_t = rank[:, :].unsqueeze(1).broadcast_to([P, 8, E])
            dve.wait_ge(route_done, 1)
            dve.wait_ge(consts_set, 1 + E)
            for bh in range(2):
                routed(v.tensor_copy(rl[:, 4 * bh:4 * bh + 4, :],
                                     ps[:, 6 - bh, 4 * bh * E:(4 * bh + 4) * E].rearrange("p (t e) -> p t e", e=E)))
            routed(v.tensor_reduce(rmax[:, :], rl[:, :, :], AX_X, ALU.max))
            routed(v.tensor_tensor(rsub[:, :, :], rl[:, :, :], over_e(rmax), ALU.subtract))
            dve.wait_ge(rexp_done, 1)
            routed(v.tensor_reduce(rs[:, :], rexp[:, :, :], AX_X, ALU.add))
            routed(v.reciprocal(rinv[:, :], rs[:, :]))
            routed(v.tensor_tensor(rp[:, :, :], rexp[:, :, :], over_e(rinv), ALU.mult))
            routed(v.tensor_reduce(m1[:, :], rp[:, :, :], AX_X, ALU.max))
            routed(v.tensor_tensor(e1[:, :, :], rp[:, :, :], over_e(m1), ALU.is_equal))
            routed(v.tensor_tensor(r1[:, :, :], e1[:, :, :], rank_t, ALU.mult))
            routed(v.tensor_reduce(k1[:, :], r1[:, :, :], AX_X, ALU.max))
            routed(v.tensor_tensor(p1[:, :, :], rank_t, over_e(k1), ALU.is_equal))
            routed(v.scalar_tensor_tensor(out=rest[:, :, :], in0=p1[:, :, :], scalar=-2.0, in1=rp[:, :, :],
                                          op0=ALU.mult, op1=ALU.add))
            routed(v.tensor_reduce(m2[:, :], rest[:, :, :], AX_X, ALU.max))
            routed(v.tensor_tensor(e2[:, :, :], rest[:, :, :], over_e(m2), ALU.is_equal))
            routed(v.tensor_tensor(r2[:, :, :], e2[:, :, :], rank_t, ALU.mult))
            routed(v.tensor_reduce(k2[:, :], r2[:, :, :], AX_X, ALU.max))
            routed(v.tensor_tensor(p2[:, :, :], rank_t, over_e(k2), ALU.is_equal))
            routed(v.tensor_tensor(both[:, :, :], p1[:, :, :], p2[:, :, :], ALU.add))
            routed(v.tensor_tensor(csel[:, :, :], both[:, :, :], rp[:, :, :], ALU.mult))
            routed(v.tensor_reduce(tot[:, :], csel[:, :, :], AX_X, ALU.add))
            routed(v.tensor_scalar(tinv[:, :], tot[:, :], 1e-12, None, ALU.max))
            routed(v.reciprocal(tot[:, :], tinv[:, :]))
            v.tensor_tensor(comb[:, :, :], csel[:, :, :], over_e(tot), ALU.mult).then_inc(comb_done, 1)
            for bh in range(2):
                dve.wait_ge(combT_done, bh + 1)
                v.tensor_copy(comb_t[0:E, bh, :], ps[0:E, 2 + bh, :]).then_inc(combT_copied, 1)
            for i in range(2 * EP):
                dve.wait_ge(gelu_done, i + 1)
                dve.wait_ge(spread_done, i + 1)
                if i >= 2:
                    dve.wait_ge(y_done, i - 1)
                v.tensor_tensor(h_cmb[:, i % 2, :], h_act[:, i % 2, :], ps[:, 4 + i % 2, :],
                                ALU.mult).then_inc(hcmb_done, 1)
            dve.wait_ge(y_done, 2 * EP)
            dve.wait_ge(base_done, 1)
            v.tensor_tensor(res[:, :], ps[:, 7, :], base_out[:, :], ALU.add).then_inc(res_done, 1)

        @block.tensor
        def _(pe):
            def mm(out_, lhsT, rhs, start=True, stop=True):
                return nc.tensor.matmul(out_, lhsT, rhs, start=start, stop=stop, skip_group_check=True)

            pe.wait_ge(x_loaded, 16)
            pe.wait_ge(w_loaded[0], 16)
            mm(ps[:, 0, :], w("proj1"), x_in[:, :]).then_inc(proj1_done, 1)
            pe.wait_ge(u_ready, 1)
            pe.wait_ge(diag5_set, 1)
            for k in range(PE5):
                last = mm(psi(1), diag5[:, k, :], u_img(k // 5, k % 5), k == 0, k == PE5 - 1)
            last.then_inc(conv5_done, 1)
            pe.wait_ge(w_loaded[3], 16)
            mm(ps[:, 3, 0:P], w("outproj_t"), w("conv"))
            mm(ps[:, 3, P:P + 1], w("conv"), w("b_outproj"))
            mm(ps[:, 3, 2 * P:3 * P], w("proj2_t"), w("center")).then_inc(combos_done, 1)
            pe.wait_ge(w_loaded[2], 16)
            pe.wait_ge(consts_set, 1)
            mm(ps[:, 0, :].rearrange("p (x c) -> p x c", c=C), ones[:, :],
               wr("b_inproj", 0, 1).unsqueeze(1).broadcast_to([1, XL, C]), True, False)
            for i in range(4):
                mm(om_ps[:, 2 * i:2 * i + 2, 0:OM], ones[:, :],
                   wr("b_offmask", 0, 1).unsqueeze(1).broadcast_to([1, 2, OM]), True, False)
            pe.wait_ge(cen3_set, 1)
            for bl in range(BL):
                pe.wait_ge(h_ready, 2)
                for k in range(PE3):
                    mm(psi(2)[:, bl], cen3[:, k, :], h_img(k // 3, k % 3)[bl], k == 0 and bl == 0, False)
            pe.wait_ge(acc3_step, 9 - PE3)
            mm(psi(2)[:, 0], w("center"), acc3[:, 0:H, :], False, False)
            mm(psi(2)[:, 1], w("center"), acc3[:, H + 1:H + 1 + H, :], False, True).then_inc(d1_done, 1)
            pe.wait_ge(h_copied, 2)
            for xl in range(XL):
                for bh in range(2):
                    p0, p1_ = bh * 64, bh * 64 + 64
                    last = mm(ps[p0:p1_, 0, xl * C:(xl + 1) * C], tokens(h_dense, p0, p1_, xl),
                              wr("inproj", p0, p1_), False, True)
            last.then_inc(v_done, 1)
            pe.wait_ge(sq1_done, 1)
            pe.wait_ge(combos_copied, 1)
            mm(ps[:, 3, :], w("mean"), sq[:, :]).then_inc(var1_done, 1)
            pe.wait_ge(x1_done, 1)
            for xl in range(XL):
                for bh in range(2):
                    p0, p1_ = bh * 64, bh * 64 + 64
                    last = mm(om_ps[p0:p1_, xl, 0:OM], tokens(x1, p0, p1_, xl), wr("offmask", p0, p1_), False, True)
            last.then_inc(off_done, 1)
            pe.wait_ge(over_done, 1)
            pe.wait_ge(v_copied, 1)
            mm(ps[0:1, 0, 0:1], over_sum[:, :], w("one")).then_inc(over_total, 1)
            for dy in range(K5):
                pe.wait_ge(prod_done, dy + 1)
                for dx in range(K5):
                    last = mm(ps[:, 1, :], w("ident"), prod[:, dy, dx, :], dy == 0 and dx == 0,
                              dy == K5 - 1 and dx == K5 - 1)
            last.then_inc(samp_read, 1)
            pe.wait_ge(samp_done, 1)
            pe.wait_ge(slow_done, 1)
            for xl in range(XL):
                for bh in range(2):
                    p0, p1_ = bh * 64, bh * 64 + 64
                    last = mm(ps[p0:p1_, 2, xl * 64:(xl + 1) * 64], samp[p0:p1_, xl * C:(xl + 1) * C],
                              wr("ident", p0, p1_, p0, p1_))
            last.then_inc(sT_done, 1)
            pe.wait_ge(sT_copied, 1)
            mm(ps[:, 3, :], w_oc[:, :], samp_t[:, :]).then_inc(attn0_done, 1)
            pe.wait_ge(xb_ready, 1)
            pe.wait_ge(hats_done, 2)
            mm(ps[:, 5, :], w("center"), xb[:, :], True, False)
            pe.wait_ge(zu_done, 1)
            mm(ps[:, 5, :], w2c[:, :], zu[:, :], False, True)
            mm(ps[:, 4, :], w("proj2"), zu[:, :]).then_inc(t0_done, 1)
            pe.wait_ge(sq2_done, 1)
            mm(ps[:, 6, :], w("mean"), sq2[:, :]).then_inc(var2_done, 1)
            pe.wait_ge(xh_done, 1)
            pe.wait_ge(std2_done, 1)
            for t in range(8):
                b, it = t // 2, t % 2
                bh, bl = b // 2, b % 2
                p0 = bh * 64
                c0 = bl * HW + it * P
                last = mm(ps[:, 6 - bh, t:t + 1], xh[p0:p0 + 64, c0:c0 + P], wr("wa", p0, p0 + 64))
            last.then_inc(acol_done, 1)
            pe.wait_ge(q_done, 1)
            for b in range(B):
                bh, bl = b // 2, b % 2
                p0 = bh * 64
                for it in range(2):
                    c0 = bl * HW + it * P
                    last = mm(ps[:, b, it * HW:(it + 1) * HW], q[p0:p0 + 64, c0:c0 + P],
                              xh[p0:p0 + 64, bl * HW:(bl + 1) * HW])
                last.then_inc(scores_done, 1)
            for t in range(4):
                last = nc.tensor.transpose(ps[:, 7, t * P:(t + 1) * P], xh[:, t * P:(t + 1) * P], w("ident"))
            last.then_inc(xtok_done, 1)
            pe.wait_ge(xtok_copied, 1)
            pe.wait_ge(acol_copied, 2)
            pe.wait_ge(t0_copied, 1)
            for b in range(B):
                pe.wait_ge(pnorm_done, 2 * b + 2)
                for jt in range(2):
                    for it in range(2):
                        c0 = jt * HW + it * P
                        last = nc.tensor.transpose(ps[:, 4 + b, c0:c0 + P], pr[:, 2 * b + it, jt * P:(jt + 1) * P],
                                                   w("ident"))
                last.then_inc(pT_done, 1)
            for i, name in enumerate(("rx", "zx", "fx")):
                mm(ps[:, 1 + i, :], w(name), xh[:, :], True, False)
            pe.wait_ge(pT_copied, B)
            for b in range(B):
                bh, bl = b // 2, b % 2
                p0 = bh * 64
                for jt in range(2):
                    last = mm(ps[p0:p0 + 64, 0, bl * HW:(bl + 1) * HW], xh_tok[:, bl * 2 + jt, p0:p0 + 64],
                              prT[:, b, jt * HW:(jt + 1) * HW], jt == 0, jt == 1)
            last.then_inc(att_done, 1)
            pe.wait_ge(att_copied, 1)
            for i, name in enumerate(("ra", "za", "fa")):
                mm(ps[:, 1 + i, :], w(name), att[:, :], False, True).then_inc(gates_done, 1)
            pe.wait_ge(t2_done, 1)
            mm(ps[:, 4, :], w("center"), t2[:, :]).then_inc(d3_done, 1)
            pe.wait_ge(sq3_done, 1)
            mm(ps[:, 5, :], w("mean"), sq3[:, :]).then_inc(var3_done, 1)
            pe.wait_ge(x2_done, 1)
            pe.wait_ge(w_loaded[4], 16)
            for t in range(8):
                b, it = t // 2, t % 2
                bh, bl = b // 2, b % 2
                p0 = bh * 64
                c0 = bl * HW + it * P
                last = mm(ps[:, 6 - bh, t * E:(t + 1) * E], x2[p0:p0 + 64, c0:c0 + P], wr("router", p0, p0 + 64))
            last.then_inc(route_done, 1)

            def hidden(i):
                ep, bh = i // 2, i % 2
                p0 = bh * 64
                if i >= 2:
                    pe.wait_ge(gelu_done, i - 1)
                mm(ps[:, i % 2, :], wr("w1", p0, p0 + 64, ep * P, (ep + 1) * P), x2[p0:p0 + 64, :]).then_inc(hid_done, 1)

            hidden(0)
            hidden(1)
            pe.wait_ge(comb_done, 1)
            for bh in range(2):
                for t in range(4):
                    last = nc.tensor.transpose(ps[0:E, 2 + bh, t * P:(t + 1) * P], comb[:, bh * 4 + t, :], w("ident"))
                last.then_inc(combT_done, 1)
            pe.wait_ge(combT_copied, 2)
            for bh in range(2):
                mm(ps[bh * 64:bh * 64 + 64, 7, :], wr("b2", 0, E), comb_t[0:E, bh, :], True, False)
            for i in range(2 * EP):
                ep, bh = i // 2, i % 2
                if i >= 2:
                    pe.wait_ge(hcmb_done, i - 1)
                mm(ps[:, 4 + i % 2, :], wr("pick", 0, E, ep * P, (ep + 1) * P), comb_t[0:E, bh, :]).then_inc(spread_done, 1)
                if i + 2 < 2 * EP:
                    hidden(i + 2)
                pe.wait_ge(hcmb_done, i + 1)
                mm(ps[bh * 64:bh * 64 + 64, 7, :], w("w2", ep * C, (ep + 1) * C), h_cmb[:, i % 2, :],
                   False, ep == EP - 1).then_inc(y_done, 1)


def _packed(i):
    import numpy as np

    def both(a):
        return np.concatenate([a, a], 0)

    def diag(a):
        out = np.zeros((P, P), np.float32)
        out[:C, :C] = a
        out[C:, C:] = a
        return out

    def top(a):
        out = np.zeros((P, a.shape[1]), np.float32)
        out[:a.shape[0]] = a
        return out

    g = {k: np.asarray(a) for k, a in i.items()}
    L0, L1, FF = "L0_conv_", "L1_attn_", "L1_ffn_"
    f = {}
    f["proj1"] = diag(g[L0 + "proj1_w"])
    f["w5"] = both(g[L0 + "conv0_w"].reshape(C, 25))
    f["w3"] = both(g[L0 + "dw_w"].reshape(C, 9))
    for name, key in (("b_proj1", "proj1_b"), ("b_conv0", "conv0_b"), ("b_dw", "dw_b"), ("g_ln", "ln_g"),
                      ("b_ln", "ln_b"), ("b_proj2", "proj2_b"), ("b_outproj", "outproj_b"), ("b_conv", "conv_b")):
        f[name] = both(g[L0 + key][:, None])
    f["eps"] = np.full((P, 1), 1e-5, np.float32)
    f["one"] = np.ones((P, 1), np.float32)
    f["minus_one"] = -np.ones((P, 1), np.float32)
    for n, name in enumerate(("wa", "wb", "wc")):
        f[name] = both(g[L1 + "att_w"][n * C:(n + 1) * C, None])
    for gate in "zrf":
        f["b_" + gate] = both(g[L1 + gate + "_b"][:, None])
        f[gate + "x"] = diag(g[L1 + gate + "_w"][:, :C].T)
        f[gate + "a"] = diag(g[L1 + gate + "_w"][:, C:].T)
    f["b1"] = g[FF + "b1"].reshape(EP, P).T
    f["ident"] = np.eye(P, dtype=np.float32)
    f["center"] = diag((np.eye(C) - 1.0 / C).astype(np.float32))
    f["mean"] = diag(np.full((C, C), 1.0 / C, np.float32))
    f["inproj"] = both(g[L0 + "inproj_w"])
    f["b_inproj"] = top(g[L0 + "inproj_b"][None])

    def order(off, mask):
        off = off.reshape(-1, G, NP_, 2).transpose(0, 3, 2, 1).reshape(-1, 2 * NP_ * G)
        mask = mask.reshape(-1, G, NP_).transpose(0, 2, 1).reshape(-1, NP_ * G)
        return np.concatenate([off, mask], 1)

    f["offmask"] = both(order(g[L0 + "off_w"], g[L0 + "mask_w"]))
    f["b_offmask"] = top(order(g[L0 + "off_b"][None], g[L0 + "mask_b"][None]))
    f["outproj_t"] = diag(g[L0 + "outproj_w"].T)
    f["conv"] = diag(g[L0 + "conv_w"])
    f["proj2"] = diag(g[L0 + "proj2_w"])
    f["proj2_t"] = diag(g[L0 + "proj2_w"].T)
    f["w1"] = both(g[FF + "w1"].reshape(EP, 2, C, C).transpose(2, 0, 1, 3).reshape(C, EP * P))
    f["w2"] = g[FF + "w2"].reshape(EP, P, C).transpose(1, 0, 2).reshape(P, EP * C)
    f["router"] = both(g[FF + "router_w"].T)
    f["b2"] = top(g[FF + "b2"])
    pick = np.zeros((P, EP, 2, C), np.float32)
    for e in range(E):
        pick[e, e // 2, e % 2] = 1.0
    f["pick"] = pick.reshape(P, EP * P)
    p = np.arange(P)
    base = np.zeros((P, 2, K3, K3, XL), np.float32)
    base[:, 0] = ((p % XH) * XL)[:, None, None, None] + np.arange(XL) + (np.arange(K3) - 1)[:, None, None]
    base[:, 1] = ((p // XH) % H)[:, None, None, None] + (np.arange(K3) - 1)[None, :, None]
    f["base"] = base.reshape(P, -1)
    f["grid"] = np.tile(np.arange(W, dtype=np.float32), (P, 1))
    cols = [f[name] for name, _ in FIELDS]
    assert [a.shape for a in cols] == [(P, n) for _, n in FIELDS]
    return np.ascontiguousarray(np.concatenate(cols, 1))


def kernel(**inputs):
    import numpy as np
    import concourse.bacc as _bacc
    from concourse.bass_utils import run_bass_kernel_spmd as _run

    x = np.asarray(inputs["x"])
    arrays = {
        "in_x": np.ascontiguousarray(x.reshape(2, BL, C, HW).transpose(0, 2, 1, 3).reshape(P, N)),
        "in_w": _packed({k: a for k, a in inputs.items() if k != "x"}),
    }
    nc = _bacc.Bacc("TRN2", target_bir_lowering=False, num_devices=1)
    A_x = nc.dram_tensor("in_x", (P, N), F32, kind="ExternalInput").ap()
    A_w = nc.dram_tensor("in_w", (P, NCOL), F32, kind="ExternalInput").ap()
    v_dram = nc.dram_tensor("v_padded", (B, VP, VP, C), F32, kind="Internal").ap()
    out = nc.dram_tensor("out_0", (P, N), F32, kind="ExternalOutput").ap()
    conv_attn_moe(nc, A_x, A_w, v_dram, out)
    r = _run(nc, [arrays], core_ids=[0])
    got = r.results[0]["out_0"]
    return np.ascontiguousarray(got.reshape(2, C, BL, H, W).transpose(0, 2, 1, 3, 4).reshape(B, C, H, W))
```

```python
from contextlib import ExitStack

import concourse.bass as bass
from concourse import mybir

ALU = mybir.AluOpType
ACT = mybir.ActivationFunctionType
AX_X = mybir.AxisListType.X
F32 = mybir.dt.float32
BF16 = mybir.dt.bfloat16
I32 = mybir.dt.int32

P = 128
B, C, H, W = 4, 64, 16, 16
BL = 2
BH = B // BL
HW = H * W
N = BL * HW
IT = HW // P
G, GC, K3 = 8, 8, 3
NPT = K3 * K3
XL = 4
XQ = W // XL
XG = XL * G
VW = XL * C
OM = 3 * G * NPT
E = 8
EP = E // 2
K5 = 5
UP, HP = W + 4, W + 2
VP = W + 4
VWX = XL + 4
PE5, PE3 = 12, 4
AR = 3
QB = 4
PARTS = 3

FIELDS = [
    ("proj1", P), ("w5", 25), ("w3", 9), ("b_proj1", 1), ("b_conv0", 1), ("b_dw", 1), ("g_ln", 1), ("b_ln", 1),
    ("eps", 1), ("one", 1), ("minus_one", 1), ("b_proj2", 1), ("b_outproj", 1), ("b_conv", 1), ("wb", 1), ("wc", 1),
    ("b_z", 1), ("b_r", 1), ("b_f", 1), ("b1", EP), ("ident", P), ("wa", BH),
    ("ident2", C), ("center", P), ("mean", P),
    ("inproj", C), ("b_inproj", C), ("offmask", OM), ("b_offmask", OM),
    ("outproj_t", P), ("conv", P), ("proj2", P), ("proj2_t", P),
    ("zx", P), ("za", P), ("rx", P), ("ra", P), ("fx", P), ("fa", P),
    ("w1", EP * BH * P), ("w2", EP * C), ("router", BH * E), ("b2", C), ("pick", EP * P), ("rank", E),
    ("base", 2 * NPT * XL), ("grid", W),
]
COL = {}
_at = 0
for _name, _width in FIELDS:
    COL[_name] = (_at, _width)
    _at += _width
NCOL = _at
CUTS = [0, COL["ident2"][0], COL["inproj"][0], COL["outproj_t"][0], COL["w1"][0], NCOL]


def conv_attn_moe(nc, A_x, A_w, v_dram, out):
    ctx = ExitStack()
    with ctx:
        def sb(name, shape, dt=F32):
            return ctx.enter_context(nc.sbuf_tensor(name, shape, dt))

        def sem(name):
            return ctx.enter_context(nc.semaphore(name))

        wts = sb("wts", [P, NCOL])

        def w(name, a=0, b=None, p0=0, p1=P):
            at, width = COL[name]
            return wts[p0:p1, at + a:at + (width if b is None else b)]

        def half(bh):
            return bh * 64, bh * 64 + 64

        x_in = sb("x_in", [P, BL, HW])
        ones = sb("ones", [1, P])
        cen3 = sb("cen3", [P, PE3, P])
        cenh = sb("cenh", [P, P])
        w_oc = sb("w_oc", [P, P])
        b_oc = sb("b_oc", [P, 1])
        w2c = sb("w2c", [P, P])
        half_rf = sb("half_rf", [P, 2])
        pick_b = sb("pick_b", [PARTS * E, EP * P], BF16)
        ident_b = sb("ident_b", [P, P], BF16)
        b2_parts = sb("b2_parts", [PARTS * E, PARTS, C], BF16)
        b2_rest = sb("b2_rest", [PARTS * E, 2, C])

        upad = sb("upad", [P, BL, UP, UP])
        u_dense = sb("u_dense", [P, BL, HW])
        acc5 = sb("acc5", [P, BL, HW])
        hpad = sb("hpad", [P, BL, HP, HP])
        h_dense = sb("h_dense", [P, BL, HW])
        acc3 = sb("acc3", [P, BL, HW])
        sq = sb("sq", [P, BL, HW])
        lnv = sb("lnv", [P, BL, HW])
        rstd = sb("rstd", [P, BL, HW])
        xn = sb("xn", [P, BL, HW])
        x1 = sb("x1", [P, BL, HW])
        v_tok = sb("v_tok", [P, BL, VW])
        v_win = sb("v_win", [P, BL, K5, VWX * C])
        lg = sb("lg", [P, BL, NPT, XG])
        lmax = sb("lmax", [P, BL, XG])
        lsub = sb("lsub", [P, BL, NPT, XG])
        prob = sb("prob", [P, BL, NPT * XG])
        psum_p = sb("psum_p", [P, BL, XG])
        rsum = sb("rsum", [P, BL, XG])
        hat = sb("hat", [P, BL, K3, 2, NPT * XG])
        o_abs = sb("o_abs", [P, BL, 2 * NPT * XG])
        over_sum = sb("over_sum", [P, BL])
        far = sb("far", [1, BL], I32)
        ym = sb("ym", [P, BL, K3, NPT * XG])
        terms = sb("terms", [P, BL, K3, K3, NPT * XG])
        diag5 = terms[:, :, :, :, :].rearrange("p b x y c -> p (b x y c)")[:, 0:PE5 * P].rearrange(
            "p (k n) -> p k n", k=PE5)
        prod = sb("prod", [P, BL, K5, K5, VW])
        samp = sb("samp", [P, BL, VW])
        samp_t = sb("samp_t", [P, BL, HW])
        zu = sb("zu", [P, BL, HW])
        xb = sb("xb", [P, BL, HW])

        s_pos = sb("s_pos", [P, BL, 2, NPT * XG])
        s_hy = sb("s_hy", [P, NPT * XG])
        s_hx = sb("s_hx", [P, NPT * XG])
        s_min = sb("s_min", [P, NPT * XG])
        s_v = sb("s_v", [P, W * C])
        zeros = s_v[:, 0:B * VP * VP * C // P]
        s_term = sb("s_term", [P, VW])
        s_out = sb("s_out", [P, VW])
        slow_mark = sb("slow_mark", [1, BL])

        taken = {"prod": 0, "terms": 0}

        def late(*shape, place="prod"):
            size = 1
            for n in shape:
                size *= n
            whole = (prod[:, :, :, :, :].rearrange("p b y x c -> p b (y x c)") if place == "prod"
                     else terms[:, :, :, :, :].rearrange("p b x y c -> p b (x y c)"))
            assert taken[place] + size <= whole.shape[2]
            flat = whole[:, :, taken[place]:taken[place] + size]
            taken[place] += size
            return flat if len(shape) == 1 else flat.rearrange("p b (a n) -> p b a n", a=shape[0])

        t0 = late(HW, place="terms")
        xh = late(HW, place="terms")
        q = late(HW, place="terms")
        t0h = late(HW, place="terms")
        base_out = late(HW, place="terms")
        xh_tok = late(IT, P, place="terms")
        t2 = late(HW, place="terms")
        pr = late(BH * IT, HW)
        prT = late(BH, IT * HW)
        norm = late(BH * IT, P)
        att = late(HW)
        zt = late(HW)
        rt = late(HW)
        ft = late(HW)
        rx_ = late(HW)
        fz_ = late(HW)
        gsum = late(HW)
        sq2 = late(HW)
        lnv2 = late(HW)
        rstd2 = late(HW)
        sq3 = late(HW)
        lnv3 = late(HW, place="terms")
        rstd3 = late(HW, place="terms")
        x2 = late(HW, place="terms")
        h_act = prod[:, :, :, :, :].rearrange("p b y x c -> p b (y x c)")[:, :, 0:EP * BH * HW].rearrange(
            "p b (e n) -> p b e n", e=EP)
        h_cmb = late(2, BH * HW)
        res = sb("res", [P, BL, HW])
        smax = sb("smax", [P, BL, IT, BH])
        a_col = sb("a_col", [P, BL, IT, BH])
        a_max = sb("a_max", [P, BL, IT, BH])
        nbias = sb("nbias", [P, BL, IT, BH])
        prsum = sb("prsum", [P, BL, IT, BH])
        prinv = sb("prinv", [P, BL, IT, BH])
        NT = IT * BH
        rmax = sb("rmax", [P, BL, NT])
        rsub = sb("rsub", [P, BL, NT, E])
        rexp = sb("rexp", [P, BL, NT, E])
        rall = sb("rall", [P, BL, NT])
        r1 = sb("r1", [P, BL, NT, E])
        k1 = sb("k1", [P, BL, NT])
        p1 = sb("p1", [P, BL, NT, E])
        rest = sb("rest", [P, BL, NT, E])
        m2 = sb("m2", [P, BL, NT])
        e2 = sb("e2", [P, BL, NT, E])
        r2 = sb("r2", [P, BL, NT, E])
        k2 = sb("k2", [P, BL, NT])
        p2 = sb("p2", [P, BL, NT, E])
        both = sb("both", [P, BL, NT, E])
        csel = sb("csel", [P, BL, NT, E])
        tot = sb("tot", [P, BL, NT])
        guard = sb("guard", [P, BL, NT])
        tinv = sb("tinv", [P, BL, NT])
        comb = sb("comb", [P, BL, NT, E])
        crest = sb("crest", [P, BL, NT, E])
        cparts = sb("cparts", [P, BL, NT, PARTS, E], BF16)
        comb_t = sb("comb_t", [PARTS * E, BL, BH * HW], BF16)

        ps = ctx.enter_context(nc.psum_tensor("ps", [P, BL * QB, 512], F32))

        def bank(bl, i):
            return ps[:, bl * QB + i, :]

        x_loaded = sem("x_loaded")
        pads_zero = sem("pads_zero")
        zeros_set = sem("zeros_set")
        v_cleared = sem("v_cleared")
        ones_set = sem("ones_set")
        diag5_set = sem("diag5_set")
        cen3_set = sem("cen3_set")
        cenh_set = sem("cenh_set")
        half_set = sem("half_set")
        pick_set = sem("pick_set")
        b2_step = sem("b2_step")
        proj1_done = sem("proj1_done")
        u_ready = sem("u_ready")
        u_copied = sem("u_copied")
        xb_ready = sem("xb_ready")
        conv5_done = sem("conv5_done")
        h_ready = sem("h_ready")
        h_copied = sem("h_copied")
        combos_done = sem("combos_done")
        combos_copied = sem("combos_copied")
        d1_done = sem("d1_done")
        v_done = sem("v_done")
        v_copied = sem("v_copied")
        sq1_done = sem("sq1_done")
        var1_done = sem("var1_done")
        ln1_done = sem("ln1_done")
        rstd1_done = sem("rstd1_done")
        xn_done = sem("xn_done")
        x1_done = sem("x1_done")
        off_done = sem("off_done")
        lg_copied = sem("lg_copied")
        abs_done = sem("abs_done")
        hats_done = sem("hats_done")
        near_hat = sem("near_hat")
        lmax_done = sem("lmax_done")
        lsub_done = sem("lsub_done")
        prob_done = sem("prob_done")
        psum_done = sem("psum_done")
        rsum_done = sem("rsum_done")
        ym_done = sem("ym_done")
        terms_done = sem("terms_done")
        over_done = sem("over_done")
        over_total = sem("over_total")
        far_set = sem("far_set")
        a5_done = sem("a5_done")
        prod_done = sem("prod_done")
        sum_done = sem("sum_done")
        samp_done = sem("samp_done")
        slow_done = sem("slow_done")
        sT_done = sem("sT_done")
        sT_copied = sem("sT_copied")
        attn0_done = sem("attn0_done")
        zu_done = sem("zu_done")
        t0_done = sem("t0_done")
        t0_copied = sem("t0_copied")
        t0h_done = sem("t0h_done")
        sq2_done = sem("sq2_done")
        var2_done = sem("var2_done")
        ln2_done = sem("ln2_done")
        rstd2_done = sem("rstd2_done")
        xh_done = sem("xh_done")
        q_done = sem("q_done")
        xtok_done = sem("xtok_done")
        xtok_copied = sem("xtok_copied")
        acol_copied = sem("acol_copied")
        scores_done = sem("scores_done")
        smax_done = sem("smax_done")
        amax_done = sem("amax_done")
        nbias_done = sem("nbias_done")
        exp_done = sem("exp_done")
        prinv_done = sem("prinv_done")
        norm_done = sem("norm_done")
        pT_done = sem("pT_done")
        pT_copied = sem("pT_copied")
        att_done = sem("att_done")
        att_copied = sem("att_copied")
        gates_done = sem("gates_done")
        r_done = sem("r_done")
        z_done = sem("z_done")
        f_done = sem("f_done")
        rx_done = sem("rx_done")
        fz_done = sem("fz_done")
        gsum_done = sem("gsum_done")
        t2_done = sem("t2_done")
        d3_done = sem("d3_done")
        sq3_done = sem("sq3_done")
        var3_done = sem("var3_done")
        ln3_done = sem("ln3_done")
        rstd3_done = sem("rstd3_done")
        x2_done = sem("x2_done")
        base_done = sem("base_done")
        route_done = sem("route_done")
        rsub_done = sem("rsub_done")
        rexp_done = sem("rexp_done")
        comb_done = sem("comb_done")
        combT_done = sem("combT_done")
        combT_copied = sem("combT_copied")
        hid_done = sem("hid_done")
        gelu_done = sem("gelu_done")
        spread_done = sem("spread_done")
        hcmb_done = sem("hcmb_done")
        y_done = sem("y_done")
        res_done = sem("res_done")
        out_stored = sem("out_stored")
        w_loaded = [sem(f"w_loaded{i}") for i in range(len(CUTS) - 1)]
        acc5_step = [sem(f"acc5_step{bl}") for bl in range(BL)]
        acc3_step = [sem(f"acc3_step{bl}") for bl in range(BL)]
        route_step = [sem(f"route_step{bl}") for bl in range(BL)]
        v_stored = [sem(f"v_stored{bl}") for bl in range(BL)]
        v_windowed = [sem(f"v_windowed{bl}") for bl in range(BL)]
        slow_loaded = [sem(f"slow_loaded{bl}") for bl in range(BL)]

        def grid(ap):
            return ap.rearrange("p (y x) -> p y x", y=H)

        def tokens(tile, bl, bh, xl):
            p0, p1_ = half(bh)
            return tile[p0:p1_, bl, xl:HW:XL]

        def om_ps(bl):
            return ps[:, bl * QB + 2:bl * QB + 4, :].rearrange("p b (k c) -> p (b k) c", k=2)

        def off_ps(bl):
            return om_ps(bl)[:, :, 0:2 * NPT * G].rearrange("p x (q g) -> p q x g", g=G)

        def msk_ps(bl):
            return om_ps(bl)[:, :, 2 * NPT * G:OM].rearrange("p x (q g) -> p q x g", g=G)

        def points(ap):
            return ap.rearrange("p (q x g) -> p q x g", x=XL, g=G)

        def a5_rows(bl, first, last):
            i, at = (0, first) if first < AR else (1, first - AR)
            return bank(bl, i)[:, at * K5 * XG:(at + last - first) * K5 * XG].rearrange(
                "p (y x c) -> p y x c", x=K5, c=XG)

        block = ctx.enter_context(nc.Block())

        @block.sync
        def _(sp):
            sp.dma_start(x_in[:, :, :], A_x).then_inc(x_loaded, 16)
            for i in (1, 3):
                sp.dma_start(wts[:, CUTS[i]:CUTS[i + 1]], A_w[:, CUTS[i]:CUTS[i + 1]]).then_inc(w_loaded[i], 16)
            sp.wait_ge(zeros_set, 1)
            sp.dma_start(v_dram.rearrange("b y x c -> (b y x c)").rearrange("(p n) -> p n", p=P),
                         zeros[:, :]).then_inc(v_cleared, 16)
            sp.wait_ge(v_cleared, 16)
            for bl in range(BL):
                sp.wait_ge(v_copied, bl + 1)
                for bh in range(BH):
                    p0, p1_ = half(bh)
                    inside = v_dram[BL * bh + bl, 2:2 + H, 2:2 + W, :].rearrange("y (q x) c -> y q (x c)", q=XQ)
                    sp.dma_start(inside, v_tok[p0:p1_, bl, :]).then_inc(v_stored[bl], 16)
                sp.wait_ge(v_stored[bl], 16 * BH)
                for dy in range(K5):
                    for bh in range(BH):
                        p0, p1_ = half(bh)
                        rows = bass.AP(v_dram.tensor, v_dram[BL * bh + bl, dy].offset,
                                       [[VP * C, H], [VW, XQ], [1, VWX * C]])
                        sp.dma_start(v_win[p0:p1_, bl, dy, :], rows).then_inc(v_windowed[bl], 16)
            for bl in range(BL):
                sp.wait_ge(res_done, bl + 1)
                sp.dma_start(out[:, bl * HW:(bl + 1) * HW], res[:, bl, :]).then_inc(out_stored, 16)
            sp.wait_ge(out_stored, 16 * BL)

        @block.gpsimd
        def _(pool):
            g = nc.gpsimd
            g.memset(upad[:, :, :, :], 0.0).then_inc(pads_zero, 1)
            g.memset(ones[:, :], 1.0).then_inc(ones_set, 1)
            g.memset(hpad[:, :, :, :], 0.0).then_inc(pads_zero, 1)
            g.memset(zeros[:, :], 0.0).then_inc(zeros_set, 1)
            pool.wait_ge(w_loaded[0], 16)
            pool.wait_ge(w_loaded[1], 16)
            g.tensor_tensor(cen3[:, :, :], w("center").unsqueeze(1).broadcast_to([P, PE3, P]),
                            w("w3", 0, PE3).unsqueeze(2).broadcast_to([P, PE3, P]), ALU.mult).then_inc(cen3_set, 1)
            for i, name in enumerate(("b_r", "b_f")):
                g.tensor_scalar(half_rf[:, i:i + 1], w(name), 0.5, None, ALU.mult).then_inc(half_set, 1)
            pool.wait_ge(x_loaded, 16)
            g.tensor_scalar(xb[:, :, :], x_in[:, :, :], w("b_proj2"), None, ALU.add).then_inc(xb_ready, 1)
            g.tensor_scalar(cenh[:, :], w("center"), 0.5, None, ALU.mult).then_inc(cenh_set, 1)
            for bl in range(BL):
                pool.wait_ge(u_ready, bl + 1)
                g.tensor_copy(grid(u_dense[:, bl, :]), upad[:, bl, 2:2 + H, 2:2 + W]).then_inc(u_copied, 1)
            pool.wait_ge(w_loaded[4], 16)
            g.tensor_copy(pick_b[:, :], w("pick", p1=PARTS * E)).then_inc(pick_set, 1)
            g.tensor_copy(ident_b[:, :], w("ident")).then_inc(pick_set, 1)
            left = w("b2", p1=PARTS * E)
            for i in range(PARTS):
                g.tensor_copy(b2_parts[:, i, :], left).then_inc(b2_step, 1)
                if i < PARTS - 1:
                    pool.wait_ge(b2_step, 2 * i + 1)
                    g.tensor_tensor(b2_rest[:, i, :], left, b2_parts[:, i, :], ALU.subtract).then_inc(b2_step, 1)
                    pool.wait_ge(b2_step, 2 * i + 2)
                    left = b2_rest[:, i, :]
            for bl in range(BL):
                pool.wait_ge(far_set, bl + 1)
                is_far = pool.value_load(far[0:1, bl:bl + 1], min_val=0, max_val=1)
                with pool.If(is_far > 0):
                    pool.wait_ge(samp_done, bl + 1)
                    pos = s_pos[:, bl, :, :].rearrange("p c n -> p (c n)")
                    g.tensor_tensor(pos, hat[:, bl, 2, :, :].rearrange("p c n -> p (c n)"),
                                    hat[:, bl, 0, :, :].rearrange("p c n -> p (c n)"), ALU.subtract)
                    g.memset(s_out[:, :], 0.0)
                    pool.drain()
                    base = w("base").rearrange("p (q x) -> p q x", x=XL).unsqueeze(3).broadcast_to([P, 2 * NPT, XL, G])
                    g.tensor_tensor(points(pos), points(pos), base, ALU.add)
                    pool.drain()
                    g0 = COL["grid"][0]

                    def hats(dst, axis, coordinate):
                        at = wts[:, bass.ds(g0 + coordinate, 1)].broadcast_to([P, NPT * XG])
                        g.tensor_tensor(dst, s_pos[:, bl, axis, :], at, ALU.subtract)
                        pool.drain()
                        g.tensor_scalar(s_min[:, :], dst, 0.0, None, ALU.min)
                        pool.drain()
                        g.tensor_scalar(dst, dst, 0.0, None, ALU.max)
                        pool.drain()
                        g.tensor_tensor(dst, s_min[:, :], dst, ALU.subtract)
                        pool.drain()
                        g.tensor_scalar(dst, dst, 1.0, 0.0, ALU.add, ALU.max)
                        pool.drain()

                    with pool.Fori(0, H) as y:
                        for bh in range(BH):
                            p0, p1_ = half(bh)
                            row = v_dram[BL * bh + bl].rearrange("y x c -> y (x c)")[bass.ds(y + 2, 1),
                                                                                      2 * C:(2 + W) * C]
                            pool.dma_start(s_v[p0:p1_, :], row.broadcast_to([64, W * C])).then_inc(slow_loaded[bl], 16)
                        hats(s_hy[:, :], 1, y)
                        pool.wait_ge(slow_loaded[bl], 16 * BH * (y + 1))
                        g.tensor_tensor(s_hy[:, :], s_hy[:, :], prob[:, bl, :], ALU.mult)
                        pool.drain()
                        with pool.Fori(0, W) as x:
                            hats(s_hx[:, :], 0, x)
                            g.tensor_tensor(s_hx[:, :], s_hx[:, :], s_hy[:, :], ALU.mult)
                            pool.drain()
                            for a, b, n in ((0, 4, 4), (0, 2, 2), (0, 1, 1), (0, 8, 1)):
                                into = s_hx[:, a * XG:(a + n) * XG]
                                g.tensor_tensor(into, into, s_hx[:, b * XG:(b + n) * XG], ALU.add)
                                pool.drain()
                            g.tensor_tensor(
                                s_term[:, :].rearrange("p (x g c) -> p x g c", x=XL, g=G),
                                s_hx[:, 0:XG].rearrange("p (x g) -> p x g", g=G).unsqueeze(3)
                                .broadcast_to([P, XL, G, GC]),
                                s_v[:, bass.ds(x * C, C)].rearrange("p (g c) -> p g c", g=G).unsqueeze(1)
                                .broadcast_to([P, XL, G, GC]), ALU.mult)
                            pool.drain()
                            g.tensor_tensor(s_out[:, :], s_out[:, :], s_term[:, :], ALU.add)
                            pool.drain()
                    g.tensor_tensor(samp[:, bl, :].rearrange("p (x c) -> p x c", c=GC),
                                    s_out[:, :].rearrange("p (x c) -> p x c", c=GC),
                                    rsum[:, bl, :].unsqueeze(2).broadcast_to([P, XG, GC]), ALU.mult)
                    pool.drain()
                g.memset(slow_mark[:, bl:bl + 1], 0.0).then_inc(slow_done, 1)
            for bl in range(BL):
                pool.wait_ge(x2_done, bl + 1)
                pool.wait_ge(t2_done, bl + 1)
                g.tensor_tensor(base_out[:, bl, :], t2[:, bl, :], x2[:, bl, :], ALU.add).then_inc(base_done, 1)

        @block.scalar
        def _(act):
            a = nc.scalar
            LN_EXP = "natural_log_exp_and_others"
            act.dma_start(wts[:, CUTS[0]:CUTS[1]], A_w[:, CUTS[0]:CUTS[1]]).then_inc(w_loaded[0], 16)
            for i in (2, 4):
                act.dma_start(wts[:, CUTS[i]:CUTS[i + 1]], A_w[:, CUTS[i]:CUTS[i + 1]]).then_inc(w_loaded[i], 16)
            a.preload_act_table(ACT.Gelu)
            act.wait_ge(w_loaded[0], 16)
            act.wait_ge(pads_zero, 1)
            for bl in range(BL):
                act.wait_ge(proj1_done, bl + 1)
                a.activation(upad[:, bl, 2:2 + H, 2:2 + W], grid(bank(bl, 0)[:, 0:HW]), ACT.Gelu,
                             bias=w("b_proj1")).then_inc(u_ready, 1)
            a.preload_act_table_set(LN_EXP)
            act.wait_ge(combos_done, 1)
            a.activation(w_oc[:, :], bank(0, 3)[:, 0:P], ACT.Copy)
            a.activation(b_oc[:, :], bank(0, 3)[:, P:P + 1], ACT.Identity, bias=w("b_conv"))
            a.activation(w2c[:, :], bank(0, 3)[:, 2 * P:3 * P], ACT.Copy).then_inc(combos_copied, 1)
            for bl in range(BL):
                act.wait_ge(h_ready, bl + 1)
                a.activation(grid(h_dense[:, bl, :]), hpad[:, bl, 1:1 + H, 1:1 + W], ACT.Copy).then_inc(h_copied, 1)

            def square(bl, src, dst, ready, done):
                act.wait_ge(ready, bl + 1)
                a.activation(dst[:, bl, :], src, ACT.Square).then_inc(done, 1)

            def inverse_std(bl, log, dst, ready, between, done):
                act.wait_ge(ready, bl + 1)
                src = {ln1_done: 3, ln2_done: 1, ln3_done: 1}[between]
                a.activation(log[:, bl, :], bank(bl, src)[:, 0:HW], ACT.Ln, bias=w("eps")).then_inc(between, 1)
                act.wait_ge(between, bl + 1)
                a.activation(dst[:, bl, :], log[:, bl, :], ACT.Exp, scale=-0.5).then_inc(done, 1)

            for bl in range(BL):
                square(bl, bank(bl, 2)[:, 0:HW], sq, d1_done, sq1_done)
            for bl in range(BL):
                act.wait_ge(v_done, bl + 1)
                a.activation(v_tok[:, bl, :], bank(bl, 0)[:, 0:VW], ACT.Copy).then_inc(v_copied, 1)
                inverse_std(bl, lnv, rstd, var1_done, ln1_done, rstd1_done)
            a.preload_act_table(ACT.Gelu)
            for bl in range(BL):
                act.wait_ge(xn_done, bl + 1)
                a.activation(x1[:, bl, :], xn[:, bl, :], ACT.Gelu, bias=w("b_ln"),
                             scale=w("g_ln")).then_inc(x1_done, 1)
            a.preload_act_table_set(LN_EXP)
            for bl in range(BL):
                act.wait_ge(off_done, bl + 1)
                a.activation(lg[:, bl, :, :].rearrange("p q (x g) -> p q x g", g=G), msk_ps(bl),
                             ACT.Copy).then_inc(lg_copied, 1)
                a.activation(points(o_abs[:, bl, :]), off_ps(bl), ACT.Abs).then_inc(abs_done, 1)
                hat_x = [points(hat[:, bl, k, :, :].rearrange("p c n -> p (c n)")) for k in range(K3)]
                a.activation(hat_x[2], off_ps(bl), ACT.Relu).then_inc(hats_done, 1)
                act.wait_ge(lsub_done, bl + 1)
                a.activation(prob[:, bl, :], lsub[:, bl, :, :].rearrange("p q x -> p (q x)"),
                             ACT.Exp).then_inc(prob_done, 1)
                a.activation(hat_x[0], off_ps(bl), ACT.Relu, scale=-1.0).then_inc(hats_done, 1)
            for bl in range(BL):
                act.wait_ge(abs_done, bl + 1)
                a.activation(s_pos[:, bl, :, :].rearrange("p c n -> p (c n)"), o_abs[:, bl, :], ACT.Relu,
                             bias=w("minus_one"), accum_out=over_sum[:, bl:bl + 1]).then_inc(over_done, 1)
            for bl in range(BL):
                act.wait_ge(sT_done, bl + 1)
                a.activation(samp_t[:, bl, :].rearrange("p (q x) -> p x q", x=XL),
                             bank(bl, 0)[:, 0:HW].rearrange("p (x q) -> p x q", x=XL), ACT.Copy).then_inc(sT_copied, 1)
            for bl in range(BL):
                square(bl, bank(bl, 3)[:, 0:HW], sq2, t0_done, sq2_done)
            for bl in range(BL):
                inverse_std(bl, lnv2, rstd2, var2_done, ln2_done, rstd2_done)
            for bl in range(BL):
                act.wait_ge(xtok_done, bl + 1)
                both_it = bank(bl, 2).rearrange("p (t c) -> p t c", t=IT)
                a.activation(a_col[:, bl, :, :], both_it[:, :, P:P + BH], ACT.Copy).then_inc(acol_copied, 1)
                a.activation(xh_tok[:, bl, :, :], both_it[:, :, 0:P], ACT.Copy).then_inc(xtok_copied, 1)
            for bl in range(BL):
                act.wait_ge(nbias_done, bl + 1)
                for bh in range(BH):
                    for it in range(IT):
                        a.activation(pr[:, bl, bh * IT + it, :], bank(bl, bh)[:, it * HW:(it + 1) * HW], ACT.Exp,
                                     bias=nbias[:, bl, it, bh:bh + 1],
                                     accum_out=prsum[:, bl, it, bh:bh + 1]).then_inc(exp_done, 1)
            a.preload_act_table(ACT.Tanh)
            for bl in range(BL):
                act.wait_ge(pT_done, 2 * bl + 1)
                a.activation(prT[:, bl, 0, :], bank(bl, 3), ACT.Copy).then_inc(pT_copied, 1)
            for bl in range(BL):
                act.wait_ge(att_done, bl + 1)
                a.activation(att[:, bl, :], bank(bl, 0)[:, 0:HW], ACT.Copy).then_inc(att_copied, 1)
            act.wait_ge(half_set, 2)
            for bl in range(BL):
                act.wait_ge(gates_done, 3 * bl + 1)
                a.activation(rt[:, bl, :], bank(bl, 1)[:, 0:HW], ACT.Tanh, bias=half_rf[:, 0:1],
                             scale=0.5).then_inc(r_done, 1)
                act.wait_ge(gates_done, 3 * bl + 2)
                a.activation(zt[:, bl, :], bank(bl, 2)[:, 0:HW], ACT.Tanh, bias=w("b_z")).then_inc(z_done, 1)
                act.wait_ge(gates_done, 3 * bl + 3)
                a.activation(ft[:, bl, :], bank(bl, 3)[:, 0:HW], ACT.Tanh, bias=half_rf[:, 1:2],
                             scale=0.5).then_inc(f_done, 1)
            a.preload_act_table_set(LN_EXP)
            for bl in range(BL):
                square(bl, bank(bl, 0)[:, 0:HW], sq3, d3_done, sq3_done)
            for bl in range(BL):
                inverse_std(bl, lnv3, rstd3, var3_done, ln3_done, rstd3_done)
            for bl in range(BL):
                act.wait_ge(rsub_done, bl + 1)
                a.activation(rexp[:, bl, :, :], rsub[:, bl, :, :], ACT.Exp).then_inc(rexp_done, 1)
            a.preload_act_table(ACT.Gelu)
            for ep in range(EP):
                for bl in range(BL):
                    act.wait_ge(hid_done, ep * BL + bl + 1)
                    a.activation(h_act[:, bl, ep, :].rearrange("p (b n) -> p b n", b=BH),
                                 ps[:, bl * QB:bl * QB + BH, 0:HW], ACT.Gelu,
                                 bias=w("b1", ep, ep + 1)).then_inc(gelu_done, 1)

        @block.vector
        def _(dve):
            v = nc.vector
            dve.wait_ge(w_loaded[0], 16)
            v.tensor_tensor(diag5[:, :, :], w("ident").unsqueeze(1).broadcast_to([P, PE5, P]),
                            w("w5", 0, PE5).unsqueeze(2).broadcast_to([P, PE5, P]), ALU.mult).then_inc(diag5_set, 1)

            def taps(first, count, side, acc, padded, weights, bias, step, ready):
                for k in range(first, count):
                    for bl in range(BL):
                        src = padded[:, bl, k // side:k // side + H, k % side:k % side + W]
                        to = grid(acc[:, bl, :])
                        if k == first:
                            dve.wait_ge(ready, bl + 1)
                            v.tensor_scalar(to, src, w(weights, k, k + 1), w(bias), ALU.mult,
                                            ALU.add).then_inc(step[bl], 1)
                        else:
                            dve.wait_ge(step[bl], k - first)
                            v.scalar_tensor_tensor(out=to, in0=src, scalar=w(weights, k, k + 1), in1=to,
                                                   op0=ALU.mult, op1=ALU.add).then_inc(step[bl], 1)

            taps(PE5, 25, 5, acc5, upad, "w5", "b_conv0", acc5_step, u_ready)
            dve.wait_ge(pads_zero, 2)
            for bl in range(BL):
                dve.wait_ge(conv5_done, bl + 1)
                dve.wait_ge(acc5_step[bl], 25 - PE5)
                v.tensor_tensor(hpad[:, bl, 1:1 + H, 1:1 + W], grid(bank(bl, 1)[:, 0:HW]), grid(acc5[:, bl, :]),
                                ALU.add).then_inc(h_ready, 1)
            taps(PE3, 9, 3, acc3, hpad, "w3", "b_dw", acc3_step, h_ready)
            for bl in range(BL):
                dve.wait_ge(rstd1_done, bl + 1)
                v.tensor_tensor(xn[:, bl, :], bank(bl, 2)[:, 0:HW], rstd[:, bl, :], ALU.mult).then_inc(xn_done, 1)

            def softmax(bl):
                dve.wait_ge(lg_copied, bl + 1)
                v.tensor_reduce(lmax[:, bl, :], lg[:, bl, :, :].rearrange("p q x -> p x q"), AX_X,
                                ALU.max).then_inc(lmax_done, 1)
                dve.wait_ge(lmax_done, bl + 1)
                v.tensor_tensor(lsub[:, bl, :, :], lg[:, bl, :, :],
                                lmax[:, bl, :].unsqueeze(1).broadcast_to([P, NPT, XG]),
                                ALU.subtract).then_inc(lsub_done, 1)
                dve.wait_ge(abs_done, bl + 1)
                v.tensor_scalar(hat[:, bl, 1, :, :].rearrange("p c n -> p (c n)"), o_abs[:, bl, :], -1.0, 1.0,
                                ALU.mult, ALU.add).then_inc(near_hat, 1)

            def window_terms(bl):
                dve.wait_ge(near_hat, bl + 1)
                dve.wait_ge(hats_done, 2 * bl + 2)
                dve.wait_ge(prob_done, bl + 1)
                v.tensor_tensor(ym[:, bl, :, :], hat[:, bl, :, 1, :],
                                prob[:, bl, :].unsqueeze(1).broadcast_to([P, K3, NPT * XG]),
                                ALU.mult).then_inc(ym_done, 1)
                dve.wait_ge(ym_done, bl + 1)
                for jx in range(K3):
                    v.tensor_tensor(terms[:, bl, jx, :, :], ym[:, bl, :, :],
                                    hat[:, bl, jx, 0, :].unsqueeze(1).broadcast_to([P, K3, NPT * XG]),
                                    ALU.mult).then_inc(terms_done, 1)

            def inverse_sum(bl):
                v.tensor_reduce(psum_p[:, bl, :], prob[:, bl, :].rearrange("p (q x) -> p x q", q=NPT), AX_X,
                                ALU.add).then_inc(psum_done, 1)
                dve.wait_ge(psum_done, bl + 1)
                v.reciprocal(rsum[:, bl, :], psum_p[:, bl, :]).then_inc(rsum_done, 1)

            def products(bl, dy):
                if dy == 0:
                    dve.wait_ge(v_windowed[bl], 16 * BH * K5)
                    dve.wait_ge(a5_done, bl + 1)
                row = v_win[:, bl, dy, 0:VW]
                win = bass.AP(row.tensor, row.offset, [list(row.ap[0]), [C, K5], [GC, XG], [1, GC]])
                v.tensor_tensor(prod[:, bl, dy, :, :].rearrange("p d (x c) -> p d x c", c=GC), win,
                                a5_rows(bl, dy, dy + 1)[:, 0].unsqueeze(3).broadcast_to([P, K5, XG, GC]),
                                ALU.mult).then_inc(prod_done, 1)

            def flags(bl):
                dve.wait_ge(over_total, bl + 1)
                v.tensor_scalar(far[:, bl:bl + 1], bank(bl, 2)[0:1, 0:1], 0.0, None, ALU.is_gt).then_inc(far_set, 1)

            def normalise(bl):
                dve.wait_ge(sum_done, bl + 1)
                dve.wait_ge(rsum_done, bl + 1)
                v.tensor_tensor(samp[:, bl, :].rearrange("p (x c) -> p x c", c=GC),
                                bank(bl, 2)[:, 0:VW].rearrange("p (x c) -> p x c", c=GC),
                                rsum[:, bl, :].unsqueeze(2).broadcast_to([P, XG, GC]), ALU.mult).then_inc(samp_done, 1)

            def gate_u(bl):
                dve.wait_ge(attn0_done, bl + 1)
                dve.wait_ge(u_copied, bl + 1)
                dve.wait_ge(combos_copied, 1)
                v.scalar_tensor_tensor(out=zu[:, bl, :], in0=bank(bl, 2)[:, 0:HW], scalar=b_oc[:, 0:1],
                                       in1=u_dense[:, bl, :], op0=ALU.add, op1=ALU.mult).then_inc(zu_done, 1)

            def copy_t0(bl):
                dve.wait_ge(t0_done, bl + 1)
                dve.wait_ge(xb_ready, 1)
                v.tensor_tensor(t0[:, bl, :], bank(bl, 0)[:, 0:HW], xb[:, bl, :], ALU.add).then_inc(t0_copied, 1)

            for bl in range(BL):
                softmax(bl)
            for bl in range(BL):
                window_terms(bl)
                inverse_sum(bl)
                if bl == 0:
                    flags(0)
            flags(1)
            for bl in range(BL):
                for dy in range(K5):
                    products(bl, dy)
            for bl in range(BL):
                normalise(bl)
            for bl in range(BL):
                gate_u(bl)
            for bl in range(BL):
                copy_t0(bl)
            for bl in range(BL):
                dve.wait_ge(rstd2_done, bl + 1)
                v.tensor_tensor(xh[:, bl, :], bank(bl, 3)[:, 0:HW], rstd2[:, bl, :], ALU.mult).then_inc(xh_done, 1)
                dve.wait_ge(xh_done, bl + 1)
                v.tensor_scalar(q[:, bl, :], xh[:, bl, :], w("wc"), w("wb"), ALU.mult, ALU.add).then_inc(q_done, 1)
            for bl in range(BL):
                dve.wait_ge(scores_done, bl + 1)
                for bh in range(BH):
                    v.tensor_reduce(smax[:, bl, :, bh], bank(bl, bh).rearrange("p (t j) -> p t j", t=IT), AX_X,
                                    ALU.max).then_inc(smax_done, 1)
                dve.wait_ge(smax_done, BH * (bl + 1))
                dve.wait_ge(acol_copied, bl + 1)
                v.tensor_tensor(a_max[:, bl, :, :], smax[:, bl, :, :], a_col[:, bl, :, :],
                                ALU.add).then_inc(amax_done, 1)
                dve.wait_ge(amax_done, bl + 1)
                v.tensor_tensor(nbias[:, bl, :, :], a_col[:, bl, :, :], a_max[:, bl, :, :],
                                ALU.subtract).then_inc(nbias_done, 1)
            for bl in range(BL):
                dve.wait_ge(t0_copied, bl + 1)
                v.scalar_tensor_tensor(out=t0h[:, bl, :], in0=xh[:, bl, :], scalar=0.5, in1=t0[:, bl, :], op0=ALU.mult,
                                       op1=ALU.add).then_inc(t0h_done, 1)
            for bl in range(BL):
                for bh in range(BH):
                    dve.wait_ge(exp_done, BH * IT * bl + IT * (bh + 1))
                    v.reciprocal(prinv[:, bl, :, bh], prsum[:, bl, :, bh]).then_inc(prinv_done, 1)
                    dve.wait_ge(prinv_done, BH * bl + bh + 1)
                    for it in range(IT):
                        v.tensor_scalar(norm[:, bl, bh * IT + it, :], w("ident"), prinv[:, bl, it, bh:bh + 1], None,
                                        ALU.mult).then_inc(norm_done, 1)
            for bl in range(BL):
                dve.wait_ge(pT_done, 2 * bl + 2)
                v.tensor_copy(prT[:, bl, 1, :], bank(bl, 2)).then_inc(pT_copied, 1)
            for bl in range(BL):
                dve.wait_ge(r_done, bl + 1)
                v.scalar_tensor_tensor(out=rx_[:, bl, :], in0=rt[:, bl, :], scalar=0.5, in1=xh[:, bl, :], op0=ALU.mult,
                                       op1=ALU.mult).then_inc(rx_done, 1)
                dve.wait_ge(rx_done, bl + 1)
                dve.wait_ge(t0h_done, bl + 1)
                v.tensor_tensor(gsum[:, bl, :], rx_[:, bl, :], t0h[:, bl, :], ALU.add).then_inc(gsum_done, 1)
                dve.wait_ge(z_done, bl + 1)
                dve.wait_ge(f_done, bl + 1)
                v.scalar_tensor_tensor(out=fz_[:, bl, :], in0=ft[:, bl, :], scalar=1.0, in1=zt[:, bl, :], op0=ALU.add,
                                       op1=ALU.mult).then_inc(fz_done, 1)
                dve.wait_ge(fz_done, bl + 1)
                dve.wait_ge(gsum_done, bl + 1)
                v.scalar_tensor_tensor(out=t2[:, bl, :], in0=fz_[:, bl, :], scalar=0.5, in1=gsum[:, bl, :],
                                       op0=ALU.mult, op1=ALU.add).then_inc(t2_done, 1)
            for bl in range(BL):
                dve.wait_ge(rstd3_done, bl + 1)
                v.tensor_tensor(x2[:, bl, :], bank(bl, 0)[:, 0:HW], rstd3[:, bl, :], ALU.mult).then_inc(x2_done, 1)

            def routed(build, *outside):
                for bl in range(BL):
                    for signal in outside:
                        dve.wait_ge(signal, bl + 1)
                    if steps[0]:
                        dve.wait_ge(route_step[bl], steps[0])
                    build(bl).then_inc(route_step[bl], 1)
                steps[0] += 1

            def over_e(t, bl):
                return t[:, bl, :].unsqueeze(2).broadcast_to([P, NT, E])

            def logits(bl):
                return bank(bl, 2)[:, 0:NT * E].rearrange("p (t e) -> p t e", e=E)

            steps = [0]
            rank = w("rank").unsqueeze(1).broadcast_to([P, NT, E])
            routed(lambda b: v.tensor_reduce(rmax[:, b, :], logits(b), AX_X, ALU.max), route_done)
            for bl in range(BL):
                dve.wait_ge(route_step[bl], 1)
                v.tensor_tensor(rsub[:, bl, :, :], logits(bl), over_e(rmax, bl), ALU.subtract).then_inc(rsub_done, 1)
            routed(lambda b: v.scalar_tensor_tensor(out=r1[:, b, :, :], in0=rsub[:, b, :, :], scalar=0.0, in1=rank,
                                                    op0=ALU.is_equal, op1=ALU.mult), rsub_done)
            routed(lambda b: v.tensor_reduce(k1[:, b, :], r1[:, b, :, :], AX_X, ALU.max))
            routed(lambda b: v.tensor_tensor(p1[:, b, :, :], rank, over_e(k1, b), ALU.is_equal))
            routed(lambda b: v.scalar_tensor_tensor(out=rest[:, b, :, :], in0=p1[:, b, :, :], scalar=-1e30,
                                                    in1=rsub[:, b, :, :], op0=ALU.mult, op1=ALU.add))
            routed(lambda b: v.tensor_reduce(m2[:, b, :], rest[:, b, :, :], AX_X, ALU.max))
            routed(lambda b: v.tensor_tensor(e2[:, b, :, :], rest[:, b, :, :], over_e(m2, b), ALU.is_equal))
            routed(lambda b: v.tensor_tensor(r2[:, b, :, :], e2[:, b, :, :], rank, ALU.mult))
            routed(lambda b: v.tensor_reduce(k2[:, b, :], r2[:, b, :, :], AX_X, ALU.max))
            routed(lambda b: v.tensor_tensor(p2[:, b, :, :], rank, over_e(k2, b), ALU.is_equal))
            routed(lambda b: v.tensor_tensor(both[:, b, :, :], p1[:, b, :, :], p2[:, b, :, :], ALU.add))
            routed(lambda b: v.tensor_tensor(csel[:, b, :, :], both[:, b, :, :], rexp[:, b, :, :], ALU.mult),
                   rexp_done)
            routed(lambda b: v.tensor_reduce(rall[:, b, :], rexp[:, b, :, :], AX_X, ALU.add))
            routed(lambda b: v.tensor_reduce(tot[:, b, :], csel[:, b, :, :], AX_X, ALU.add))
            routed(lambda b: v.scalar_tensor_tensor(out=guard[:, b, :], in0=rall[:, b, :], scalar=1e-12,
                                                    in1=tot[:, b, :], op0=ALU.mult, op1=ALU.max))
            routed(lambda b: v.reciprocal(tinv[:, b, :], guard[:, b, :]))
            routed(lambda b: v.tensor_tensor(comb[:, b, :, :], csel[:, b, :, :], over_e(tinv, b), ALU.mult))
            routed(lambda b: v.tensor_copy(cparts[:, b, :, 0, :], comb[:, b, :, :]))
            routed(lambda b: v.tensor_tensor(crest[:, b, :, :], comb[:, b, :, :], cparts[:, b, :, 0, :],
                                             ALU.subtract))
            routed(lambda b: v.tensor_copy(cparts[:, b, :, 1, :], crest[:, b, :, :]))
            for bl in range(BL):
                dve.wait_ge(route_step[bl], steps[0])
                v.tensor_tensor(cparts[:, bl, :, 2, :], crest[:, bl, :, :], cparts[:, bl, :, 1, :],
                                ALU.subtract).then_inc(comb_done, 1)
            for bl in range(BL):
                dve.wait_ge(combT_done, bl + 1)
                v.tensor_copy(comb_t[:, bl, :],
                              bank(bl, 2).bitcast(BF16)[0:PARTS * E, 0:BH * HW]).then_inc(combT_copied, 1)
            for ep in range(EP):
                for bl in range(BL):
                    n = ep * BL + bl
                    dve.wait_ge(gelu_done, n + 1)
                    dve.wait_ge(spread_done, n + 1)
                    if ep >= 2:
                        dve.wait_ge(y_done, n - 2 * BL + 1)
                    v.tensor_tensor(h_cmb[:, bl, ep % 2, :], h_act[:, bl, ep, :], bank(bl, 2),
                                    ALU.mult).then_inc(hcmb_done, 1)
            for bl in range(BL):
                dve.wait_ge(y_done, (EP - 1) * BL + bl + 1)
                dve.wait_ge(base_done, bl + 1)
                v.tensor_tensor(res[:, bl, :], bank(bl, 3)[:, 0:HW], base_out[:, bl, :], ALU.add).then_inc(res_done, 1)

        @block.tensor
        def _(pe):
            def mm(out_, lhsT, rhs, start=True, stop=True):
                return nc.tensor.matmul(out_, lhsT, rhs, start=start, stop=stop, skip_group_check=True)

            pe.wait_ge(x_loaded, 16)
            pe.wait_ge(w_loaded[0], 16)
            for bl in range(BL):
                mm(bank(bl, 0)[:, 0:HW], w("proj1"), x_in[:, bl, :]).then_inc(proj1_done, 1)
            pe.wait_ge(w_loaded[1], 16)
            pe.wait_ge(w_loaded[3], 16)
            mm(bank(0, 3)[:, 0:P], w("outproj_t"), w("conv"))
            mm(bank(0, 3)[:, P:P + 1], w("conv"), w("b_outproj"))
            mm(bank(0, 3)[:, 2 * P:3 * P], w("proj2_t"), w("center")).then_inc(combos_done, 1)
            pe.wait_ge(diag5_set, 1)
            for bl in range(BL):
                pe.wait_ge(u_ready, bl + 1)
                for k in range(PE5):
                    last = mm(grid(bank(bl, 1)[:, 0:HW]), diag5[:, k, :],
                              upad[:, bl, k // 5:k // 5 + H, k % 5:k % 5 + W], k == 0, k == PE5 - 1)
                last.then_inc(conv5_done, 1)
            pe.wait_ge(cen3_set, 1)
            for bl in range(BL):
                pe.wait_ge(h_ready, bl + 1)
                for k in range(PE3):
                    mm(grid(bank(bl, 2)[:, 0:HW]), cen3[:, k, :],
                       hpad[:, bl, k // 3:k // 3 + H, k % 3:k % 3 + W], k == 0, False)
            for bl in range(BL):
                pe.wait_ge(acc3_step[bl], 9 - PE3)
                mm(bank(bl, 2)[:, 0:HW], w("center"), acc3[:, bl, :], False, True).then_inc(d1_done, 1)
            pe.wait_ge(w_loaded[2], 16)
            pe.wait_ge(ones_set, 1)
            for bl in range(BL):
                pe.wait_ge(h_copied, bl + 1)
                mm(bank(bl, 0)[:, 0:VW].rearrange("p (x c) -> p x c", c=C), ones[:, :],
                   w("b_inproj", p1=1).unsqueeze(1).broadcast_to([1, XL, C]), True, False)
                for xl in range(XL):
                    for bh in range(BH):
                        p0, p1_ = half(bh)
                        last = mm(bank(bl, 0)[p0:p1_, xl * C:(xl + 1) * C], tokens(h_dense, bl, bh, xl),
                                  w("inproj", p0=p0, p1=p1_), False, True)
                last.then_inc(v_done, 1)
                pe.wait_ge(sq1_done, bl + 1)
                pe.wait_ge(combos_copied, 1)
                mm(bank(bl, 3)[:, 0:HW], w("mean"), sq[:, bl, :]).then_inc(var1_done, 1)
            for bl in range(BL):
                pe.wait_ge(xn_done, bl + 1)
                for i in range(2):
                    mm(om_ps(bl)[:, 2 * i:2 * i + 2, 0:OM], ones[:, :],
                       w("b_offmask", p1=1).unsqueeze(1).broadcast_to([1, 2, OM]), True, False)
            for bl in range(BL):
                pe.wait_ge(x1_done, bl + 1)
                for xl in range(XL):
                    for bh in range(BH):
                        p0, p1_ = half(bh)
                        last = mm(om_ps(bl)[p0:p1_, xl, 0:OM], tokens(x1, bl, bh, xl), w("offmask", p0=p0, p1=p1_),
                                  False, True)
                last.then_inc(off_done, 1)

            def window_weights(bl):
                pe.wait_ge(v_copied, bl + 1)
                for jx in range(K3):
                    pe.wait_ge(terms_done, K3 * bl + jx + 1)
                    for jy in range(K3):
                        term = terms[:, bl, jx, jy, :].rearrange("p (i j c) -> p j i c", i=K3, j=K3)
                        cut = AR - jy
                        last = mm(a5_rows(bl, jy, AR)[:, :, jx:jx + K3, :], w("ident"), term[:, 0:cut],
                                  jx == 0 and jy == 0, jx == K3 - 1 and jy == K3 - 1)
                        if jy:
                            last = mm(a5_rows(bl, AR, AR + jy)[:, :, jx:jx + K3, :], w("ident"), term[:, cut:K3],
                                      jx == 0 and jy == 1, jx == K3 - 1 and jy == K3 - 1)
                last.then_inc(a5_done, 1)

            def flags(bl):
                pe.wait_ge(over_done, bl + 1)
                pe.wait_ge(hats_done, 2 * bl + 2)
                mm(bank(bl, 2)[0:1, 0:1], over_sum[:, bl:bl + 1], w("one")).then_inc(over_total, 1)

            def window_sum(bl, dy):
                if dy == 0:
                    pe.wait_ge(far_set, bl + 1)
                pe.wait_ge(prod_done, K5 * bl + dy + 1)
                for dx in range(K5):
                    last = mm(bank(bl, 2)[:, 0:VW], w("ident"), prod[:, bl, dy, dx, :],
                              dy == 0 and dx == 0, dy == K5 - 1 and dx == K5 - 1)
                if dy == K5 - 1:
                    last.then_inc(sum_done, 1)

            def to_channels(bl):
                pe.wait_ge(samp_done, bl + 1)
                pe.wait_ge(slow_done, bl + 1)
                for xl in range(XL):
                    for bh in range(BH):
                        p0, p1_ = half(bh)
                        last = mm(bank(bl, 0)[p0:p1_, xl * 64:xl * 64 + 64], samp[p0:p1_, bl, xl * C:(xl + 1) * C],
                                  w("ident2", p0=p0, p1=p1_))
                last.then_inc(sT_done, 1)

            def project(bl):
                pe.wait_ge(sT_copied, bl + 1)
                mm(bank(bl, 2)[:, 0:HW], w_oc[:, :], samp_t[:, bl, :]).then_inc(attn0_done, 1)
                pe.wait_ge(xb_ready, 1)
                mm(bank(bl, 3)[:, 0:HW], w("center"), xb[:, bl, :], True, False)

            def close_l0(bl):
                pe.wait_ge(zu_done, bl + 1)
                mm(bank(bl, 3)[:, 0:HW], w2c[:, :], zu[:, bl, :], False, True)
                mm(bank(bl, 0)[:, 0:HW], w("proj2"), zu[:, bl, :]).then_inc(t0_done, 1)

            def variance(bl, tile, ready, done):
                pe.wait_ge(ready, bl + 1)
                mm(bank(bl, 1)[:, 0:HW], w("mean"), tile[:, bl, :]).then_inc(done, 1)

            for bl in range(BL):
                window_weights(bl)
                if bl == 0:
                    flags(0)
            flags(1)
            for bl in range(BL):
                for dy in range(K5):
                    window_sum(bl, dy)
            for bl in range(BL):
                to_channels(bl)
            for bl in range(BL):
                project(bl)
            for bl in range(BL):
                close_l0(bl)
            for bl in range(BL):
                variance(bl, sq2, sq2_done, var2_done)
            for bl in range(BL):
                pe.wait_ge(q_done, bl + 1)
                pe.wait_ge(t0_copied, bl + 1)
                for it in range(IT):
                    for m in range(2):
                        for bh in range(BH):
                            p0, p1_ = half(bh)
                            o0, o1 = half(m)
                            c0 = it * P + m * 64
                            last = mm(bank(bl, bh)[o0:o1, it * HW:(it + 1) * HW], q[p0:p1_, bl, c0:c0 + 64],
                                      xh[p0:p1_, bl, :])
                last.then_inc(scores_done, 1)
                at = COL["ident"][0]
                for it in range(IT):
                    last = mm(bank(bl, 2)[:, it * HW:it * HW + P + BH], xh[:, bl, it * P:(it + 1) * P],
                              wts[:, at:at + P + BH])
                last.then_inc(xtok_done, 1)
            for bl in range(BL):
                for bh in range(BH):
                    pe.wait_ge(norm_done, BH * IT * bl + IT * (bh + 1))
                    if bh:
                        pe.wait_ge(xtok_copied, bl + 1)
                    for it in range(IT):
                        for jt in range(IT):
                            c0 = jt * HW + it * P
                            last = mm(bank(bl, 3 - bh)[:, c0:c0 + P], pr[:, bl, bh * IT + it, jt * P:(jt + 1) * P],
                                      norm[:, bl, bh * IT + it, :])
                    last.then_inc(pT_done, 1)
            for bl in range(BL):
                pe.wait_ge(exp_done, BH * IT * (bl + 1))
                mm(bank(bl, 1)[:, 0:HW], w("rx"), xh[:, bl, :], True, False)
            for bl in range(BL):
                pe.wait_ge(pT_copied, 2 * BL)
                for jt in range(IT):
                    for bh in range(BH):
                        p0, p1_ = half(bh)
                        last = mm(bank(bl, 0)[p0:p1_, 0:HW], xh_tok[:, bl, jt, p0:p1_],
                                  prT[:, bl, bh, jt * HW:(jt + 1) * HW], jt == 0, jt == IT - 1)
                last.then_inc(att_done, 1)
            for bl in range(BL):
                mm(bank(bl, 2)[:, 0:HW], w("zx"), xh[:, bl, :], True, False)
                mm(bank(bl, 3)[:, 0:HW], w("fx"), xh[:, bl, :], True, False)
            for bl in range(BL):
                pe.wait_ge(att_copied, bl + 1)
                for i, name in enumerate(("ra", "za", "fa")):
                    mm(bank(bl, 1 + i)[:, 0:HW], w(name), att[:, bl, :], False, True).then_inc(gates_done, 1)
            pe.wait_ge(cenh_set, 1)
            for bl in range(BL):
                pe.wait_ge(gsum_done, bl + 1)
                mm(bank(bl, 0)[:, 0:HW], w("center"), gsum[:, bl, :], True, False)
                pe.wait_ge(fz_done, bl + 1)
                mm(bank(bl, 0)[:, 0:HW], cenh[:, :], fz_[:, bl, :], False, True).then_inc(d3_done, 1)
            for bl in range(BL):
                variance(bl, sq3, sq3_done, var3_done)
            for bl in range(BL):
                pe.wait_ge(x2_done, bl + 1)
                for it in range(IT):
                    last = mm(bank(bl, 2)[:, it * BH * E:(it + 1) * BH * E], x2[:, bl, it * P:(it + 1) * P], w("router"))
                last.then_inc(route_done, 1)
            for ep in range(EP):
                for bl in range(BL):
                    if ep:
                        pe.wait_ge(gelu_done, (ep - 1) * BL + bl + 1)
                    for bh in range(BH):
                        at = (ep * BH + bh) * P
                        last = mm(bank(bl, bh)[:, 0:HW], w("w1", at, at + P), x2[:, bl, :])
                    last.then_inc(hid_done, 1)
            pe.wait_ge(pick_set, 2)
            pe.wait_ge(b2_step, 2 * PARTS - 1)
            for bl in range(BL):
                pe.wait_ge(comb_done, bl + 1)
                turned = bank(bl, 2).bitcast(BF16)
                for bh in range(BH):
                    for it in range(IT):
                        c0 = bh * HW + it * P
                        last = nc.tensor.transpose(
                            turned[0:PARTS * E, c0:c0 + P],
                            cparts[:, bl, it * BH + bh, :, :].rearrange("p a e -> p (a e)"), ident_b[:, :])
                last.then_inc(combT_done, 1)
            for bl in range(BL):
                pe.wait_ge(combT_copied, bl + 1)
                for i in range(PARTS):
                    for bh in range(BH):
                        p0, p1_ = half(bh)
                        mm(bank(bl, 3)[p0:p1_, 0:HW], b2_parts[:, i, :], comb_t[:, bl, bh * HW:(bh + 1) * HW],
                           i == 0, False)

            def spread(ep, bl):
                if ep:
                    pe.wait_ge(hcmb_done, (ep - 1) * BL + bl + 1)
                mm(bank(bl, 2), pick_b[:, ep * P:(ep + 1) * P], comb_t[:, bl, :]).then_inc(spread_done, 1)

            for bl in range(BL):
                spread(0, bl)
            for ep in range(EP):
                for bl in range(BL):
                    pe.wait_ge(hcmb_done, ep * BL + bl + 1)
                    if ep + 1 < EP:
                        spread(ep + 1, bl)
                    for bh in range(BH):
                        p0, p1_ = half(bh)
                        last = mm(bank(bl, 3)[p0:p1_, 0:HW], w("w2", ep * C, (ep + 1) * C),
                                  h_cmb[:, bl, ep % 2, bh * HW:(bh + 1) * HW], False, ep == EP - 1)
                    last.then_inc(y_done, 1)


def _packed(i):
    import numpy as np

    def both(a):
        return np.concatenate([a, a], 0)

    def diag(a):
        out = np.zeros((P, P), np.float32)
        out[:C, :C] = a
        out[C:, C:] = a
        return out

    def sides(a):
        out = np.zeros((2, C, 2, a.shape[1]), np.float32)
        out[0, :, 0] = a
        out[1, :, 1] = a
        return out.reshape(P, -1)

    def top(a):
        out = np.zeros((P, a.shape[1]), np.float32)
        out[:a.shape[0]] = a
        return out

    g = {k: np.asarray(a) for k, a in i.items()}
    L0, L1, FF = "L0_conv_", "L1_attn_", "L1_ffn_"
    f = {}
    f["proj1"] = diag(g[L0 + "proj1_w"])
    f["w5"] = both(g[L0 + "conv0_w"].reshape(C, 25))
    f["w3"] = both(g[L0 + "dw_w"].reshape(C, 9))
    for name, key in (("b_proj1", "proj1_b"), ("b_conv0", "conv0_b"), ("b_dw", "dw_b"), ("g_ln", "ln_g"),
                      ("b_ln", "ln_b"), ("b_proj2", "proj2_b"), ("b_outproj", "outproj_b"), ("b_conv", "conv_b")):
        f[name] = both(g[L0 + key][:, None])
    f["eps"] = np.full((P, 1), 1e-5, np.float32)
    f["one"] = np.ones((P, 1), np.float32)
    f["minus_one"] = -np.ones((P, 1), np.float32)
    for n, name in ((1, "wb"), (2, "wc")):
        f[name] = both(g[L1 + "att_w"][n * C:(n + 1) * C, None])
    f["wa"] = sides(g[L1 + "att_w"][:C, None])
    for gate in "zrf":
        f["b_" + gate] = both(g[L1 + gate + "_b"][:, None])
        f[gate + "x"] = diag(g[L1 + gate + "_w"][:, :C].T)
        f[gate + "a"] = diag(g[L1 + gate + "_w"][:, C:].T)
    f["b1"] = g[FF + "b1"].reshape(EP, P).T
    f["ident"] = np.eye(P, dtype=np.float32)
    f["ident2"] = both(np.eye(C, dtype=np.float32))
    f["center"] = diag((np.eye(C) - 1.0 / C).astype(np.float32))
    f["mean"] = diag(np.full((C, C), 1.0 / C, np.float32))
    f["inproj"] = both(g[L0 + "inproj_w"])
    f["b_inproj"] = top(g[L0 + "inproj_b"][None])

    def order(off, mask):
        off = off.reshape(-1, G, NPT, 2).transpose(0, 3, 2, 1).reshape(-1, 2 * NPT * G)
        mask = mask.reshape(-1, G, NPT).transpose(0, 2, 1).reshape(-1, NPT * G)
        return np.concatenate([off, mask], 1)

    f["offmask"] = both(order(g[L0 + "off_w"], g[L0 + "mask_w"]))
    f["b_offmask"] = top(order(g[L0 + "off_b"][None], g[L0 + "mask_b"][None]))
    f["outproj_t"] = diag(g[L0 + "outproj_w"].T)
    f["conv"] = diag(g[L0 + "conv_w"])
    f["proj2"] = diag(g[L0 + "proj2_w"])
    f["proj2_t"] = diag(g[L0 + "proj2_w"].T)
    w1 = np.zeros((BH, C, EP, BH, 2, C), np.float32)
    for bh in range(BH):
        w1[bh, :, :, bh] = g[FF + "w1"].reshape(EP, 2, C, C).transpose(2, 0, 1, 3)
    f["w1"] = w1.reshape(P, -1)
    f["w2"] = g[FF + "w2"].reshape(EP, P, C).transpose(1, 0, 2).reshape(P, EP * C)
    f["router"] = sides(g[FF + "router_w"].T)
    f["b2"] = top(np.tile(g[FF + "b2"], (PARTS, 1)))
    pick = np.zeros((P, EP, 2, C), np.float32)
    for e in range(E):
        pick[e:PARTS * E:E, e // 2, e % 2] = 1.0
    f["pick"] = pick.reshape(P, EP * P)
    p = np.arange(P)
    base = np.zeros((P, 2, K3, K3, XL), np.float32)
    base[:, 0] = ((p % XQ) * XL)[:, None, None, None] + np.arange(XL) + (np.arange(K3) - 1)[:, None, None]
    base[:, 1] = ((p // XQ) % H)[:, None, None, None] + (np.arange(K3) - 1)[None, :, None]
    f["rank"] = np.tile(E - np.arange(E, dtype=np.float32), (P, 1))
    f["base"] = base.reshape(P, -1)
    f["grid"] = np.tile(np.arange(W, dtype=np.float32), (P, 1))
    cols = [f[name] for name, _ in FIELDS]
    assert [a.shape for a in cols] == [(P, n) for _, n in FIELDS]
    return np.ascontiguousarray(np.concatenate(cols, 1))


def kernel(**inputs):
    import numpy as np
    import concourse.bacc as _bacc
    from concourse.bass_utils import run_bass_kernel_spmd as _run

    x = np.asarray(inputs["x"])
    arrays = {
        "in_x": np.ascontiguousarray(x.reshape(BH, BL, C, HW).transpose(0, 2, 1, 3).reshape(P, N)),
        "in_w": _packed({k: a for k, a in inputs.items() if k != "x"}),
    }
    nc = _bacc.Bacc("TRN2", target_bir_lowering=False, num_devices=1)
    A_x = nc.dram_tensor("in_x", (P, N), F32, kind="ExternalInput").ap()
    A_w = nc.dram_tensor("in_w", (P, NCOL), F32, kind="ExternalInput").ap()
    v_dram = nc.dram_tensor("v_padded", (B, VP, VP, C), F32, kind="Internal").ap()
    out = nc.dram_tensor("out_0", (P, N), F32, kind="ExternalOutput").ap()
    conv_attn_moe(nc, A_x, A_w, v_dram, out)
    r = _run(nc, [arrays], core_ids=[0])
    got = r.results[0]["out_0"]
    return np.ascontiguousarray(got.reshape(2, C, BL, H, W).transpose(0, 2, 1, 3, 4).reshape(B, C, H, W))
```

```python
from contextlib import ExitStack

import concourse.bass as bass
from concourse import mybir

ALU = mybir.AluOpType
ACT = mybir.ActivationFunctionType
AX_X = mybir.AxisListType.X
F32 = mybir.dt.float32
BF16 = mybir.dt.bfloat16
I32 = mybir.dt.int32

P = 128
B, C, H, W = 4, 64, 16, 16
BL = 2
BH = B // BL
HW = H * W
N = BL * HW
IT = HW // P
G, GC, K3 = 8, 8, 3
NPT = K3 * K3
XL = 4
XQ = W // XL
XG = XL * G
VW = XL * C
OM = 3 * G * NPT
E = 8
EP = E // 2
K5 = 5
UP, HP = W + 4, W + 2
VP = W + 4
VWX = XL + 4
PE5, DVE5 = 9, 11
PE3, DVE3 = 3, 4
AR = 3
MERGED = 5, 4
WARM = {"projection": 8, "conv5": 4, "v": 1, "offsets": 1, "offsets1": 1, "weights": 10, "close_l0": 2, "route": 4}
QB = 4
PARTS = 3

FIELDS = [
    ("proj1", P), ("w5", 25), ("w3", 9), ("b_proj1", 1), ("b_conv0", 1), ("b_dw", 1), ("g_ln", 1), ("b_ln", 1),
    ("eps", 1), ("one", 1), ("minus_one", 1), ("b_proj2", 1), ("b_outproj", 1), ("b_conv", 1), ("wb", 1), ("wc", 1),
    ("b_z", 1), ("b_r", 1), ("b_f", 1), ("b1", EP), ("later", 2), ("ident", P), ("wa", BH),
    ("ident2", C), ("center", P), ("mean", P),
    ("inproj", C), ("offmask", OM), ("b_row", C + OM),
    ("outproj_t", P), ("conv", P), ("proj2", P), ("proj2_t", P),
    ("zx", P), ("za", P), ("rx", P), ("ra", P), ("fx", P), ("fa", P),
    ("w1", EP * BH * P), ("w2", EP * C), ("router", BH * E), ("b2", C), ("pick", EP * P), ("rank", E),
    ("base", 2 * NPT * XL), ("grid", W),
]
COL = {}
_at = 0
for _name, _width in FIELDS:
    COL[_name] = (_at, _width)
    _at += _width
NCOL = _at
CUTS = [0, COL["ident2"][0], COL["inproj"][0], COL["outproj_t"][0], COL["w1"][0], NCOL]


def conv_attn_moe(nc, A_x, A_w, v_dram, out):
    ctx = ExitStack()
    with ctx:
        def sb(name, shape, dt=F32):
            return ctx.enter_context(nc.sbuf_tensor(name, shape, dt))

        def sem(name):
            return ctx.enter_context(nc.semaphore(name))

        wts = sb("wts", [P, NCOL])

        def w(name, a=0, b=None, p0=0, p1=P):
            at, width = COL[name]
            return wts[p0:p1, at + a:at + (width if b is None else b)]

        def half(bh):
            return bh * 64, bh * 64 + 64

        x_in = sb("x_in", [P, BL, HW])
        ones = sb("ones", [PARTS, P], BF16)
        idle = sb("idle", [P, 512], BF16)
        cen3 = sb("cen3", [P, PE3, P])
        cenh = sb("cenh", [P, P])
        w_oc = sb("w_oc", [P, P])
        b_oc = sb("b_oc", [P, 1])
        w2c = sb("w2c", [P, P])
        half_rf = sb("half_rf", [P, 2])
        pick_b = sb("pick_b", [PARTS * E, EP * P], BF16)
        ident_b = sb("ident_b", [P, P], BF16)
        b_row = sb("b_row", [PARTS, C + OM], BF16)
        b_row_rest = sb("b_row_rest", [PARTS, 2, C + OM])
        b_row_part = sb("b_row_part", [PARTS, 2, C + OM], BF16)
        b2_parts = sb("b2_parts", [PARTS * E, PARTS, C], BF16)
        b2_rest = sb("b2_rest", [PARTS * E, 2, C])

        upad = sb("upad", [P, BL, UP, UP])
        acc5 = sb("acc5", [P, BL, HW])
        hpad = sb("hpad", [P, BL, HP, HP])
        h_dense = sb("h_dense", [P, BL, HW])
        acc3 = sb("acc3", [P, BL, HW])
        sq = sb("sq", [P, BL, HW])
        lnv = sb("lnv", [P, BL, HW])
        rstd = sb("rstd", [P, BL, HW])
        xn = sb("xn", [P, BL, HW])
        x1 = sb("x1", [P, BL, HW])
        v_tok = sb("v_tok", [P, BL, VW])
        v_win = sb("v_win", [P, BL, K5, VWX * C])
        lg = sb("lg", [P, BL, NPT, XG])
        lmax = sb("lmax", [P, BL, XG])
        lsub = sb("lsub", [P, BL, NPT, XG])
        prob = sb("prob", [P, BL, NPT * XG])
        psum_p = sb("psum_p", [P, BL, XG])
        rsum = sb("rsum", [P, BL, XG])
        hat = sb("hat", [P, BL, K3, 2, NPT * XG])
        o_abs = sb("o_abs", [P, BL, 2 * NPT * XG])
        over_sum = sb("over_sum", [P, BL])
        far = sb("far", [1, BL], I32)
        ym = sb("ym", [P, BL, K3, NPT * XG])
        terms = sb("terms", [P, BL, K3, K3, NPT * XG])
        diag5 = terms[:, :, :, :, :].rearrange("p b x y c -> p (b x y c)")[:, 0:PE5 * P].rearrange(
            "p (k n) -> p k n", k=PE5)
        prod = sb("prod", [P, BL, K5, K5, VW])
        tap_room = prod[:, :, :, :, :].rearrange("p b y x c -> p b (y x c)")
        N5, N3 = 25 - PE5 - DVE5, 9 - PE3 - DVE3
        scaled5 = tap_room[:, :, 0:N5 * HW].rearrange("p b (k n) -> p b k n", k=N5)
        scaled3 = tap_room[:, :, N5 * HW:(N5 + N3) * HW].rearrange("p b (k n) -> p b k n", k=N3)
        part5 = tap_room[:, :, (N5 + N3) * HW:(N5 + N3 + 1) * HW]
        part3 = tap_room[:, :, (N5 + N3 + 1) * HW:(N5 + N3 + 2) * HW]
        samp = sb("samp", [P, BL, VW])
        samp_t = sb("samp_t", [P, BL, HW])
        zu = sb("zu", [P, BL, HW])
        xb = sb("xb", [P, BL, HW])

        s_pos = sb("s_pos", [P, BL, 2, NPT * XG])
        s_hy = sb("s_hy", [P, NPT * XG])
        s_hx = sb("s_hx", [P, NPT * XG])
        s_min = sb("s_min", [P, NPT * XG])
        s_v = sb("s_v", [P, W * C])
        zeros = s_v[:, 0:B * VP * VP * C // P]
        s_term = sb("s_term", [P, VW])
        s_out = sb("s_out", [P, VW])
        slow_mark = sb("slow_mark", [1, BL])

        taken = {"prod": 0, "terms": 0}

        def late(*shape, place="prod"):
            size = 1
            for n in shape:
                size *= n
            whole = (prod[:, :, :, :, :].rearrange("p b y x c -> p b (y x c)") if place == "prod"
                     else terms[:, :, :, :, :].rearrange("p b x y c -> p b (x y c)"))
            assert taken[place] + size <= whole.shape[2]
            flat = whole[:, :, taken[place]:taken[place] + size]
            taken[place] += size
            return flat if len(shape) == 1 else flat.rearrange("p b (a n) -> p b a n", a=shape[0])

        t0 = late(HW, place="terms")
        xh = late(HW, place="terms")
        q = late(HW, place="terms")
        t0h = late(HW, place="terms")
        base_out = late(HW, place="terms")
        xh_tok = late(IT, P, place="terms")
        t2 = late(HW, place="terms")
        pr = late(BH * IT, HW)
        prT = late(BH, IT * HW)
        norm = late(BH * IT, P)
        att = late(HW)
        zt = late(HW)
        rt = late(HW)
        ft = late(HW)
        rx_ = late(HW)
        fz_ = late(HW)
        gsum = late(HW)
        sq2 = late(HW)
        lnv2 = late(HW)
        rstd2 = late(HW)
        sq3 = late(HW)
        lnv3 = late(HW, place="terms")
        rstd3 = late(HW, place="terms")
        x2 = late(HW, place="terms")
        h_act = prod[:, :, :, :, :].rearrange("p b y x c -> p b (y x c)")[:, :, 0:EP * BH * HW].rearrange(
            "p b (e n) -> p b e n", e=EP)
        h_cmb = late(2, BH * HW)
        res = sb("res", [P, BL, HW])
        smax = sb("smax", [P, BL, IT, BH])
        a_col = sb("a_col", [P, BL, IT, BH])
        a_max = sb("a_max", [P, BL, IT, BH])
        nbias = sb("nbias", [P, BL, IT, BH])
        prsum = sb("prsum", [P, BL, IT, BH])
        prinv = sb("prinv", [P, BL, IT, BH])
        NT = IT * BH
        rmax = sb("rmax", [P, BL, NT])
        rsub = sb("rsub", [P, BL, NT, E])
        rexp = sb("rexp", [P, BL, NT, E])
        rall = sb("rall", [P, BL, NT])
        rsums = sb("rsums", [P, BL, NT, E // 2])
        r1 = sb("r1", [P, BL, NT, E])
        k1 = sb("k1", [P, BL, NT])
        p1 = sb("p1", [P, BL, NT, E])
        rest = sb("rest", [P, BL, NT, E])
        m2 = sb("m2", [P, BL, NT])
        e2 = sb("e2", [P, BL, NT, E])
        r2 = sb("r2", [P, BL, NT, E])
        k2 = sb("k2", [P, BL, NT])
        p2 = sb("p2", [P, BL, NT, E])
        both = sb("both", [P, BL, NT, E])
        csel = sb("csel", [P, BL, NT, E])
        tot = sb("tot", [P, BL, NT])
        guard = sb("guard", [P, BL, NT])
        tinv = sb("tinv", [P, BL, NT])
        comb = sb("comb", [P, BL, NT, E])
        crest = sb("crest", [P, BL, NT, E])
        cparts = sb("cparts", [P, BL, NT, PARTS, E], BF16)
        comb_t = sb("comb_t", [PARTS * E, BL, BH * HW], BF16)

        ps = ctx.enter_context(nc.psum_tensor("ps", [P, BL * QB, 512], F32))

        def bank(bl, i):
            return ps[:, bl * QB + i, :]

        x_loaded = sem("x_loaded")
        pads_zero = sem("pads_zero")
        zeros_set = sem("zeros_set")
        v_cleared = sem("v_cleared")
        ones_set = sem("ones_set")
        idle_set = sem("idle_set")
        diag5_set = sem("diag5_set")
        cen3_set = sem("cen3_set")
        cenh_set = sem("cenh_set")
        half_set = sem("half_set")
        pick_set = sem("pick_set")
        b2_step = sem("b2_step")
        b_row_step = sem("b_row_step")
        proj1_done = sem("proj1_done")
        u_ready = sem("u_ready")
        scaled5_done = sem("scaled5_done")
        scaled3_done = sem("scaled3_done")
        xb_ready = sem("xb_ready")
        conv5_done = sem("conv5_done")
        h_ready = sem("h_ready")
        h_copied = sem("h_copied")
        combos_done = sem("combos_done")
        combos_copied = sem("combos_copied")
        d1_done = sem("d1_done")
        v_done = sem("v_done")
        v_copied = sem("v_copied")
        sq1_done = sem("sq1_done")
        var1_done = sem("var1_done")
        ln1_done = sem("ln1_done")
        rstd1_done = sem("rstd1_done")
        xn_done = sem("xn_done")
        x1_done = sem("x1_done")
        off_done = sem("off_done")
        lg_copied = sem("lg_copied")
        abs_done = sem("abs_done")
        hats_y_done = sem("hats_y_done")
        hats_done = sem("hats_done")
        lmax_done = sem("lmax_done")
        lsub_done = sem("lsub_done")
        prob_done = sem("prob_done")
        psum_done = sem("psum_done")
        rsum_done = sem("rsum_done")
        ym_done = sem("ym_done")
        terms_done = sem("terms_done")
        over_done = sem("over_done")
        over_total = sem("over_total")
        far_set = sem("far_set")
        a5_done = sem("a5_done")
        prod_done = sem("prod_done")
        sum_done = sem("sum_done")
        samp_done = sem("samp_done")
        slow_done = sem("slow_done")
        side_terms_done = sem("side_terms_done")
        merge_done = sem("merge_done")
        last_merged = sem("last_merged")
        sT_done = sem("sT_done")
        sT_copied = sem("sT_copied")
        attn0_done = sem("attn0_done")
        zu_done = sem("zu_done")
        t0_done = sem("t0_done")
        t0_copied = sem("t0_copied")
        t0h_done = sem("t0h_done")
        sq2_done = sem("sq2_done")
        var2_done = sem("var2_done")
        ln2_done = sem("ln2_done")
        rstd2_done = sem("rstd2_done")
        xh_done = sem("xh_done")
        q_done = sem("q_done")
        xtok_done = sem("xtok_done")
        xtok_copied = sem("xtok_copied")
        acol_copied = sem("acol_copied")
        scores_done = sem("scores_done")
        smax_done = sem("smax_done")
        amax_done = sem("amax_done")
        nbias_done = sem("nbias_done")
        exp_done = sem("exp_done")
        prinv_done = sem("prinv_done")
        norm_done = sem("norm_done")
        pT_done = sem("pT_done")
        pT_copied_act = sem("pT_copied_act")
        pT_copied_dve = sem("pT_copied_dve")
        att_done = sem("att_done")
        att_copied = sem("att_copied")
        gates_done = sem("gates_done")
        r_done = sem("r_done")
        z_done = sem("z_done")
        f_done = sem("f_done")
        rx_done = sem("rx_done")
        fz_done = sem("fz_done")
        gsum_done = sem("gsum_done")
        t2_done = sem("t2_done")
        d3_done = sem("d3_done")
        sq3_done = sem("sq3_done")
        var3_done = sem("var3_done")
        ln3_done = sem("ln3_done")
        rstd3_done = sem("rstd3_done")
        x2_done = sem("x2_done")
        base_done = sem("base_done")
        route_done = sem("route_done")
        rsub_done = sem("rsub_done")
        rexp_done = sem("rexp_done")
        rall_done = sem("rall_done")
        comb_done = sem("comb_done")
        combT_done = sem("combT_done")
        combT_copied = sem("combT_copied")
        hid_done = sem("hid_done")
        gelu_done = sem("gelu_done")
        spread_done = sem("spread_done")
        hcmb_done = sem("hcmb_done")
        y_done = sem("y_done")
        res_done = sem("res_done")
        out_stored = sem("out_stored")
        w_loaded = [sem(f"w_loaded{i}") for i in range(len(CUTS) - 1)]
        acc5_step = [sem(f"acc5_step{bl}") for bl in range(BL)]
        acc3_step = [sem(f"acc3_step{bl}") for bl in range(BL)]
        part5_step = [sem(f"part5_step{bl}") for bl in range(BL)]
        part3_step = [sem(f"part3_step{bl}") for bl in range(BL)]
        near_hat = [sem(f"near_hat{bl}") for bl in range(BL)]
        rall_step = [sem(f"rall_step{bl}") for bl in range(BL)]
        route_step = [sem(f"route_step{bl}") for bl in range(BL)]
        v_stored = [sem(f"v_stored{bl}") for bl in range(BL)]
        v_windowed = [sem(f"v_windowed{bl}") for bl in range(BL)]
        slow_loaded = [sem(f"slow_loaded{bl}") for bl in range(BL)]

        def grid(ap):
            return ap.rearrange("p (y x) -> p y x", y=H)

        def tokens(tile, bl, bh, xl):
            p0, p1_ = half(bh)
            return tile[p0:p1_, bl, xl:HW:XL]

        def hid_bank(bl, ep):
            return bank(bl, (0, 1, 3, 0)[ep])

        def om_ps(bl):
            return ps[:, bl * QB + 2:bl * QB + 4, :].rearrange("p b (k c) -> p (b k) c", k=2)

        def off_ps(bl):
            return om_ps(bl)[:, :, 0:2 * NPT * G].rearrange("p x (q g) -> p q x g", g=G)

        def msk_ps(bl):
            return om_ps(bl)[:, :, 2 * NPT * G:OM].rearrange("p x (q g) -> p q x g", g=G)

        def points(ap):
            return ap.rearrange("p (q x g) -> p q x g", x=XL, g=G)

        def a5_rows(bl, first, last):
            i, at = (0, first) if first < AR else (1, first - AR)
            return bank(bl, i)[:, at * K5 * XG:(at + last - first) * K5 * XG].rearrange(
                "p (y x c) -> p y x c", x=K5, c=XG)

        block = ctx.enter_context(nc.Block())

        @block.sync
        def _(sp):
            sp.dma_start(x_in[:, :, :], A_x).then_inc(x_loaded, 16)
            for i in (1, 3):
                sp.dma_start(wts[:, CUTS[i]:CUTS[i + 1]], A_w[:, CUTS[i]:CUTS[i + 1]]).then_inc(w_loaded[i], 16)
            sp.wait_ge(zeros_set, 1)
            sp.dma_start(v_dram.rearrange("b y x c -> (b y x c)").rearrange("(p n) -> p n", p=P),
                         zeros[:, :]).then_inc(v_cleared, 16)
            sp.wait_ge(v_cleared, 16)
            for bl in range(BL):
                sp.wait_ge(v_copied, bl + 1)
                for bh in range(BH):
                    p0, p1_ = half(bh)
                    inside = v_dram[BL * bh + bl, 2:2 + H, 2:2 + W, :].rearrange("y (q x) c -> y q (x c)", q=XQ)
                    sp.dma_start(inside, v_tok[p0:p1_, bl, :]).then_inc(v_stored[bl], 16)
                sp.wait_ge(v_stored[bl], 16 * BH)
                for dy in range(K5):
                    for bh in range(BH):
                        p0, p1_ = half(bh)
                        rows = bass.AP(v_dram.tensor, v_dram[BL * bh + bl, dy].offset,
                                       [[VP * C, H], [VW, XQ], [1, VWX * C]])
                        sp.dma_start(v_win[p0:p1_, bl, dy, :], rows).then_inc(v_windowed[bl], 16)
            for bl in range(BL):
                sp.wait_ge(res_done, bl + 1)
                sp.dma_start(out[:, bl * HW:(bl + 1) * HW], res[:, bl, :]).then_inc(out_stored, 16)
            sp.wait_ge(out_stored, 16 * BL)

        @block.gpsimd
        def _(pool):
            g = nc.gpsimd
            g.memset(upad[:, :, :, :], 0.0).then_inc(pads_zero, 1)
            g.memset(ones[:, :], 1.0).then_inc(ones_set, 1)
            g.memset(hpad[:, :, :, :], 0.0).then_inc(pads_zero, 1)
            g.memset(zeros[:, :], 0.0).then_inc(zeros_set, 1)
            pool.wait_ge(w_loaded[0], 16)
            pool.wait_ge(w_loaded[1], 16)
            g.tensor_tensor(cen3[:, :, :], w("center").unsqueeze(1).broadcast_to([P, PE3, P]),
                            w("w3", 0, PE3).unsqueeze(2).broadcast_to([P, PE3, P]), ALU.mult).then_inc(cen3_set, 1)
            for i, name in enumerate(("b_r", "b_f")):
                g.tensor_scalar(half_rf[:, i:i + 1], w(name), 0.5, None, ALU.mult).then_inc(half_set, 1)

            def add_scaled(scaled, count, part, step, ready):
                for k in range(1, count):
                    for bl in range(BL):
                        pool.wait_ge(ready, BL * k + bl + 1)
                        if k > 1:
                            pool.wait_ge(step[bl], k - 1)
                        g.tensor_tensor(part[:, bl, :], scaled[:, bl, 0, :] if k == 1 else part[:, bl, :],
                                        scaled[:, bl, k, :], ALU.add).then_inc(step[bl], 1)

            add_scaled(scaled5, N5, part5, part5_step, scaled5_done)
            add_scaled(scaled3, N3, part3, part3_step, scaled3_done)
            g.tensor_scalar(cenh[:, :], w("center"), 0.5, None, ALU.mult).then_inc(cenh_set, 1)
            g.tensor_scalar(xb[:, :, :], x_in[:, :, :], w("b_proj2"), None, ALU.add).then_inc(xb_ready, 1)
            pool.wait_ge(w_loaded[4], 16)
            g.tensor_copy(pick_b[:, :], w("pick", p1=PARTS * E)).then_inc(pick_set, 1)
            g.tensor_copy(ident_b[:, :], w("ident")).then_inc(pick_set, 1)
            left = w("b2", p1=PARTS * E)
            for i in range(PARTS):
                if i:
                    pool.wait_ge(b2_step, 2 * i)
                g.tensor_copy(b2_parts[:, i, :], left).then_inc(b2_step, 1)
                if i < PARTS - 1:
                    pool.wait_ge(b2_step, 2 * i + 1)
                    g.tensor_tensor(b2_rest[:, i, :], left, b2_parts[:, i, :], ALU.subtract).then_inc(b2_step, 1)
                    left = b2_rest[:, i, :]

            def side_terms(bl):
                pool.wait_ge(ym_done, bl + 1)
                pool.wait_ge(hats_done, 2 * bl + 2)
                g.tensor_tensor(terms[:, bl, K3 - 1, :, :], ym[:, bl, :, :],
                                hat[:, bl, K3 - 1, 0, :].unsqueeze(1).broadcast_to([P, K3, NPT * XG]),
                                ALU.mult).then_inc(side_terms_done, 1)

            def merge(bl):
                for dy in range(MERGED[bl]):
                    pool.wait_ge(prod_done, K5 * bl + dy + 1)
                    into = prod[:, bl, dy, 0:2, :]
                    g.tensor_tensor(into, into, prod[:, bl, dy, 3:5, :], ALU.add).then_inc(merge_done, 1)

            for bl in range(BL):
                side_terms(bl)
            for bl in range(BL):
                merge(bl)
                pool.wait_ge(far_set, bl + 1)
                is_far = pool.value_load(far[0:1, bl:bl + 1], min_val=0, max_val=1)
                with pool.If(is_far > 0):
                    pool.wait_ge(samp_done, bl + 1)
                    pos = s_pos[:, bl, :, :].rearrange("p c n -> p (c n)")
                    g.tensor_tensor(pos, hat[:, bl, 2, :, :].rearrange("p c n -> p (c n)"),
                                    hat[:, bl, 0, :, :].rearrange("p c n -> p (c n)"), ALU.subtract)
                    g.memset(s_out[:, :], 0.0)
                    pool.drain()
                    base = w("base").rearrange("p (q x) -> p q x", x=XL).unsqueeze(3).broadcast_to([P, 2 * NPT, XL, G])
                    g.tensor_tensor(points(pos), points(pos), base, ALU.add)
                    pool.drain()
                    g0 = COL["grid"][0]

                    def hats(dst, axis, coordinate):
                        at = wts[:, bass.ds(g0 + coordinate, 1)].broadcast_to([P, NPT * XG])
                        g.tensor_tensor(dst, s_pos[:, bl, axis, :], at, ALU.subtract)
                        pool.drain()
                        g.tensor_scalar(s_min[:, :], dst, 0.0, None, ALU.min)
                        pool.drain()
                        g.tensor_scalar(dst, dst, 0.0, None, ALU.max)
                        pool.drain()
                        g.tensor_tensor(dst, s_min[:, :], dst, ALU.subtract)
                        pool.drain()
                        g.tensor_scalar(dst, dst, 1.0, 0.0, ALU.add, ALU.max)
                        pool.drain()

                    with pool.Fori(0, H) as y:
                        for bh in range(BH):
                            p0, p1_ = half(bh)
                            row = v_dram[BL * bh + bl].rearrange("y x c -> y (x c)")[bass.ds(y + 2, 1),
                                                                                      2 * C:(2 + W) * C]
                            pool.dma_start(s_v[p0:p1_, :], row.broadcast_to([64, W * C])).then_inc(slow_loaded[bl], 16)
                        hats(s_hy[:, :], 1, y)
                        pool.wait_ge(slow_loaded[bl], 16 * BH * (y + 1))
                        g.tensor_tensor(s_hy[:, :], s_hy[:, :], prob[:, bl, :], ALU.mult)
                        pool.drain()
                        with pool.Fori(0, W) as x:
                            hats(s_hx[:, :], 0, x)
                            g.tensor_tensor(s_hx[:, :], s_hx[:, :], s_hy[:, :], ALU.mult)
                            pool.drain()
                            for a, b, n in ((0, 4, 4), (0, 2, 2), (0, 1, 1), (0, 8, 1)):
                                into = s_hx[:, a * XG:(a + n) * XG]
                                g.tensor_tensor(into, into, s_hx[:, b * XG:(b + n) * XG], ALU.add)
                                pool.drain()
                            g.tensor_tensor(
                                s_term[:, :].rearrange("p (x g c) -> p x g c", x=XL, g=G),
                                s_hx[:, 0:XG].rearrange("p (x g) -> p x g", g=G).unsqueeze(3)
                                .broadcast_to([P, XL, G, GC]),
                                s_v[:, bass.ds(x * C, C)].rearrange("p (g c) -> p g c", g=G).unsqueeze(1)
                                .broadcast_to([P, XL, G, GC]), ALU.mult)
                            pool.drain()
                            g.tensor_tensor(s_out[:, :], s_out[:, :], s_term[:, :], ALU.add)
                            pool.drain()
                    g.tensor_tensor(samp[:, bl, :].rearrange("p (x c) -> p x c", c=GC),
                                    s_out[:, :].rearrange("p (x c) -> p x c", c=GC),
                                    rsum[:, bl, :].unsqueeze(2).broadcast_to([P, XG, GC]), ALU.mult)
                    pool.drain()
                g.memset(slow_mark[:, bl:bl + 1], 0.0).then_inc(slow_done, 1)
            for bl in range(BL):
                pool.wait_ge(x2_done, bl + 1)
                pool.wait_ge(t2_done, bl + 1)
                g.tensor_tensor(base_out[:, bl, :], t2[:, bl, :], x2[:, bl, :], ALU.add).then_inc(base_done, 1)
            for bl in range(BL):
                pool.wait_ge(rexp_done, bl + 1)
                n = E // 2
                left = rexp[:, bl, :, :]
                for step in range(3):
                    if step:
                        pool.wait_ge(rall_step[bl], step)
                    to = rall[:, bl, :].unsqueeze(2) if n == 1 else rsums[:, bl, :, 0:n]
                    g.tensor_tensor(to, left[:, :, 0:n], left[:, :, n:2 * n], ALU.add).then_inc(
                        rall_done if n == 1 else rall_step[bl], 1)
                    left = rsums[:, bl, :, :]
                    n //= 2

        @block.scalar
        def _(act):
            a = nc.scalar
            LN_EXP = "natural_log_exp_and_others"
            act.dma_start(wts[:, CUTS[0]:CUTS[1]], A_w[:, CUTS[0]:CUTS[1]]).then_inc(w_loaded[0], 16)
            for i in (2, 4):
                act.dma_start(wts[:, CUTS[i]:CUTS[i + 1]], A_w[:, CUTS[i]:CUTS[i + 1]]).then_inc(w_loaded[i], 16)
            a.preload_act_table(ACT.Gelu)
            act.wait_ge(w_loaded[0], 16)
            act.wait_ge(pads_zero, 1)
            for bl in range(BL):
                act.wait_ge(proj1_done, bl + 1)
                a.activation(upad[:, bl, 2:2 + H, 2:2 + W], grid(bank(bl, 0)[:, 0:HW]), ACT.Gelu,
                             bias=w("b_proj1")).then_inc(u_ready, 1)
            a.preload_act_table_set(LN_EXP)

            def scale_taps(first, count, side, padded, weights, scaled, done):
                for k in range(count):
                    y0, x0 = (first + k) // side, (first + k) % side
                    for bl in range(BL):
                        a.activation(grid(scaled[:, bl, k, :]), padded[:, bl, y0:y0 + H, x0:x0 + W], ACT.Copy,
                                     scale=w(weights, first + k, first + k + 1)).then_inc(done, 1)

            act.wait_ge(u_ready, BL)
            scale_taps(PE5 + DVE5, N5, 5, upad, "w5", scaled5, scaled5_done)
            act.wait_ge(h_ready, BL)
            scale_taps(PE3 + DVE3, N3, 3, hpad, "w3", scaled3, scaled3_done)
            for bl in range(BL):
                a.activation(grid(h_dense[:, bl, :]), hpad[:, bl, 1:1 + H, 1:1 + W], ACT.Copy).then_inc(h_copied, 1)

            def square(bl, src, dst, ready, done):
                act.wait_ge(ready, bl + 1)
                a.activation(dst[:, bl, :], src, ACT.Square).then_inc(done, 1)

            def inverse_std(bl, log, dst, ready, between, done):
                act.wait_ge(ready, bl + 1)
                at = HW if between is ln1_done else 0
                a.activation(log[:, bl, :], bank(bl, 1)[:, at:at + HW], ACT.Ln, bias=w("eps")).then_inc(between, 1)
                act.wait_ge(between, bl + 1)
                a.activation(dst[:, bl, :], log[:, bl, :], ACT.Exp, scale=-0.5).then_inc(done, 1)

            for bl in range(BL):
                square(bl, bank(bl, 1)[:, 0:HW], sq, d1_done, sq1_done)
            for bl in range(BL):
                inverse_std(bl, lnv, rstd, var1_done, ln1_done, rstd1_done)
            a.preload_act_table(ACT.Gelu)
            for bl in range(BL):
                act.wait_ge(xn_done, bl + 1)
                a.activation(x1[:, bl, :], xn[:, bl, :], ACT.Gelu, bias=w("b_ln"),
                             scale=w("g_ln")).then_inc(x1_done, 1)
            a.preload_act_table_set(LN_EXP)
            def hats(bl):
                act.wait_ge(off_done, bl + 1)
                a.activation(lg[:, bl, :, :].rearrange("p q (x g) -> p q x g", g=G), msk_ps(bl),
                             ACT.Copy).then_inc(lg_copied, 1)
                a.activation(points(o_abs[:, bl, :]), off_ps(bl), ACT.Abs).then_inc(abs_done, 1)

                def far_hats(axis, done):
                    off = off_ps(bl)[:, axis * NPT:(axis + 1) * NPT]
                    a.activation(points(hat[:, bl, 2, axis, :]), off, ACT.Relu).then_inc(done, 1)
                    a.activation(points(hat[:, bl, 0, axis, :]), off, ACT.Relu, scale=-1.0).then_inc(done, 1)

                far_hats(1, hats_y_done)
                if bl:
                    act.wait_ge(abs_done, bl + 1)
                    a.activation(hat[:, bl, 1, :, :].rearrange("p c n -> p (c n)"), o_abs[:, bl, :], ACT.Identity,
                                 bias=w("one"), scale=-1.0).then_inc(near_hat[bl], 1)
                    far_hats(0, hats_done)
                act.wait_ge(lsub_done, bl + 1)
                a.activation(prob[:, bl, :], lsub[:, bl, :, :].rearrange("p q x -> p (q x)"),
                             ACT.Exp).then_inc(prob_done, 1)
                if bl == 0:
                    far_hats(0, hats_done)

            def over(bl):
                act.wait_ge(abs_done, bl + 1)
                a.activation(s_pos[:, bl, :, :].rearrange("p c n -> p (c n)"), o_abs[:, bl, :], ACT.Relu,
                             bias=w("minus_one"), accum_out=over_sum[:, bl:bl + 1]).then_inc(over_done, 1)

            def samples(bl):
                act.wait_ge(sT_done, bl + 1)
                a.activation(samp_t[:, bl, :].rearrange("p (q x) -> p x q", x=XL),
                             bank(bl, 0)[:, 0:HW].rearrange("p (x q) -> p x q", x=XL), ACT.Copy).then_inc(sT_copied, 1)

            def copy_tokens(bl):
                act.wait_ge(xtok_done, bl + 1)
                both_it = bank(bl, 2).rearrange("p (t c) -> p t c", t=IT)
                a.activation(a_col[:, bl, :, :], both_it[:, :, P:P + BH], ACT.Copy).then_inc(acol_copied, 1)
                a.activation(xh_tok[:, bl, :, :], both_it[:, :, 0:P], ACT.Copy).then_inc(xtok_copied, 1)

            def softmax_exp(bl):
                act.wait_ge(nbias_done, bl + 1)
                for bh in range(BH):
                    for it in range(IT):
                        a.activation(pr[:, bl, bh * IT + it, :], bank(bl, bh)[:, it * HW:(it + 1) * HW], ACT.Exp,
                                     bias=nbias[:, bl, it, bh:bh + 1],
                                     accum_out=prsum[:, bl, it, bh:bh + 1]).then_inc(exp_done, 1)

            def copy_turned(bl):
                act.wait_ge(pT_done, 2 * bl + 1)
                a.activation(prT[:, bl, 0, :], bank(bl, 0), ACT.Copy).then_inc(pT_copied_act, 1)

            def copy_att(bl):
                act.wait_ge(att_done, bl + 1)
                a.activation(att[:, bl, :], bank(bl, 2)[:, HW:2 * HW], ACT.Copy).then_inc(att_copied, 1)

            def gates(bl):
                act.wait_ge(gates_done, 2 * bl + 1)
                a.activation(rt[:, bl, :], bank(bl, 3)[:, HW:2 * HW], ACT.Tanh, bias=half_rf[:, 0:1],
                             scale=0.5).then_inc(r_done, 1)
                a.activation(zt[:, bl, :], bank(bl, 3)[:, 0:HW], ACT.Tanh, bias=w("b_z")).then_inc(z_done, 1)
                act.wait_ge(gates_done, 2 * bl + 2)
                a.activation(ft[:, bl, :], bank(bl, 2)[:, 0:HW], ACT.Tanh, bias=half_rf[:, 1:2],
                             scale=0.5).then_inc(f_done, 1)

            hats(0)
            hats(1)
            over(0)
            over(1)
            samples(0)
            samples(1)
            square(0, bank(0, 3)[:, 0:HW], sq2, t0_done, sq2_done)
            inverse_std(0, lnv2, rstd2, var2_done, ln2_done, rstd2_done)
            square(1, bank(1, 3)[:, 0:HW], sq2, t0_done, sq2_done)
            inverse_std(1, lnv2, rstd2, var2_done, ln2_done, rstd2_done)
            a.preload_act_table_set("exp_and_others")
            copy_tokens(0)
            softmax_exp(0)
            copy_tokens(1)
            softmax_exp(1)
            act.wait_ge(half_set, 2)
            for bl in range(BL):
                copy_turned(bl)
            for bl in range(BL):
                copy_att(bl)
            for bl in range(BL):
                gates(bl)
            square(0, bank(0, 0)[:, 0:HW], sq3, d3_done, sq3_done)
            a.preload_act_table_set(LN_EXP)
            square(1, bank(1, 0)[:, 0:HW], sq3, d3_done, sq3_done)
            for bl in range(BL):
                inverse_std(bl, lnv3, rstd3, var3_done, ln3_done, rstd3_done)
            for bl in range(BL):
                act.wait_ge(rsub_done, bl + 1)
                a.activation(rexp[:, bl, :, :], rsub[:, bl, :, :], ACT.Exp).then_inc(rexp_done, 1)
            a.preload_act_table(ACT.Gelu)
            for ep in range(EP):
                for bl in range(BL):
                    act.wait_ge(hid_done, ep * BL + bl + 1)
                    a.activation(h_act[:, bl, ep, :], hid_bank(bl, ep), ACT.Gelu,
                                 bias=w("b1", ep, ep + 1)).then_inc(gelu_done, 1)

        @block.vector
        def _(dve):
            v = nc.vector
            v.memset(idle[:, :], 0.0).then_inc(idle_set, 1)
            dve.wait_ge(w_loaded[0], 16)
            v.tensor_tensor(diag5[:, :, :], w("ident").unsqueeze(1).broadcast_to([P, PE5, P]),
                            w("w5", 0, PE5).unsqueeze(2).broadcast_to([P, PE5, P]), ALU.mult).then_inc(diag5_set, 1)

            def taps(first, count, side, acc, padded, weights, bias, step, ready):
                for k in range(first, first + count):
                    for bl in range(BL):
                        src = padded[:, bl, k // side:k // side + H, k % side:k % side + W]
                        to = grid(acc[:, bl, :])
                        if k == first:
                            dve.wait_ge(ready, bl + 1)
                            v.tensor_scalar(to, src, w(weights, k, k + 1), w(bias), ALU.mult,
                                            ALU.add).then_inc(step[bl], 1)
                        else:
                            dve.wait_ge(step[bl], k - first)
                            v.scalar_tensor_tensor(out=to, in0=src, scalar=w(weights, k, k + 1), in1=to,
                                                   op0=ALU.mult, op1=ALU.add).then_inc(step[bl], 1)

            def bias_row():
                left = w("b_row", p1=PARTS)
                for i in range(PARTS - 1):
                    if i:
                        dve.wait_ge(b_row_step, 2 * i)
                    v.tensor_copy(b_row_part[:, i, :], left).then_inc(b_row_step, 1)
                    dve.wait_ge(b_row_step, 2 * i + 1)
                    v.scalar_tensor_tensor(out=b_row_rest[:, i, :], in0=b_row_part[:, i, :],
                                           scalar=w("later", i, i + 1, 0, PARTS), in1=left, op0=ALU.mult,
                                           op1=ALU.add).then_inc(b_row_step, 1)
                    left = b_row_rest[:, i, :]
                dve.wait_ge(b_row_step, 2 * PARTS - 2)
                v.tensor_copy(b_row[:, :], left).then_inc(b_row_step, 1)

            taps(PE5, DVE5, 5, acc5, upad, "w5", "b_conv0", acc5_step, u_ready)
            dve.wait_ge(pads_zero, 2)
            dve.wait_ge(part5_step[0], N5 - 1)
            dve.wait_ge(acc5_step[0], DVE5)
            v.tensor_tensor(acc5[:, 0, :], acc5[:, 0, :], part5[:, 0, :], ALU.add).then_inc(acc5_step[0], 1)
            for bl in range(BL):
                dve.wait_ge(conv5_done, bl + 1)
                dve.wait_ge(acc5_step[bl], DVE5 + (bl == 0))
                v.tensor_tensor(hpad[:, bl, 1:1 + H, 1:1 + W], grid(bank(bl, 1)[:, 0:HW]), grid(acc5[:, bl, :]),
                                ALU.add).then_inc(h_ready, 1)
            taps(PE3, DVE3, 3, acc3, hpad, "w3", "b_dw", acc3_step, h_ready)
            dve.wait_ge(w_loaded[2], 16)
            bias_row()
            def normed1(bl):
                dve.wait_ge(rstd1_done, bl + 1)
                v.tensor_tensor(xn[:, bl, :], bank(bl, 1)[:, 0:HW], rstd[:, bl, :], ALU.mult).then_inc(xn_done, 1)

            def copy_combos():
                dve.wait_ge(combos_done, 1)
                v.tensor_copy(w_oc[:, :], bank(0, 3)[:, 0:P])
                v.tensor_tensor(b_oc[:, :], bank(0, 3)[:, P:P + 1], w("b_conv"), ALU.add)
                v.tensor_copy(w2c[:, :], bank(0, 3)[:, 2 * P:3 * P]).then_inc(combos_copied, 1)

            normed1(0)
            copy_combos()
            normed1(1)
            for bl in range(BL):
                dve.wait_ge(v_done, bl + 1)
                v.tensor_copy(v_tok[:, bl, :], bank(bl, 0)[:, 0:VW]).then_inc(v_copied, 1)

            def softmax(bl):
                dve.wait_ge(lg_copied, bl + 1)
                v.tensor_reduce(lmax[:, bl, :], lg[:, bl, :, :].rearrange("p q x -> p x q"), AX_X,
                                ALU.max).then_inc(lmax_done, 1)
                dve.wait_ge(lmax_done, bl + 1)
                v.tensor_tensor(lsub[:, bl, :, :], lg[:, bl, :, :],
                                lmax[:, bl, :].unsqueeze(1).broadcast_to([P, NPT, XG]),
                                ALU.subtract).then_inc(lsub_done, 1)
                if bl == 0:
                    dve.wait_ge(abs_done, bl + 1)
                    v.tensor_scalar(hat[:, bl, 1, :, :].rearrange("p c n -> p (c n)"), o_abs[:, bl, :], -1.0, 1.0,
                                    ALU.mult, ALU.add).then_inc(near_hat[bl], 1)

            def masked_hats(bl):
                dve.wait_ge(near_hat[bl], 1)
                dve.wait_ge(hats_y_done, 2 * bl + 2)
                dve.wait_ge(prob_done, bl + 1)
                v.tensor_tensor(ym[:, bl, :, :], hat[:, bl, :, 1, :],
                                prob[:, bl, :].unsqueeze(1).broadcast_to([P, K3, NPT * XG]),
                                ALU.mult).then_inc(ym_done, 1)

            def window_terms(bl, jx):
                dve.wait_ge(ym_done, bl + 1)
                if jx != 1:
                    dve.wait_ge(hats_done, 2 * bl + 2)
                v.tensor_tensor(terms[:, bl, jx, :, :], ym[:, bl, :, :],
                                hat[:, bl, jx, 0, :].unsqueeze(1).broadcast_to([P, K3, NPT * XG]),
                                ALU.mult).then_inc(terms_done, 1)

            def mask_sums(bl):
                v.tensor_reduce(psum_p[:, bl, :], prob[:, bl, :].rearrange("p (q x) -> p x q", q=NPT), AX_X,
                                ALU.add).then_inc(psum_done, 1)

            def inverse_sums():
                dve.wait_ge(psum_done, BL)
                v.reciprocal(rsum[:, :, :], psum_p[:, :, :]).then_inc(rsum_done, 1)

            def products(bl, dy):
                if dy == 0:
                    dve.wait_ge(v_windowed[bl], 16 * BH * K5)
                    dve.wait_ge(a5_done, bl + 1)
                row = v_win[:, bl, dy, 0:VW]
                win = bass.AP(row.tensor, row.offset, [list(row.ap[0]), [C, K5], [GC, XG], [1, GC]])
                v.tensor_tensor(prod[:, bl, dy, :, :].rearrange("p d (x c) -> p d x c", c=GC), win,
                                a5_rows(bl, dy, dy + 1)[:, 0].unsqueeze(3).broadcast_to([P, K5, XG, GC]),
                                ALU.mult).then_inc(prod_done, 1)

            def merge_last():
                dve.wait_ge(prod_done, K5 * BL)
                into = prod[:, 1, K5 - 1, 0:2, :]
                v.tensor_tensor(into, into, prod[:, 1, K5 - 1, 3:5, :], ALU.add).then_inc(last_merged, 1)

            def flags(bl):
                dve.wait_ge(over_total, bl + 1)
                v.tensor_scalar(far[:, bl:bl + 1], bank(bl, 2)[0:1, 0:1], 0.0, None, ALU.is_gt).then_inc(far_set, 1)

            def normalise(bl):
                dve.wait_ge(sum_done, bl + 1)
                dve.wait_ge(rsum_done, 1)
                v.tensor_tensor(samp[:, bl, :].rearrange("p (x c) -> p x c", c=GC),
                                bank(bl, 2)[:, 0:VW].rearrange("p (x c) -> p x c", c=GC),
                                rsum[:, bl, :].unsqueeze(2).broadcast_to([P, XG, GC]), ALU.mult).then_inc(samp_done, 1)

            def gate_u(bl):
                dve.wait_ge(attn0_done, bl + 1)
                dve.wait_ge(u_ready, bl + 1)
                dve.wait_ge(combos_copied, 1)
                v.scalar_tensor_tensor(out=grid(zu[:, bl, :]), in0=grid(bank(bl, 2)[:, 0:HW]), scalar=b_oc[:, 0:1],
                                       in1=upad[:, bl, 2:2 + H, 2:2 + W], op0=ALU.add,
                                       op1=ALU.mult).then_inc(zu_done, 1)

            def copy_t0(bl):
                dve.wait_ge(t0_done, bl + 1)
                dve.wait_ge(xb_ready, 1)
                v.tensor_tensor(t0[:, bl, :], bank(bl, 0)[:, 0:HW], xb[:, bl, :], ALU.add).then_inc(t0_copied, 1)

            def normed2(bl):
                dve.wait_ge(rstd2_done, bl + 1)
                v.tensor_tensor(xh[:, bl, :], bank(bl, 3)[:, 0:HW], rstd2[:, bl, :], ALU.mult).then_inc(xh_done, 1)
                dve.wait_ge(xh_done, bl + 1)
                v.tensor_scalar(q[:, bl, :], xh[:, bl, :], w("wc"), w("wb"), ALU.mult, ALU.add).then_inc(q_done, 1)

            def score_max(bl):
                dve.wait_ge(scores_done, bl + 1)
                for bh in range(BH):
                    v.tensor_reduce(smax[:, bl, :, bh], bank(bl, bh).rearrange("p (t j) -> p t j", t=IT), AX_X,
                                    ALU.max).then_inc(smax_done, 1)
                dve.wait_ge(smax_done, BH * (bl + 1))
                dve.wait_ge(acol_copied, bl + 1)
                v.tensor_tensor(a_max[:, bl, :, :], smax[:, bl, :, :], a_col[:, bl, :, :],
                                ALU.add).then_inc(amax_done, 1)
                dve.wait_ge(amax_done, bl + 1)
                v.tensor_tensor(nbias[:, bl, :, :], a_col[:, bl, :, :], a_max[:, bl, :, :],
                                ALU.subtract).then_inc(nbias_done, 1)

            def t0_xh(bl):
                dve.wait_ge(t0_copied, bl + 1)
                dve.wait_ge(xh_done, bl + 1)
                v.scalar_tensor_tensor(out=t0h[:, bl, :], in0=xh[:, bl, :], scalar=0.5, in1=t0[:, bl, :], op0=ALU.mult,
                                       op1=ALU.add).then_inc(t0h_done, 1)

            def inverse_rows(bl):
                for bh in range(BH):
                    dve.wait_ge(exp_done, BH * IT * bl + IT * (bh + 1))
                    v.reciprocal(prinv[:, bl, :, bh], prsum[:, bl, :, bh]).then_inc(prinv_done, 1)
                    dve.wait_ge(prinv_done, BH * bl + bh + 1)
                    for it in range(IT):
                        v.tensor_scalar(norm[:, bl, bh * IT + it, :], w("ident"), prinv[:, bl, it, bh:bh + 1], None,
                                        ALU.mult).then_inc(norm_done, 1)

            def copy_turned(bl):
                dve.wait_ge(pT_done, 2 * bl + 2)
                v.tensor_copy(prT[:, bl, 1, :], bank(bl, 1)).then_inc(pT_copied_dve, 1)

            def gated(bl):
                dve.wait_ge(r_done, bl + 1)
                v.scalar_tensor_tensor(out=rx_[:, bl, :], in0=rt[:, bl, :], scalar=0.5, in1=xh[:, bl, :], op0=ALU.mult,
                                       op1=ALU.mult).then_inc(rx_done, 1)
                dve.wait_ge(rx_done, bl + 1)
                dve.wait_ge(t0h_done, bl + 1)
                v.tensor_tensor(gsum[:, bl, :], rx_[:, bl, :], t0h[:, bl, :], ALU.add).then_inc(gsum_done, 1)
                dve.wait_ge(z_done, bl + 1)
                dve.wait_ge(f_done, bl + 1)
                v.scalar_tensor_tensor(out=fz_[:, bl, :], in0=ft[:, bl, :], scalar=1.0, in1=zt[:, bl, :], op0=ALU.add,
                                       op1=ALU.mult).then_inc(fz_done, 1)
                dve.wait_ge(fz_done, bl + 1)
                dve.wait_ge(gsum_done, bl + 1)
                v.scalar_tensor_tensor(out=t2[:, bl, :], in0=fz_[:, bl, :], scalar=0.5, in1=gsum[:, bl, :],
                                       op0=ALU.mult, op1=ALU.add).then_inc(t2_done, 1)

            def normed3(bl):
                dve.wait_ge(rstd3_done, bl + 1)
                v.tensor_tensor(x2[:, bl, :], bank(bl, 0)[:, 0:HW], rstd3[:, bl, :], ALU.mult).then_inc(x2_done, 1)

            softmax(0)
            masked_hats(0)
            window_terms(0, 1)
            softmax(1)
            window_terms(0, 0)
            masked_hats(1)
            window_terms(1, 1)
            window_terms(1, 0)
            mask_sums(0)
            products(0, 0)
            flags(0)
            mask_sums(1)
            products(0, 1)
            inverse_sums()
            products(0, 2)
            flags(1)
            products(0, 3)
            products(0, 4)
            products(1, 0)
            products(1, 1)
            products(1, 2)
            normalise(0)
            products(1, 3)
            products(1, 4)
            merge_last()
            normalise(1)
            gate_u(0)
            gate_u(1)
            copy_t0(0)
            normed2(0)
            copy_t0(1)
            normed2(1)
            for bl in range(BL):
                score_max(bl)
                t0_xh(bl)
            for bl in range(BL):
                inverse_rows(bl)
            for bl in range(BL):
                copy_turned(bl)
            for bl in range(BL):
                gated(bl)
            for bl in range(BL):
                normed3(bl)

            def routed(build, *outside):
                for bl in range(BL):
                    for signal in outside:
                        dve.wait_ge(signal, bl + 1)
                    if steps[0]:
                        dve.wait_ge(route_step[bl], steps[0])
                    build(bl).then_inc(route_step[bl], 1)
                steps[0] += 1

            def over_e(t, bl):
                return t[:, bl, :].unsqueeze(2).broadcast_to([P, NT, E])

            def logits(bl):
                return bank(bl, 2)[:, 0:NT * E].rearrange("p (t e) -> p t e", e=E)

            steps = [0]
            rank = w("rank").unsqueeze(1).broadcast_to([P, NT, E])
            routed(lambda b: v.tensor_reduce(rmax[:, b, :], logits(b), AX_X, ALU.max), route_done)
            for bl in range(BL):
                dve.wait_ge(route_step[bl], 1)
                v.tensor_tensor(rsub[:, bl, :, :], logits(bl), over_e(rmax, bl), ALU.subtract).then_inc(rsub_done, 1)
            routed(lambda b: v.scalar_tensor_tensor(out=r1[:, b, :, :], in0=rsub[:, b, :, :], scalar=0.0, in1=rank,
                                                    op0=ALU.is_equal, op1=ALU.mult), rsub_done)
            routed(lambda b: v.tensor_reduce(k1[:, b, :], r1[:, b, :, :], AX_X, ALU.max))
            routed(lambda b: v.tensor_tensor(p1[:, b, :, :], rank, over_e(k1, b), ALU.is_equal))
            routed(lambda b: v.scalar_tensor_tensor(out=rest[:, b, :, :], in0=p1[:, b, :, :], scalar=-1e30,
                                                    in1=rsub[:, b, :, :], op0=ALU.mult, op1=ALU.add))
            routed(lambda b: v.tensor_reduce(m2[:, b, :], rest[:, b, :, :], AX_X, ALU.max))
            routed(lambda b: v.tensor_tensor(e2[:, b, :, :], rest[:, b, :, :], over_e(m2, b), ALU.is_equal))
            routed(lambda b: v.tensor_tensor(r2[:, b, :, :], e2[:, b, :, :], rank, ALU.mult))
            routed(lambda b: v.tensor_reduce(k2[:, b, :], r2[:, b, :, :], AX_X, ALU.max))
            routed(lambda b: v.tensor_tensor(p2[:, b, :, :], rank, over_e(k2, b), ALU.is_equal))
            routed(lambda b: v.tensor_tensor(both[:, b, :, :], p1[:, b, :, :], p2[:, b, :, :], ALU.add))
            routed(lambda b: v.tensor_tensor(csel[:, b, :, :], both[:, b, :, :], rexp[:, b, :, :], ALU.mult),
                   rexp_done)
            routed(lambda b: v.tensor_reduce(tot[:, b, :], csel[:, b, :, :], AX_X, ALU.add))
            routed(lambda b: v.scalar_tensor_tensor(out=guard[:, b, :], in0=rall[:, b, :], scalar=1e-12,
                                                    in1=tot[:, b, :], op0=ALU.mult, op1=ALU.max), rall_done)
            routed(lambda b: v.reciprocal(tinv[:, b, :], guard[:, b, :]))
            routed(lambda b: v.tensor_tensor(comb[:, b, :, :], csel[:, b, :, :], over_e(tinv, b), ALU.mult))
            routed(lambda b: v.tensor_copy(cparts[:, b, :, 0, :], comb[:, b, :, :]))
            routed(lambda b: v.tensor_tensor(crest[:, b, :, :], comb[:, b, :, :], cparts[:, b, :, 0, :],
                                             ALU.subtract))
            routed(lambda b: v.tensor_copy(cparts[:, b, :, 1, :], crest[:, b, :, :]))
            for bl in range(BL):
                dve.wait_ge(route_step[bl], steps[0])
                v.tensor_tensor(cparts[:, bl, :, 2, :], crest[:, bl, :, :], cparts[:, bl, :, 1, :],
                                ALU.subtract).then_inc(comb_done, 1)
            for bl in range(BL):
                dve.wait_ge(combT_done, bl + 1)
                v.tensor_copy(comb_t[:, bl, :],
                              bank(bl, 2).bitcast(BF16)[0:PARTS * E, 0:BH * HW]).then_inc(combT_copied, 1)
            for ep in range(EP):
                for bl in range(BL):
                    n = ep * BL + bl
                    dve.wait_ge(gelu_done, n + 1)
                    dve.wait_ge(spread_done, n + 1)
                    if ep >= 2:
                        dve.wait_ge(y_done, n - 2 * BL + 1)
                    v.tensor_tensor(h_cmb[:, bl, ep % 2, :], h_act[:, bl, ep, :], bank(bl, 2),
                                    ALU.mult).then_inc(hcmb_done, 1)
            for bl in range(BL):
                dve.wait_ge(y_done, (EP - 1) * BL + bl + 1)
                dve.wait_ge(base_done, bl + 1)
                v.tensor_tensor(res[:, bl, :], bank(bl, 3)[:, 0:HW], base_out[:, bl, :], ALU.add).then_inc(res_done, 1)

        @block.tensor
        def _(pe):
            def mm(out_, lhsT, rhs, start=True, stop=True):
                return nc.tensor.matmul(out_, lhsT, rhs, start=start, stop=stop, skip_group_check=True)

            def keep_warm(n, into):
                for _ in range(n):
                    mm(into, idle[:, 0:P], idle[:, :])

            pe.wait_ge(idle_set, 1)
            keep_warm(WARM["projection"], bank(1, 3))
            pe.wait_ge(x_loaded, 16)
            pe.wait_ge(w_loaded[0], 16)
            for bl in range(BL):
                mm(bank(bl, 0)[:, 0:HW], w("proj1"), x_in[:, bl, :]).then_inc(proj1_done, 1)
            keep_warm(WARM["conv5"], bank(1, 3))
            pe.wait_ge(diag5_set, 1)
            for bl in range(BL):
                pe.wait_ge(u_ready, bl + 1)
                for k in range(PE5):
                    last = mm(grid(bank(bl, 1)[:, 0:HW]), diag5[:, k, :],
                              upad[:, bl, k // 5:k // 5 + H, k % 5:k % 5 + W], k == 0, bl == 0 and k == PE5 - 1)
                if bl == 0:
                    last.then_inc(conv5_done, 1)
            pe.wait_ge(part5_step[1], N5 - 1)
            mm(bank(1, 1)[:, 0:HW], w("ident"), part5[:, 1, :], False, True).then_inc(conv5_done, 1)
            pe.wait_ge(w_loaded[1], 16)
            pe.wait_ge(cen3_set, 1)
            for bl in range(BL):
                pe.wait_ge(h_ready, bl + 1)
                for k in range(PE3):
                    mm(grid(bank(bl, 1)[:, 0:HW]), cen3[:, k, :],
                       hpad[:, bl, k // 3:k // 3 + H, k % 3:k % 3 + W], k == 0, False)
            for bl in range(BL):
                pe.wait_ge(part3_step[bl], N3 - 1)
                mm(bank(bl, 1)[:, 0:HW], w("center"), part3[:, bl, :], False, False)
                pe.wait_ge(acc3_step[bl], DVE3)
                mm(bank(bl, 1)[:, 0:HW], w("center"), acc3[:, bl, :], False, True).then_inc(d1_done, 1)
            for bl in range(BL):
                pe.wait_ge(sq1_done, bl + 1)
                mm(bank(bl, 1)[:, HW:2 * HW], w("mean"), sq[:, bl, :]).then_inc(var1_done, 1)
            pe.wait_ge(w_loaded[1], 16)
            pe.wait_ge(w_loaded[3], 16)
            mm(bank(0, 3)[:, 0:P], w("outproj_t"), w("conv"))
            mm(bank(0, 3)[:, P:P + 1], w("conv"), w("b_outproj"))
            mm(bank(0, 3)[:, 2 * P:3 * P], w("proj2_t"), w("center")).then_inc(combos_done, 1)
            keep_warm(WARM["v"], bank(1, 0))
            pe.wait_ge(w_loaded[2], 16)
            pe.wait_ge(ones_set, 1)
            pe.wait_ge(b_row_step, 2 * PARTS - 1)
            for bl in range(BL):
                pe.wait_ge(h_copied, bl + 1)
                mm(bank(bl, 0)[:, 0:VW].rearrange("p (x c) -> p x c", c=C), ones[:, :],
                   b_row[:, 0:C].unsqueeze(1).broadcast_to([PARTS, XL, C]), True, False)
                for xl in range(XL):
                    for bh in range(BH):
                        p0, p1_ = half(bh)
                        last = mm(bank(bl, 0)[p0:p1_, xl * C:(xl + 1) * C], tokens(h_dense, bl, bh, xl),
                                  w("inproj", p0=p0, p1=p1_), False, True)
                last.then_inc(v_done, 1)
                pe.wait_ge(combos_copied, 1)
                for i in range(2):
                    mm(om_ps(bl)[:, 2 * i:2 * i + 2, 0:OM], ones[:, :],
                       b_row[:, C:C + OM].unsqueeze(1).broadcast_to([PARTS, 2, OM]), True, False)
            pe.wait_ge(v_copied, 1)
            keep_warm(WARM["offsets"], bank(0, 0))
            for bl in range(BL):
                if bl:
                    keep_warm(WARM["offsets1"], bank(0, 0))
                pe.wait_ge(x1_done, bl + 1)
                for xl in range(XL):
                    for bh in range(BH):
                        p0, p1_ = half(bh)
                        last = mm(om_ps(bl)[p0:p1_, xl, 0:OM], tokens(x1, bl, bh, xl), w("offmask", p0=p0, p1=p1_),
                                  False, True)
                last.then_inc(off_done, 1)

            def window_weights(bl):
                pe.wait_ge(v_copied, bl + 1)
                pe.wait_ge(xn_done, bl + 1)
                order = (1, 2, 0)
                for jx in order:
                    if jx < K3 - 1:
                        pe.wait_ge(terms_done, (K3 - 1) * bl + 2 - jx)
                    else:
                        pe.wait_ge(side_terms_done, bl + 1)
                    for jy in range(K3):
                        term = terms[:, bl, jx, jy, :].rearrange("p (i j c) -> p j i c", i=K3, j=K3)
                        cut = AR - jy
                        last = mm(a5_rows(bl, jy, AR)[:, :, jx:jx + K3, :], w("ident"), term[:, 0:cut],
                                  jx == order[0] and jy == 0, jx == order[-1] and jy == K3 - 1)
                        if jy:
                            last = mm(a5_rows(bl, AR, AR + jy)[:, :, jx:jx + K3, :], w("ident"), term[:, cut:K3],
                                      jx == order[0] and jy == 1,
                                      jx == order[-1] and jy == K3 - 1)
                last.then_inc(a5_done, 1)

            def flags(bl):
                pe.wait_ge(over_done, bl + 1)
                pe.wait_ge(hats_done, 2 * bl + 2)
                mm(bank(bl, 2)[0:1, 0:1], over_sum[:, bl:bl + 1], w("one")).then_inc(over_total, 1)

            def window_sum(bl, dy):
                if dy == 0:
                    pe.wait_ge(far_set, bl + 1)
                pe.wait_ge(prod_done, K5 * bl + dy + 1)
                for dx in (2, 0, 1):
                    if dx == 0:
                        if dy < MERGED[bl]:
                            pe.wait_ge(merge_done, MERGED[0] * bl + dy + 1)
                        else:
                            pe.wait_ge(last_merged, 1)
                    last = mm(bank(bl, 2)[:, 0:VW], w("ident"), prod[:, bl, dy, dx, :],
                              dy == 0 and dx == 2, dy == K5 - 1 and dx == 1)
                if dy == K5 - 1:
                    last.then_inc(sum_done, 1)

            def to_channels(bl):
                pe.wait_ge(samp_done, bl + 1)
                pe.wait_ge(slow_done, bl + 1)
                for xl in range(XL):
                    for bh in range(BH):
                        p0, p1_ = half(bh)
                        last = mm(bank(bl, 0)[p0:p1_, xl * 64:xl * 64 + 64], samp[p0:p1_, bl, xl * C:(xl + 1) * C],
                                  w("ident2", p0=p0, p1=p1_))
                last.then_inc(sT_done, 1)

            def shortcut(bl):
                pe.wait_ge(xb_ready, 1)
                mm(bank(bl, 3)[:, 0:HW], w("center"), xb[:, bl, :], True, False)

            def project(bl):
                pe.wait_ge(sT_copied, bl + 1)
                mm(bank(bl, 2)[:, 0:HW], w_oc[:, :], samp_t[:, bl, :]).then_inc(attn0_done, 1)

            def close_l0(bl):
                pe.wait_ge(zu_done, bl + 1)
                mm(bank(bl, 3)[:, 0:HW], w2c[:, :], zu[:, bl, :], False, True)
                mm(bank(bl, 0)[:, 0:HW], w("proj2"), zu[:, bl, :]).then_inc(t0_done, 1)

            def variance(bl, tile, ready, done):
                pe.wait_ge(ready, bl + 1)
                mm(bank(bl, 1)[:, 0:HW], w("mean"), tile[:, bl, :]).then_inc(done, 1)

            def scores(bl, it):
                if it == 0:
                    pe.wait_ge(q_done, bl + 1)
                    pe.wait_ge(t0_copied, bl + 1)
                for m in range(2):
                    for bh in range(BH):
                        p0, p1_ = half(bh)
                        o0, o1 = half(m)
                        c0 = it * P + m * 64
                        last = mm(bank(bl, bh)[o0:o1, it * HW:(it + 1) * HW], q[p0:p1_, bl, c0:c0 + 64],
                                  xh[p0:p1_, bl, :])
                if it == IT - 1:
                    last.then_inc(scores_done, 1)

            def token_major(bl):
                pe.wait_ge(xh_done, bl + 1)
                at = COL["ident"][0]
                for it in range(IT):
                    last = mm(bank(bl, 2)[:, it * HW:it * HW + P + BH], xh[:, bl, it * P:(it + 1) * P],
                              wts[:, at:at + P + BH])
                last.then_inc(xtok_done, 1)

            def turn(bl):
                for bh in range(BH):
                    pe.wait_ge(norm_done, BH * IT * bl + IT * (bh + 1))
                    for it in range(IT):
                        for jt in range(IT):
                            c0 = jt * HW + it * P
                            last = mm(bank(bl, bh)[:, c0:c0 + P], pr[:, bl, bh * IT + it, jt * P:(jt + 1) * P],
                                      norm[:, bl, bh * IT + it, :])
                    last.then_inc(pT_done, 1)

            def attend(bl):
                pe.wait_ge(pT_copied_act, bl + 1)
                pe.wait_ge(pT_copied_dve, bl + 1)
                for jt in range(IT):
                    for bh in range(BH):
                        p0, p1_ = half(bh)
                        last = mm(bank(bl, 2)[p0:p1_, HW:2 * HW], xh_tok[:, bl, jt, p0:p1_],
                                  prT[:, bl, bh, jt * HW:(jt + 1) * HW], False, jt == IT - 1)
                last.then_inc(att_done, 1)

            def gates_x(bl):
                mm(bank(bl, 3)[:, HW:2 * HW], w("rx"), xh[:, bl, :], True, False)
                mm(bank(bl, 3)[:, 0:HW], w("zx"), xh[:, bl, :], False, False)
                pe.wait_ge(xtok_copied, bl + 1)
                mm(bank(bl, 2)[:, 0:HW], w("fx"), xh[:, bl, :], True, False)

            def gates(bl):
                pe.wait_ge(att_copied, bl + 1)
                mm(bank(bl, 3)[:, HW:2 * HW], w("ra"), att[:, bl, :], False, True)
                mm(bank(bl, 3)[:, 0:HW], w("za"), att[:, bl, :], False, True).then_inc(gates_done, 1)
                mm(bank(bl, 2)[:, 0:HW], w("fa"), att[:, bl, :], False, True).then_inc(gates_done, 1)

            def centre3(bl):
                pe.wait_ge(cenh_set, 1)
                pe.wait_ge(gsum_done, bl + 1)
                mm(bank(bl, 0)[:, 0:HW], w("center"), gsum[:, bl, :], True, False)
                pe.wait_ge(fz_done, bl + 1)
                mm(bank(bl, 0)[:, 0:HW], cenh[:, :], fz_[:, bl, :], False, True).then_inc(d3_done, 1)

            pe.wait_ge(v_copied, BL)
            keep_warm(WARM["weights"], bank(1, 0))
            window_weights(0)
            flags(0)
            flags(1)
            for bl in range(BL):
                shortcut(bl)
            window_weights(1)
            for dy in range(K5):
                window_sum(0, dy)
            window_sum(1, 0)
            window_sum(1, 1)
            window_sum(1, 2)
            to_channels(0)
            window_sum(1, 3)
            window_sum(1, 4)
            project(0)
            to_channels(1)
            close_l0(0)
            project(1)
            variance(0, sq2, sq2_done, var2_done)
            keep_warm(WARM["close_l0"], bank(1, 1))
            close_l0(1)
            variance(1, sq2, sq2_done, var2_done)
            scores(0, 0)
            scores(0, 1)
            token_major(0)
            scores(1, 0)
            scores(1, 1)
            token_major(1)
            for bl in range(BL):
                gates_x(bl)
            for bl in range(BL):
                turn(bl)
            for bl in range(BL):
                attend(bl)
            for bl in range(BL):
                gates(bl)
            for bl in range(BL):
                centre3(bl)
            for bl in range(BL):
                variance(bl, sq3, sq3_done, var3_done)
            def route(bl):
                pe.wait_ge(x2_done, bl + 1)
                for it in range(IT):
                    last = mm(bank(bl, 2)[:, it * BH * E:(it + 1) * BH * E], x2[:, bl, it * P:(it + 1) * P], w("router"))
                last.then_inc(route_done, 1)

            def hidden(ep, bl):
                if ep == 3:
                    pe.wait_ge(gelu_done, bl + 1)
                for bh in range(BH):
                    at = (ep * BH + bh) * P
                    last = mm(hid_bank(bl, ep)[:, bh * HW:(bh + 1) * HW], w("w1", at, at + P), x2[:, bl, :])
                last.then_inc(hid_done, 1)

            def turn_comb(bl):
                pe.wait_ge(pick_set, 2)
                pe.wait_ge(comb_done, bl + 1)
                turned = bank(bl, 2).bitcast(BF16)
                for bh in range(BH):
                    for it in range(IT):
                        c0 = bh * HW + it * P
                        last = nc.tensor.transpose(
                            turned[0:PARTS * E, c0:c0 + P],
                            cparts[:, bl, it * BH + bh, :, :].rearrange("p a e -> p (a e)"), ident_b[:, :])
                last.then_inc(combT_done, 1)

            def bias2(bl):
                pe.wait_ge(b2_step, 2 * PARTS - 1)
                for i in range(PARTS):
                    for bh in range(BH):
                        p0, p1_ = half(bh)
                        mm(bank(bl, 3)[p0:p1_, 0:HW], b2_parts[:, i, :], comb_t[:, bl, bh * HW:(bh + 1) * HW],
                           False, False)

            def spread(ep, bl):
                if ep:
                    pe.wait_ge(hcmb_done, (ep - 1) * BL + bl + 1)
                else:
                    pe.wait_ge(combT_copied, bl + 1)
                mm(bank(bl, 2), pick_b[:, ep * P:(ep + 1) * P], comb_t[:, bl, :]).then_inc(spread_done, 1)

            keep_warm(WARM["route"], bank(0, 3))
            for bl in range(BL):
                route(bl)
            for ep in range(EP - 1):
                for bl in range(BL):
                    hidden(ep, bl)
            for bl in range(BL):
                turn_comb(bl)
            hidden(EP - 1, 0)
            for bl in range(BL):
                spread(0, bl)
            hidden(EP - 1, 1)
            for ep in range(EP):
                for bl in range(BL):
                    if ep == 0:
                        pe.wait_ge(gelu_done, 2 * BL + bl + 1)
                    elif ep == EP - 1:
                        bias2(bl)
                    pe.wait_ge(hcmb_done, ep * BL + bl + 1)
                    if ep + 1 < EP:
                        spread(ep + 1, bl)
                    for bh in range(BH):
                        p0, p1_ = half(bh)
                        last = mm(bank(bl, 3)[p0:p1_, 0:HW], w("w2", ep * C, (ep + 1) * C),
                                  h_cmb[:, bl, ep % 2, bh * HW:(bh + 1) * HW], ep == 0, ep == EP - 1)
                    last.then_inc(y_done, 1)


def _packed(i):
    import numpy as np

    def both(a):
        return np.concatenate([a, a], 0)

    def diag(a):
        out = np.zeros((P, P), np.float32)
        out[:C, :C] = a
        out[C:, C:] = a
        return out

    def sides(a):
        out = np.zeros((2, C, 2, a.shape[1]), np.float32)
        out[0, :, 0] = a
        out[1, :, 1] = a
        return out.reshape(P, -1)

    def top(a):
        out = np.zeros((P, a.shape[1]), np.float32)
        out[:a.shape[0]] = a
        return out

    g = {k: np.asarray(a) for k, a in i.items()}
    L0, L1, FF = "L0_conv_", "L1_attn_", "L1_ffn_"
    f = {}
    f["proj1"] = diag(g[L0 + "proj1_w"])
    f["w5"] = both(g[L0 + "conv0_w"].reshape(C, 25))
    f["w3"] = both(g[L0 + "dw_w"].reshape(C, 9))
    for name, key in (("b_proj1", "proj1_b"), ("b_conv0", "conv0_b"), ("b_dw", "dw_b"), ("g_ln", "ln_g"),
                      ("b_ln", "ln_b"), ("b_proj2", "proj2_b"), ("b_outproj", "outproj_b"), ("b_conv", "conv_b")):
        f[name] = both(g[L0 + key][:, None])
    f["eps"] = np.full((P, 1), 1e-5, np.float32)
    f["one"] = np.ones((P, 1), np.float32)
    f["minus_one"] = -np.ones((P, 1), np.float32)
    for n, name in ((1, "wb"), (2, "wc")):
        f[name] = both(g[L1 + "att_w"][n * C:(n + 1) * C, None])
    f["wa"] = sides(g[L1 + "att_w"][:C, None])
    for gate in "zrf":
        f["b_" + gate] = both(g[L1 + gate + "_b"][:, None])
        f[gate + "x"] = diag(g[L1 + gate + "_w"][:, :C].T)
        f[gate + "a"] = diag(g[L1 + gate + "_w"][:, C:].T)
    rows = np.arange(P)[:, None]
    f["later"] = -(rows > np.arange(2)).astype(np.float32)
    f["b1"] = g[FF + "b1"].reshape(EP, P).T
    f["ident"] = np.eye(P, dtype=np.float32)
    f["ident2"] = both(np.eye(C, dtype=np.float32))
    f["center"] = diag((np.eye(C) - 1.0 / C).astype(np.float32))
    f["mean"] = diag(np.full((C, C), 1.0 / C, np.float32))
    f["inproj"] = both(g[L0 + "inproj_w"])

    def order(off, mask):
        off = off.reshape(-1, G, NPT, 2).transpose(0, 3, 2, 1).reshape(-1, 2 * NPT * G)
        mask = mask.reshape(-1, G, NPT).transpose(0, 2, 1).reshape(-1, NPT * G)
        return np.concatenate([off, mask], 1)

    f["offmask"] = both(order(g[L0 + "off_w"], g[L0 + "mask_w"]))
    b_row = np.concatenate([g[L0 + "inproj_b"][None], order(g[L0 + "off_b"][None], g[L0 + "mask_b"][None])], 1)
    f["b_row"] = top(np.tile(b_row, (PARTS, 1)))
    f["outproj_t"] = diag(g[L0 + "outproj_w"].T)
    f["conv"] = diag(g[L0 + "conv_w"])
    f["proj2"] = diag(g[L0 + "proj2_w"])
    f["proj2_t"] = diag(g[L0 + "proj2_w"].T)
    w1 = np.zeros((BH, C, EP, BH, 2, C), np.float32)
    for bh in range(BH):
        w1[bh, :, :, bh] = g[FF + "w1"].reshape(EP, 2, C, C).transpose(2, 0, 1, 3)
    f["w1"] = w1.reshape(P, -1)
    f["w2"] = g[FF + "w2"].reshape(EP, P, C).transpose(1, 0, 2).reshape(P, EP * C)
    f["router"] = sides(g[FF + "router_w"].T)
    f["b2"] = top(np.tile(g[FF + "b2"], (PARTS, 1)))
    pick = np.zeros((P, EP, 2, C), np.float32)
    for e in range(E):
        pick[e:PARTS * E:E, e // 2, e % 2] = 1.0
    f["pick"] = pick.reshape(P, EP * P)
    p = np.arange(P)
    base = np.zeros((P, 2, K3, K3, XL), np.float32)
    base[:, 0] = ((p % XQ) * XL)[:, None, None, None] + np.arange(XL) + (np.arange(K3) - 1)[:, None, None]
    base[:, 1] = ((p // XQ) % H)[:, None, None, None] + (np.arange(K3) - 1)[None, :, None]
    f["rank"] = np.tile(E - np.arange(E, dtype=np.float32), (P, 1))
    f["base"] = base.reshape(P, -1)
    f["grid"] = np.tile(np.arange(W, dtype=np.float32), (P, 1))
    cols = [f[name] for name, _ in FIELDS]
    assert [a.shape for a in cols] == [(P, n) for _, n in FIELDS]
    return np.ascontiguousarray(np.concatenate(cols, 1))


def kernel(**inputs):
    import numpy as np
    import concourse.bacc as _bacc
    from concourse.bass_utils import run_bass_kernel_spmd as _run

    x = np.asarray(inputs["x"])
    arrays = {
        "in_x": np.ascontiguousarray(x.reshape(BH, BL, C, HW).transpose(0, 2, 1, 3).reshape(P, N)),
        "in_w": _packed({k: a for k, a in inputs.items() if k != "x"}),
    }
    nc = _bacc.Bacc("TRN2", target_bir_lowering=False, num_devices=1)
    A_x = nc.dram_tensor("in_x", (P, N), F32, kind="ExternalInput").ap()
    A_w = nc.dram_tensor("in_w", (P, NCOL), F32, kind="ExternalInput").ap()
    v_dram = nc.dram_tensor("v_padded", (B, VP, VP, C), F32, kind="Internal").ap()
    out = nc.dram_tensor("out_0", (P, N), F32, kind="ExternalOutput").ap()
    conv_attn_moe(nc, A_x, A_w, v_dram, out)
    r = _run(nc, [arrays], core_ids=[0])
    got = r.results[0]["out_0"]
    return np.ascontiguousarray(got.reshape(2, C, BL, H, W).transpose(0, 2, 1, 3, 4).reshape(B, C, H, W))
```
